# Optimizing a Trainium2 kernel written in Bass

```python
import numpy as np
import jax
import jax.numpy as jnp

def _softmax(x, axis=-1):
    return jax.nn.softmax(x, axis=axis)

def _gelu(x):
    return jax.nn.gelu(x, approximate=True)

def _silu(x):
    return jax.nn.silu(x)

def _sigmoid(x):
    return jax.nn.sigmoid(x)

def _layernorm(x, axis=-1, eps=1e-05):
    m = jnp.mean(x, axis=axis, keepdims=True)
    v = jnp.var(x, axis=axis, keepdims=True)
    return (x - m) / jnp.sqrt(v + eps)

def _scatter_add(tgt, idx, src, axis=0):
    return tgt.at[idx].add(src)

def _segment_sum(src, seg, n):
    return jax.ops.segment_sum(src, seg, n)
kernel_name = 'mk_seq_postln_d1_jaxref_r4_56b29e'

def setup_inputs(seed: int=0):
    np.random.seed(seed)
    _w = jnp.asarray

    def _L0_attn_setup():
        import jax, jax.numpy as jnp
        import numpy as np
        EMB = 256
        H = 16
        D = EMB // H
        EPS = 1e-05
        SM_SCALE = 1.0
        CAUSAL = True
        NEG = -1e+30

        def _layernorm(t, g, b):
            m = jnp.mean(t, axis=-1, keepdims=True)
            v = jnp.mean(jnp.square(t - m), axis=-1, keepdims=True)
            return (t - m) * jax.lax.rsqrt(v + EPS) * g + b
        key = jax.random.key(seed)
        ks = jax.random.split(key, 8)
        N, L = (2, 512)
        x = jax.random.normal(ks[0], (N, L, EMB), dtype=jnp.float32)
        mask = jnp.ones((N, L), dtype=jnp.int32)
        s = 0.02
        Wq = jax.random.normal(ks[1], (EMB, EMB), dtype=jnp.float32) * s
        Wk = jax.random.normal(ks[2], (EMB, EMB), dtype=jnp.float32) * s
        Wv = jax.random.normal(ks[3], (EMB, EMB), dtype=jnp.float32) * s
        Wo = jax.random.normal(ks[4], (EMB, EMB), dtype=jnp.float32) * s
        bo = jnp.zeros((EMB,), dtype=jnp.float32)
        gq = jnp.ones((D,), dtype=jnp.float32)
        bq = jnp.zeros((D,), dtype=jnp.float32)
        gk = jnp.ones((D,), dtype=jnp.float32)
        bk = jnp.zeros((D,), dtype=jnp.float32)
        return {'x': x, 'mask': mask, 'Wq': Wq, 'Wk': Wk, 'Wv': Wv, 'gq': gq, 'bq': bq, 'gk': gk, 'bk': bk, 'Wo': Wo, 'bo': bo}
    _L0_attn_in = _L0_attn_setup()

    def _L0_ffn_setup():
        import jax, jax.numpy as jnp
        import numpy as np
        DIM = 256
        DEPTH = 2
        HEADS = 8
        DIM_HEAD = 64
        WINDOW = 128
        INNER = HEADS * DIM_HEAD
        HID = int(DIM * 4 * 2 / 3)
        B, N = (2, 2048)
        QK_SCALE = 8.0

        def shift_token(t):
            t1, t2 = jnp.split(t, 2, axis=-1)
            t2 = jnp.pad(t2, ((0, 0), (1, 0), (0, 0)))[:, :-1]
            return jnp.concatenate([t1, t2], axis=-1)

        def l2norm(t):
            return t / jnp.clip(jnp.linalg.norm(t, axis=-1, keepdims=True), 1e-12)

        def rotate_half(x):
            x1, x2 = jnp.split(x, 2, axis=-1)
            return jnp.concatenate([-x2, x1], axis=-1)

        def rotary_xpos(q, k):
            n = q.shape[-2]
            half_idx = jnp.arange(0, DIM_HEAD, 2, dtype=jnp.float32)
            inv_freq = 1.0 / 10000.0 ** (half_idx / DIM_HEAD)
            t = jnp.arange(n, dtype=jnp.float32)
            freqs = t[:, None] * inv_freq[None, :]
            freqs = jnp.concatenate([freqs, freqs], axis=-1)
            base = (half_idx + 0.4 * DIM_HEAD) / (1.4 * DIM_HEAD)
            power = (t - n // 2) / float(WINDOW // 2)
            scale = base[None, :] ** power[:, None]
            scale = jnp.concatenate([scale, scale], axis=-1)
            cos, sin = (jnp.cos(freqs), jnp.sin(freqs))
            q = q * cos * scale + rotate_half(q) * sin * scale
            k = k * cos / scale + rotate_half(k) * sin / scale
            return (q, k)

        def local_attention(q, k, v):
            b, h, n, d = q.shape
            w = n // WINDOW
            bq = q.reshape(b, h, w, WINDOW, d) * QK_SCALE
            bk = k.reshape(b, h, w, WINDOW, d)
            bv = v.reshape(b, h, w, WINDOW, d)

            def look_around(t):
                p = jnp.pad(t, ((0, 0), (0, 0), (1, 0), (0, 0), (0, 0)))
                return jnp.concatenate([p[:, :, :w], p[:, :, 1:]], axis=3)
            bk, bv = (look_around(bk), look_around(bv))
            bt = jnp.arange(n).reshape(w, WINDOW)
            btp = jnp.pad(bt, ((1, 0), (0, 0)), constant_values=-1)
            btk = jnp.concatenate([btp[:w], btp[1:]], axis=1)
            sim = jnp.einsum('bhwid,bhwjd->bhwij', bq, bk)
            i = bt[:, :, None]
            j = btk[:, None, :]
            mask = (i < j) | (i > j + WINDOW) | (j == -1)
            sim = jnp.where(mask, -jnp.finfo(sim.dtype).max, sim)
            attn = jax.nn.softmax(sim, axis=-1)
            out = jnp.einsum('bhwij,bhwjd->bhwid', attn, bv)
            return out.reshape(b, h, n, d)

        def _layer(x, wqkv, qs, ksc, wo, lg, lb, w1, b1, w2, b2):
            b, n, _ = x.shape
            h = shift_token(x)
            qkv = h @ wqkv
            q, k, v = jnp.split(qkv, 3, axis=-1)
            to_heads = lambda t: t.reshape(b, n, HEADS, DIM_HEAD).transpose(0, 2, 1, 3)
            q, k, v = (to_heads(q), to_heads(k), to_heads(v))
            q = l2norm(q) * qs
            k = l2norm(k) * ksc
            q, k = rotary_xpos(q, k)
            o = local_attention(q, k, v)
            o = o.transpose(0, 2, 1, 3).reshape(b, n, INNER)
            x = x + o @ wo
            h = shift_token(x)
            mu = h.mean(-1, keepdims=True)
            var = h.var(-1, keepdims=True)
            h = (h - mu) / jnp.sqrt(var + 1e-05) * lg + lb
            h = h @ w1 + b1
            a, g = jnp.split(h, 2, axis=-1)
            h = a * jax.nn.gelu(g, approximate=False)
            x = x + h @ w2 + b2
            return x
        key = jax.random.key(seed)
        ks = jax.random.split(key, 6)
        return {'x': jax.random.normal(ks[0], (B, N, DIM), jnp.float32), 'wqkv': jax.random.normal(ks[1], (DEPTH, DIM, 3 * INNER), jnp.float32) * 0.02, 'q_scale': jnp.ones((DEPTH, DIM_HEAD), jnp.float32), 'k_scale': jnp.ones((DEPTH, DIM_HEAD), jnp.float32), 'wo': jax.random.normal(ks[2], (DEPTH, INNER, DIM), jnp.float32) * 0.02, 'ln_g': jnp.ones((DEPTH, DIM), jnp.float32), 'ln_b': jnp.zeros((DEPTH, DIM), jnp.float32), 'w1': jax.random.normal(ks[3], (DEPTH, DIM, 2 * HID), jnp.float32) * 0.02, 'b1': jnp.zeros((DEPTH, 2 * HID), jnp.float32), 'w2': jax.random.normal(ks[4], (DEPTH, HID, DIM), jnp.float32) * 0.02, 'b2': jnp.zeros((DEPTH, DIM), jnp.float32)}
    _L0_ffn_in = _L0_ffn_setup()
    _d = {'L0_attn_x': _L0_attn_in['x'], 'L0_attn_mask': _L0_attn_in['mask'], 'L0_attn_Wq': _L0_attn_in['Wq'], 'L0_attn_Wk': _L0_attn_in['Wk'], 'L0_attn_Wv': _L0_attn_in['Wv'], 'L0_attn_gq': _L0_attn_in['gq'], 'L0_attn_bq': _L0_attn_in['bq'], 'L0_attn_gk': _L0_attn_in['gk'], 'L0_attn_bk': _L0_attn_in['bk'], 'L0_attn_Wo': _L0_attn_in['Wo'], 'L0_attn_bo': _L0_attn_in['bo'], 'L0_ffn_wqkv': _L0_ffn_in['wqkv'], 'L0_ffn_q_scale': _L0_ffn_in['q_scale'], 'L0_ffn_k_scale': _L0_ffn_in['k_scale'], 'L0_ffn_wo': _L0_ffn_in['wo'], 'L0_ffn_ln_g': _L0_ffn_in['ln_g'], 'L0_ffn_ln_b': _L0_ffn_in['ln_b'], 'L0_ffn_w1': _L0_ffn_in['w1'], 'L0_ffn_b1': _L0_ffn_in['b1'], 'L0_ffn_w2': _L0_ffn_in['w2'], 'L0_ffn_b2': _L0_ffn_in['b2']}
    _x0 = _d['L0_attn_x']
    _d['L0_attn_x'] = jax.random.normal(jax.random.fold_in(jax.random.key(seed), 1), (8, 1024, 256), dtype=_x0.dtype)
    del _x0
    return _d

def reference(L0_attn_x, L0_attn_mask, L0_attn_Wq, L0_attn_Wk, L0_attn_Wv, L0_attn_gq, L0_attn_bq, L0_attn_gk, L0_attn_bk, L0_attn_Wo, L0_attn_bo, L0_ffn_wqkv, L0_ffn_q_scale, L0_ffn_k_scale, L0_ffn_wo, L0_ffn_ln_g, L0_ffn_ln_b, L0_ffn_w1, L0_ffn_b1, L0_ffn_w2, L0_ffn_b2):

    def _L0_attn_ref(x, mask, Wq, Wk, Wv, gq, bq, gk, bk, Wo, bo):
        import jax, jax.numpy as jnp
        import numpy as np
        EMB = 256
        H = 16
        D = EMB // H
        EPS = 1e-05
        SM_SCALE = 1.0
        CAUSAL = True
        NEG = -1e+30

        def _layernorm(t, g, b):
            m = jnp.mean(t, axis=-1, keepdims=True)
            v = jnp.mean(jnp.square(t - m), axis=-1, keepdims=True)
            return (t - m) * jax.lax.rsqrt(v + EPS) * g + b
        N, L, _ = x.shape
        q = (x @ Wq.T).reshape(N, L, H, D).transpose(0, 2, 1, 3)
        k = (x @ Wk.T).reshape(N, L, H, D).transpose(0, 2, 1, 3)
        v = (x @ Wv.T).reshape(N, L, H, D).transpose(0, 2, 1, 3)
        q = _layernorm(q, gq, bq)
        k = _layernorm(k, gk, bk)
        scores = jnp.einsum('nhld,nhmd->nhlm', q, k) * SM_SCALE
        if CAUSAL:
            causal = jnp.tril(jnp.ones((L, L), dtype=bool))
            scores = jnp.where(causal, scores, NEG)
        attn = jax.nn.softmax(scores, axis=-1)
        out = jnp.einsum('nhlm,nhmd->nhld', attn, v)
        out = out.transpose(0, 2, 1, 3).reshape(N, L, EMB)
        return out @ Wo.T + bo

    def _L0_ffn_ref(x, wqkv, q_scale, k_scale, wo, ln_g, ln_b, w1, b1, w2, b2):
        import jax, jax.numpy as jnp
        import numpy as np
        DIM = 256
        DEPTH = 2
        HEADS = 8
        DIM_HEAD = 64
        WINDOW = 128
        INNER = HEADS * DIM_HEAD
        HID = int(DIM * 4 * 2 / 3)
        B, N = (2, 2048)
        QK_SCALE = 8.0

        def shift_token(t):
            t1, t2 = jnp.split(t, 2, axis=-1)
            t2 = jnp.pad(t2, ((0, 0), (1, 0), (0, 0)))[:, :-1]
            return jnp.concatenate([t1, t2], axis=-1)

        def l2norm(t):
            return t / jnp.clip(jnp.linalg.norm(t, axis=-1, keepdims=True), 1e-12)

        def rotate_half(x):
            x1, x2 = jnp.split(x, 2, axis=-1)
            return jnp.concatenate([-x2, x1], axis=-1)

        def rotary_xpos(q, k):
            n = q.shape[-2]
            half_idx = jnp.arange(0, DIM_HEAD, 2, dtype=jnp.float32)
            inv_freq = 1.0 / 10000.0 ** (half_idx / DIM_HEAD)
            t = jnp.arange(n, dtype=jnp.float32)
            freqs = t[:, None] * inv_freq[None, :]
            freqs = jnp.concatenate([freqs, freqs], axis=-1)
            base = (half_idx + 0.4 * DIM_HEAD) / (1.4 * DIM_HEAD)
            power = (t - n // 2) / float(WINDOW // 2)
            scale = base[None, :] ** power[:, None]
            scale = jnp.concatenate([scale, scale], axis=-1)
            cos, sin = (jnp.cos(freqs), jnp.sin(freqs))
            q = q * cos * scale + rotate_half(q) * sin * scale
            k = k * cos / scale + rotate_half(k) * sin / scale
            return (q, k)

        def local_attention(q, k, v):
            b, h, n, d = q.shape
            w = n // WINDOW
            bq = q.reshape(b, h, w, WINDOW, d) * QK_SCALE
            bk = k.reshape(b, h, w, WINDOW, d)
            bv = v.reshape(b, h, w, WINDOW, d)

            def look_around(t):
                p = jnp.pad(t, ((0, 0), (0, 0), (1, 0), (0, 0), (0, 0)))
                return jnp.concatenate([p[:, :, :w], p[:, :, 1:]], axis=3)
            bk, bv = (look_around(bk), look_around(bv))
            bt = jnp.arange(n).reshape(w, WINDOW)
            btp = jnp.pad(bt, ((1, 0), (0, 0)), constant_values=-1)
            btk = jnp.concatenate([btp[:w], btp[1:]], axis=1)
            sim = jnp.einsum('bhwid,bhwjd->bhwij', bq, bk)
            i = bt[:, :, None]
            j = btk[:, None, :]
            mask = (i < j) | (i > j + WINDOW) | (j == -1)
            sim = jnp.where(mask, -jnp.finfo(sim.dtype).max, sim)
            attn = jax.nn.softmax(sim, axis=-1)
            out = jnp.einsum('bhwij,bhwjd->bhwid', attn, bv)
            return out.reshape(b, h, n, d)

        def _layer(x, wqkv, qs, ksc, wo, lg, lb, w1, b1, w2, b2):
            b, n, _ = x.shape
            h = shift_token(x)
            qkv = h @ wqkv
            q, k, v = jnp.split(qkv, 3, axis=-1)
            to_heads = lambda t: t.reshape(b, n, HEADS, DIM_HEAD).transpose(0, 2, 1, 3)
            q, k, v = (to_heads(q), to_heads(k), to_heads(v))
            q = l2norm(q) * qs
            k = l2norm(k) * ksc
            q, k = rotary_xpos(q, k)
            o = local_attention(q, k, v)
            o = o.transpose(0, 2, 1, 3).reshape(b, n, INNER)
            x = x + o @ wo
            h = shift_token(x)
            mu = h.mean(-1, keepdims=True)
            var = h.var(-1, keepdims=True)
            h = (h - mu) / jnp.sqrt(var + 1e-05) * lg + lb
            h = h @ w1 + b1
            a, g = jnp.split(h, 2, axis=-1)
            h = a * jax.nn.gelu(g, approximate=False)
            x = x + h @ w2 + b2
            return x
        for l in range(DEPTH):
            x = _layer(x, wqkv[l], q_scale[l], k_scale[l], wo[l], ln_g[l], ln_b[l], w1[l], b1[l], w2[l], b2[l])
        return x
    x = L0_attn_x
    x = _layernorm(x + _L0_attn_ref(x, L0_attn_mask, L0_attn_Wq, L0_attn_Wk, L0_attn_Wv, L0_attn_gq, L0_attn_bq, L0_attn_gk, L0_attn_bk, L0_attn_Wo, L0_attn_bo), axis=-1)
    x = _layernorm(x + _L0_ffn_ref(x, L0_ffn_wqkv, L0_ffn_q_scale, L0_ffn_k_scale, L0_ffn_wo, L0_ffn_ln_g, L0_ffn_ln_b, L0_ffn_w1, L0_ffn_b1, L0_ffn_w2, L0_ffn_b2), axis=-1)
    return x

_drawn_inputs = setup_inputs


def setup_inputs(seed=0):
    import zlib

    import numpy as np

    out = dict(_drawn_inputs(seed))
    spreads = {'L0_attn_gq': (1.0, 0.6),
     'L0_attn_bq': (0.0, 0.8),
     'L0_attn_gk': (1.0, 0.6),
     'L0_attn_bk': (0.0, 0.8),
     'L0_attn_bo': (0.0, 0.1),
     'L0_ffn_q_scale': (1.0, 0.6),
     'L0_ffn_k_scale': (1.0, 0.6),
     'L0_ffn_ln_g': (1.0, 0.6),
     'L0_ffn_ln_b': (0.0, 0.8),
     'L0_ffn_b1': (0.0, 0.8),
     'L0_ffn_b2': (0.0, 0.1)}
    factors = {'L0_ffn_wqkv': 3.032, 'L0_ffn_wo': 2.915}
    for name, (base, spread) in spreads.items():
        noise = np.random.default_rng([zlib.crc32(name.encode()), seed]).standard_normal(out[name].shape)
        drawn = base * np.exp(spread * noise) if base else spread * noise
        out[name] = jnp.asarray(drawn.astype(out[name].dtype))
    for name, factor in factors.items():
        out[name] = (out[name] * factor).astype(out[name].dtype)
    return out
```

```python
from contextlib import ExitStack

import concourse.bass as bass
from concourse import mybir

F32 = mybir.dt.float32
F32R = mybir.dt.float32r
BF16 = mybir.dt.bfloat16
ALU = mybir.AluOpType
ACT = mybir.ActivationFunctionType
AX = mybir.AxisListType

P = 128
BANK = 512
EPS = 1e-5


def wait_alone(eng, sem, value, spare):
    eng.wait_ge(sem, value)
    eng.sem_inc(spare, 1)


def causal_attention(nc, x, w_qkv, w_out, ln_g, ln_b, b_out, ident_in, mask_in, x_mid):
    B, L, E = x.shape
    TILES = L // P
    KC = E // P
    D = 16
    GROUPS = 4
    HG = 4
    GW = 3 * HG * D
    QW = HG * D
    CH = BANK // P
    CHUNKS = TILES // CH
    UNITS = CHUNKS * HG * CH
    BLOCKS = CHUNKS * HG
    TCH = sum(-(-(i + 1) // CH) for i in range(TILES)) * HG
    NT = 3
    assert TCH % NT == 0

    with ExitStack() as ctx:
        def sb(name, shape, dt):
            return ctx.enter_context(nc.sbuf_tensor(name, shape, dt))

        def ps(name, shape, dt=F32):
            return ctx.enter_context(nc.psum_tensor(name, shape, dt))

        def sem(name):
            return ctx.enter_context(nc.semaphore(name))

        ident = sb("a_ident", [P, P], F32)
        ident_b = sb("a_ident_b", [P, P], BF16)
        mask_f = sb("a_mask_f", [P, P], F32)
        mask_b = sb("a_mask_b", [P, P], BF16)
        g_row = sb("a_g_row", [P, 2, HG, D], F32)
        b_row = sb("a_b_row", [P, 2, HG, D], F32)
        bo_row = sb("a_bo_row", [P, E], F32)
        w_hi = sb("a_w_hi", [P, KC, GROUPS, GW], F32R)
        w_lo = sb("a_w_lo", [P, KC, GROUPS, GW], F32R)
        wo_hi = sb("a_wo_hi", [P, GROUPS, E], F32R)
        wo_lo = sb("a_wo_lo", [P, GROUPS, E], F32R)
        xb = sb("a_xb", [P, TILES, E], F32)
        xT_hi = sb("a_xT_hi", [P, KC, L], F32R)
        xT_lo = sb("a_xT_lo", [P, KC, L], F32R)
        qk = sb("a_qk", [P, 2, TILES * HG, D], F32)
        qkc = sb("a_qkc", [P, 2, TILES * HG, D], F32)
        qk_sq = sb("a_qk_sq", [P, 2, TILES * HG, D], F32)
        st = sb("a_st", [P, 5, 2 * TILES * HG], F32)
        qT = sb("a_qT", [P, 2, L], F32R)
        kT = sb("a_kT", [P, 2, L], F32R)
        v_st = sb("a_v_st", [P, TILES, HG * (P + 2 * D)], F32R)
        oT_hi = sb("a_oT_hi", [P, GROUPS, L], F32R)
        oT_lo = sb("a_oT_lo", [P, GROUPS, L], F32R)
        NP = 2
        prob = sb("a_prob", [P, NP, L], F32)
        pT_hi = sb("a_pT_hi", [P, 2, TILES, BANK], F32R)
        pT_lo = sb("a_pT_lo", [P, TILES, BANK], F32R)
        parts = pT_hi[:, 0, :, :].rearrange("p (s t) n -> p s (t n)", s=2).rearrange(
            "p s (m r d) -> p s m r d", r=4, d=D)
        parts_f = parts.bitcast(F32)
        stats = sb("a_stats", [P, 3, UNITS], F32)
        bn = sb("a_bn", [P, TILES, 6], F32)
        mv = sb("a_mv", [P, TILES, 2], F32)
        rstd = sb("a_rstd", [P, 3, TILES], F32)
        zrow = sb("a_zrow", [B, E], F32)
        stage = xb

        S = [ps(f"a_S{i}", [P, 2 * BANK]) for i in range(2)]
        T = [ps(f"a_T{i}", [P, BANK]) for i in range(NT)]
        O = ps("a_O", [P, BANK])
        pX = [S[0][:, 0:BANK], S[0][:, BANK:2 * BANK], S[1][:, 0:BANK], S[1][:, BANK:2 * BANK]]
        pR = [T[0], T[1], T[2], O]

        d_const = [sem(f"a_d_const{i}") for i in range(9)]
        d_x = sem("a_d_x")
        d_y = sem("a_d_y")
        d_z = [sem(f"a_d_z{s}") for s in range(3)]
        w_ready = sem("a_w_ready")
        zero_ready = sem("a_zero_ready")
        xT_done = sem("a_xT_done")
        xT_hi_done = sem("a_xT_hi_done")
        xT_lo_done = sem("a_xT_lo_done")
        qkv_done = sem("a_qkv_done")
        qk_ready = sem("a_qk_ready")
        v_hi_done = sem("a_v_hi_done")
        v_lo_done = sem("a_v_lo_done")
        cen_done = sem("a_cen_done")
        sq_done = sem("a_sq_done")
        gain_done = sem("a_gain_done")
        var_done = sem("a_var_done")
        sd_done = sem("a_sd_done")
        norm_done = sem("a_norm_done")
        part_hi = sem("a_part_hi")
        part_lo = sem("a_part_lo")
        pt_done = sem("a_pt_done")
        pt_act = sem("a_pt_act")
        pt_dve = sem("a_pt_dve")
        s_done = sem("a_s_done")
        max_done = sem("a_max_done")
        exp_done = sem("a_exp_done")
        rec_done = sem("a_rec_done")
        prob_ok = sem("a_prob_ok")
        t_done = sem("a_t_done")
        thi_done = sem("a_thi_done")
        tlo_done = sem("a_tlo_done")
        pv_done = sem("a_pv_done")
        ohi_done = sem("a_ohi_done")
        olo_done = sem("a_olo_done")
        wo_done = sem("a_wo_done")
        res_done = sem("a_res_done")
        veps_done = sem("a_veps_done")
        ysd_done = sem("a_ysd_done")
        bns_done = sem("a_bns_done")
        agg_done = sem("a_agg_done")
        yr_done = sem("a_yr_done")
        y_done = sem("a_y_done")
        xb_bias = sem("a_xb_bias")
        link = sem("a_link")
        glink = sem("a_glink")
        spare = sem("a_spare")

        def v_at(tile, off):
            return v_st[:, tile, :].rearrange("p (h n) -> p h n", h=HG)[:, :, off:off + D]

        unit = [(c, j, ii) for c in range(CHUNKS) for j in range(HG) for ii in range(CH)]
        tch = [(q, m, min(c * CH + ii + 1, m + CH)) for q, (c, j, ii) in enumerate(unit)
               for m in range(0, c * CH + ii + 1, CH)]
        first_tch = [min(n for n, t in enumerate(tch) if t[0] == q) for q in range(UNITS)] + [len(tch)]
        assert len(tch) == TCH

        block = ctx.enter_context(nc.Block())

        @block.sync
        def _(sp):
            for n, (dst, src) in enumerate([
                    (ident[:, :], ident_in), (mask_f[:, :], mask_in),
                    (g_row[:, :, :, :], ln_g), (b_row[:, :, :, :], ln_b), (bo_row[:, :], b_out)]):
                sp.dma_start(dst, src).then_inc(d_const[n], 16)
            for k in range(KC):
                sp.dma_start(stage[:, 4 * k:4 * k + 3, :], w_qkv[:, k]).then_inc(d_const[5 + k], 16)
            sp.wait_ge(w_ready, 2 * KC)
            sp.dma_start(stage[:, 0:GROUPS, :], w_out).then_inc(d_const[7], 16)
            sp.wait_ge(zero_ready, 1)
            for s in range(3):
                sp.dma_start(x_mid[s, :, 0, :], zrow[:, :]).then_inc(d_z[s], 16)
            sp.wait_ge(w_ready, 2 * KC + 2)
            with sp.Fori(0, B) as b:
                sp.wait_ge(y_done, b * TILES + 1)
                sp.dma_start(xb[:, :, :], x[b].rearrange("(t p) e -> p t e", p=P)).then_inc(d_x, 16)
                sp.wait_ge(y_done, b * TILES + TILES + 1)
                sp.dma_start(x_mid[0, b, 1:L + 1, :].rearrange("(t p) e -> p t e", p=P),
                             xb[:, :, :]).then_inc(d_y, 16)
                wait_alone(sp, d_y, b * 16 + 16, spare)
            for s in range(3):
                sp.wait_ge(d_z[s], 16)

        @block.gpsimd
        def _(pool):
            pool.memset(v_st[:, :, :].bitcast(F32), 0.0).then_inc(glink, 1)
            pool.memset(zrow[:, :], 0.0).then_inc(zero_ready, 1)
            pool.wait_ge(glink, 1)
            with pool.Fori(0, B) as b:
                pool.wait_ge(xT_done, b * (TILES // 2) + TILES // 2)
                pool.tensor_tensor(xb[:, :, :], xb[:, :, :], bo_row[:, :].unsqueeze(1).broadcast_to([P, TILES, E]),
                                   ALU.add).then_inc(xb_bias, 1)
                with pool.Fori(0, GROUPS) as g:
                    n = b * GROUPS + g
                    pool.wait_ge(cen_done, n + 1)
                    for s in range(2):
                        pool.tensor_tensor(
                            qk[:, s].rearrange("p (t h) d -> p t (h d)", h=HG),
                            qkc[:, s].rearrange("p (t h) d -> p t (h d)", h=HG),
                            g_row[:, s].rearrange("p h d -> p (h d)").unsqueeze(1).broadcast_to([P, TILES, QW]),
                            ALU.mult).then_inc(gain_done, 1)
                    for q in range(UNITS):
                        c, j, ii = unit[q]
                        w = (c * CH + ii + 1) * P
                        pool.wait_ge(rec_done, n * UNITS + q + 1)
                        pool.tensor_tensor(prob[:, q % NP, 0:w], prob[:, q % NP, 0:w],
                                           stats[:, 2, q:q + 1].broadcast_to([P, w]), ALU.mult).then_inc(prob_ok, 1)

        @block.tensor
        def _(pe):
            pe.wait_ge(w_ready, 2 * KC + 4)
            with pe.Fori(0, B) as b:
                pe.wait_ge(d_x, b * 16 + 16)
                for m in range(TILES // 2):
                    pe.wait_ge(res_done, b * TILES + 1)
                    for k in range(KC):
                        for i in range(2):
                            t = pe.transpose(pX[m][:, (2 * k + i) * P:(2 * k + i + 1) * P],
                                             xb[:, 2 * m + i, k * P:(k + 1) * P], ident[:, :])
                    t.then_inc(xT_done, 1)
                with pe.Fori(0, GROUPS) as g:
                    n = b * GROUPS + g
                    pe.wait_ge(xT_lo_done, b * (TILES // 2) + TILES // 2)
                    for i in range(TILES):
                        if i == 0:
                            pe.wait_ge(exp_done, n * UNITS + 1)
                        o = pX[i // 2][:, (i % 2) * GW:(i % 2 + 1) * GW]
                        passes = [(a, w, k) for k in range(KC) for a, w in
                                  ((xT_hi, w_hi), (xT_lo, w_hi), (xT_hi, w_lo))]
                        for z, (a, w, k) in enumerate(passes):
                            mm = pe.matmul(o, a[:, k, i * P:(i + 1) * P], w[:, k, bass.ds(g, 1), :],
                                           start=(z == 0), stop=(z == len(passes) - 1))
                        if i % 2:
                            mm.then_inc(qkv_done, 1)
                    pe.wait_ge(part_lo, 2 * n + 2)
                    for z in range(8):
                        s, p, c = z // 4, z // 2 % 2, z % 2
                        if z < 4:
                            if z == 0:
                                pe.wait_ge(tlo_done, n * TCH + 1)
                                pe.wait_ge(olo_done, n * CHUNKS + 1)
                        elif z % 2 == 0:
                            pe.wait_ge(pt_act, n * 4 + (z - 4) // 2 + 1)
                        else:
                            pe.wait_ge(pt_dve, n * 4 + (z - 4) // 2 + 1)
                        for ii in range(CH):
                            i = c * CH + ii
                            t = pe.transpose(
                                pR[z % 4][:, ii * P:(ii + 1) * P],
                                parts_f[:, s, i * HG + 2 * p:i * HG + 2 * p + 2].rearrange("p m r d -> p (m r d)"),
                                ident[:, :])
                        t.then_inc(pt_done, 1)

                    def scores(q):
                        c, j, ii = unit[q]
                        i, r, p = c * CH + ii, j % 2, j // 2
                        w = (i + 1) * P
                        if q == 0:
                            pe.wait_ge(pt_act, n * 4 + 4)
                            pe.wait_ge(pt_dve, n * 4 + 4)
                            pe.wait_ge(v_hi_done, n * 4 + 4)
                            pe.wait_ge(v_lo_done, n * 4 + 4)
                        if q >= 2:
                            pe.wait_ge(exp_done, n * UNITS + q)
                        out = S[q % 2]
                        for k0 in range(0, w, BANK):
                            k1 = min(w, k0 + BANK)
                            pe.matmul(out[:, k0:k1], qT[64 * r:64 * r + 64, p, i * P:(i + 1) * P],
                                      kT[64 * r:64 * r + 64, p, k0:k1], start=True, stop=(k1 < w))
                        pe.matmul(out[:, i * P:w], ident_b[:, :], mask_b[:, :], start=False, stop=True,
                                  ).then_inc(s_done, 1)

                    def turn(q):
                        pe.wait_ge(prob_ok, n * UNITS + q + 1)
                        for z in range(first_tch[q], first_tch[q + 1]):
                            _, k0, k1 = tch[z]
                            if z >= NT:
                                pe.wait_ge(tlo_done, n * TCH + z - NT + 2)
                            for kt in range(k0, k1):
                                t = pe.transpose(T[z % NT][:, (kt - k0) * P:(kt - k0 + 1) * P],
                                                 prob[:, q % NP, kt * P:(kt + 1) * P], ident[:, :])
                            t.then_inc(t_done, 1)

                    def mix(v):
                        c, j = v // HG, v % HG
                        pe.wait_ge(tlo_done, n * TCH + first_tch[CH * v + CH] + 1)
                        if j == 0 and c:
                            pe.wait_ge(olo_done, n * CHUNKS + c + 1)
                        for kt in range((c + 1) * CH):
                            off = max(0, kt - c * CH) * P
                            for a in (pT_hi[:, v % 2], pT_lo):
                                mm = pe.matmul(O[:, off:BANK], v_st[:, kt, j * P:(j + 1) * P], a[:, kt, off:BANK],
                                               start=(j == 0 and kt == 0 and a is not pT_lo),
                                               stop=(j == HG - 1 and kt == (c + 1) * CH - 1 and a is pT_lo))
                        mm.then_inc(pv_done, 1)

                    for q in range(UNITS + 3):
                        if q < UNITS:
                            scores(q)
                        if q >= 3 and (q - 3) % CH == CH - 1:
                            mix((q - 3) // CH)
                        if 2 <= q < UNITS + 2:
                            turn(q - 2)
                pe.wait_ge(olo_done, (b + 1) * GROUPS * CHUNKS + 1)
                for i in range(TILES):
                    o = pX[i // 2][:, (i % 2) * E:(i % 2 + 1) * E]
                    passes = [(a, w, k) for k in range(GROUPS) for a, w in
                              ((oT_hi, wo_hi), (oT_lo, wo_hi), (oT_hi, wo_lo))]
                    for z, (a, w, k) in enumerate(passes):
                        mm = pe.matmul(o, a[:, k, i * P:(i + 1) * P], w[:, k, :],
                                       start=(z == 0), stop=(z == len(passes) - 1))
                    mm.then_inc(wo_done, 1)

        @block.scalar
        def _(act):
            act.nop().then_inc(exp_done, 1)
            with act.Fori(0, B) as b:
                for m in range(TILES // 2):
                    act.wait_ge(xT_done, b * (TILES // 2) + m + 1)
                    act.activation(xT_hi[:, :, 2 * m * P:(2 * m + 2) * P],
                                   pX[m].rearrange("p (k n) -> p k n", k=KC), ACT.Copy).then_inc(xT_hi_done, 1)
                with act.Fori(0, GROUPS) as g:
                    n = b * GROUPS + g
                    for m in range(TILES // 2):
                        act.wait_ge(qkv_done, n * 4 + m + 1)
                        src = pX[m][:, 0:2 * GW].rearrange("p (i s h d) -> p i s h d", i=2, s=3, h=HG)
                        for s in range(2):
                            act.activation(qk[:, s, 2 * m * HG:(2 * m + 2) * HG, :].rearrange(
                                "p (i h) d -> p i (h d)", i=2), src[:, :, s].rearrange("p i h d -> p i (h d)"),
                                ACT.Copy).then_inc(qk_ready, 1)
                        for i in range(2):
                            t = act.activation(v_at(2 * m + i, 0), src[:, i, 2], ACT.Copy)
                        t.then_inc(v_hi_done, 1)
                    act.wait_ge(cen_done, n + 1)
                    act.activation(qk_sq[:, :, :, :], qkc[:, :, :, :], ACT.Square).then_inc(sq_done, 1)
                    act.wait_ge(var_done, n + 1)
                    act.activation(st[:, 2, :], st[:, 1, :], ACT.Sqrt).then_inc(sd_done, 1)
                    act.wait_ge(norm_done, n + 1)
                    act.activation(parts[:, 0, :, 0:2, :], qkc[:, 0].unsqueeze(2).broadcast_to([P, TILES * HG, 2, D]),
                                   ACT.Copy).then_inc(part_hi, 1)
                    act.activation(parts[:, 1, :, 0:4:2, :], qkc[:, 1].unsqueeze(2).broadcast_to([P, TILES * HG, 2, D]),
                                   ACT.Copy).then_inc(part_hi, 1)
                    for z in range(0, 8, 2):
                        s, p, c = z // 4, z // 2 % 2, z % 2
                        act.wait_ge(pt_done, n * 8 + z + 1)
                        act.activation((qT, kT)[s][:, p, c * BANK:(c + 1) * BANK], pR[z % 4][:, :],
                                       ACT.Copy).then_inc(pt_act, 1)

                    def expo(q):
                        c, j, ii = unit[q]
                        w = (c * CH + ii + 1) * P
                        act.wait_ge(max_done, n * UNITS + q + 1)
                        if q >= NP:
                            act.wait_ge(t_done, n * TCH + first_tch[q - NP + 1])
                        act.activation(prob[:, q % NP, 0:w], S[q % 2][:, 0:w], ACT.Exp, bias=stats[:, 0, q:q + 1],
                                       accum_out=stats[:, 1, q:q + 1]).then_inc(exp_done, 1)

                    def turned(q):
                        c, j, ii = unit[q]
                        v = q // CH
                        if v >= 2 and ii == 0:
                            act.wait_ge(pv_done, n * BLOCKS + v - 1)
                        for z in range(first_tch[q], first_tch[q + 1]):
                            _, k0, k1 = tch[z]
                            act.wait_ge(t_done, n * TCH + z + 1)
                            act.activation(pT_hi[:, v % 2, k0:k1, ii * P:(ii + 1) * P],
                                           T[z % NT][:, 0:(k1 - k0) * P].rearrange("p (k n) -> p k n", n=P),
                                           ACT.Copy).then_inc(thi_done, 1)

                    def taken(c):
                        act.wait_ge(pv_done, n * BLOCKS + (c + 1) * HG)
                        act.activation(oT_hi[:, bass.ds(g, 1), c * BANK:(c + 1) * BANK], O[:, :],
                                       ACT.Copy).then_inc(ohi_done, 1)

                    for q in range(UNITS + 4):
                        if q < UNITS:
                            expo(q)
                        if 2 <= q < UNITS + 2:
                            turned(q - 2)
                        if q >= 4 and (q - 4) % (CH * HG) == CH * HG - 1:
                            taken((q - 4) // (CH * HG))
                act.wait_ge(veps_done, b + 1)
                act.activation(rstd[:, 1, :], rstd[:, 0, :], ACT.Sqrt).then_inc(ysd_done, 1)

        @block.vector
        def _(dve):
            count = [0]

            def chain(ins, base):
                count[0] += 1
                ins.then_inc(link, 1)
                dve.wait_ge(link, base + count[0])

            dve.wait_ge(d_const[0], 16)
            for k in range(KC):
                dve.wait_ge(d_const[5 + k], 16)
                src = stage[:, 4 * k:4 * k + 3, :].rearrange("p a e -> p (a e)")
                wh, wl = (w[:, k].rearrange("p g n -> p (g n)") for w in (w_hi, w_lo))
                dve.tensor_copy(wh, src).then_inc(w_ready, 1)
                dve.wait_ge(w_ready, 2 * k + 1)
                dve.tensor_tensor(wl, src, wh.bitcast(F32), ALU.subtract).then_inc(w_ready, 1)
            dve.wait_ge(d_const[7], 16)
            dve.tensor_copy(wo_hi[:, :, :], stage[:, 0:GROUPS, :]).then_inc(w_ready, 1)
            dve.wait_ge(w_ready, 2 * KC + 1)
            dve.tensor_tensor(wo_lo[:, :, :], stage[:, 0:GROUPS, :], wo_hi[:, :, :].bitcast(F32),
                              ALU.subtract).then_inc(w_ready, 1)
            dve.tensor_copy(ident_b[:, :], ident[:, :]).then_inc(w_ready, 1)
            dve.wait_ge(d_const[1], 16)
            dve.tensor_copy(mask_b[:, :], mask_f[:, :]).then_inc(w_ready, 1)
            for n in range(2, 5):
                dve.wait_ge(d_const[n], 16)
            dve.nop().then_inc(y_done, 1)
            dve.nop().then_inc(res_done, 1)
            dve.nop().then_inc(tlo_done, 1)
            dve.nop().then_inc(olo_done, 1)
            LINKS = 4
            with dve.Fori(0, B) as b:
                for m in range(TILES // 2):
                    dve.wait_ge(xT_hi_done, b * (TILES // 2) + m + 1)
                    dst = slice(2 * m * P, (2 * m + 2) * P)
                    dve.tensor_tensor(xT_lo[:, :, dst], pX[m].rearrange("p (k n) -> p k n", k=KC),
                                      xT_hi[:, :, dst].bitcast(F32), ALU.subtract).then_inc(xT_lo_done, 1)
                with dve.Fori(0, GROUPS) as g:
                    n = b * GROUPS + g
                    count[0] = 0
                    base = n * LINKS
                    for m in range(TILES // 2):
                        dve.wait_ge(v_hi_done, n * 4 + m + 1)
                        src = pX[m][:, 0:2 * GW].rearrange("p (i s h d) -> p i s h d", i=2, s=3, h=HG)
                        for i in range(2):
                            t = dve.tensor_tensor(v_at(2 * m + i, D), src[:, i, 2],
                                                  v_at(2 * m + i, 0).bitcast(F32), ALU.subtract)
                        t.then_inc(v_lo_done, 1)
                    dve.wait_ge(qk_ready, n * 8 + 8)
                    qk_m = qk[:, :, :, :].rearrange("p s m d -> p (s m) d")
                    cen_m = qkc[:, :, :, :].rearrange("p s m d -> p (s m) d")
                    M = 2 * TILES * HG
                    chain(dve.tensor_reduce(st[:, 0, :], qk_m, AX.X, ALU.add), base)
                    dve.scalar_tensor_tensor(cen_m, st[:, 0, :].unsqueeze(2).broadcast_to([P, M, D]),
                                             -1.0 / D, qk_m, ALU.mult, ALU.add).then_inc(cen_done, 1)
                    dve.wait_ge(sq_done, n + 1)
                    chain(dve.tensor_reduce(st[:, 0, :], qk_sq[:, :, :, :].rearrange("p s m d -> p (s m) d"),
                                            AX.X, ALU.add), base)
                    dve.tensor_scalar(st[:, 1, :], st[:, 0, :], 1.0 / D, EPS, ALU.mult, ALU.add).then_inc(var_done, 1)
                    dve.wait_ge(sd_done, n + 1)
                    chain(dve.reciprocal(st[:, 0, :], st[:, 2, :]), base)
                    dve.wait_ge(gain_done, 2 * n + 2)
                    chain(dve.tensor_tensor(qk_m, qk_m, st[:, 0, :].unsqueeze(2).broadcast_to([P, M, D]),
                                            ALU.mult), base)
                    for s in range(2):
                        t = dve.tensor_tensor(
                            qkc[:, s].rearrange("p (t h) d -> p t (h d)", h=HG),
                            qk[:, s].rearrange("p (t h) d -> p t (h d)", h=HG),
                            b_row[:, s].rearrange("p h d -> p (h d)").unsqueeze(1).broadcast_to([P, TILES, QW]), ALU.add)
                    t.then_inc(norm_done, 1)
                    assert count[0] == LINKS
                    dve.wait_ge(part_hi, 2 * n + 1)
                    dve.wait_ge(norm_done, n + 1)
                    dve.tensor_tensor(parts[:, 0, :, 2:4, :],
                                      qkc[:, 0].unsqueeze(2).broadcast_to([P, TILES * HG, 2, D]),
                                      parts_f[:, 0, :, 0:2, :], ALU.subtract).then_inc(part_lo, 1)
                    dve.wait_ge(part_hi, 2 * n + 2)
                    dve.tensor_tensor(parts[:, 1, :, 1:4:2, :],
                                      qkc[:, 1].unsqueeze(2).broadcast_to([P, TILES * HG, 2, D]),
                                      parts_f[:, 1, :, 0:4:2, :], ALU.subtract).then_inc(part_lo, 1)
                    for z in range(1, 8, 2):
                        s, p, c = z // 4, z // 2 % 2, z % 2
                        dve.wait_ge(pt_done, n * 8 + z + 1)
                        dve.tensor_copy((qT, kT)[s][:, p, c * BANK:(c + 1) * BANK], pR[z % 4][:, :]).then_inc(pt_dve, 1)

                    def maximum(q):
                        c, j, ii = unit[q]
                        w = (c * CH + ii + 1) * P
                        dve.wait_ge(s_done, n * UNITS + q + 1)
                        dve.tensor_reduce(stats[:, 0, q:q + 1], S[q % 2][:, 0:w], AX.X, ALU.max,
                                          negate=True).then_inc(max_done, 1)

                    def total(q):
                        dve.wait_ge(exp_done, n * UNITS + q + 2)
                        dve.reciprocal(stats[:, 2, q:q + 1], stats[:, 1, q:q + 1]).then_inc(rec_done, 1)

                    def turned(q):
                        c, j, ii = unit[q]
                        v = q // CH
                        if ii == 0 and v >= 1:
                            dve.wait_ge(pv_done, n * BLOCKS + v)
                        for z in range(first_tch[q], first_tch[q + 1]):
                            _, k0, k1 = tch[z]
                            dve.wait_ge(thi_done, n * TCH + z + 1)
                            dve.tensor_tensor(pT_lo[:, k0:k1, ii * P:(ii + 1) * P],
                                              T[z % NT][:, 0:(k1 - k0) * P].rearrange("p (k n) -> p k n", n=P),
                                              pT_hi[:, v % 2, k0:k1, ii * P:(ii + 1) * P].bitcast(F32),
                                              ALU.subtract).then_inc(tlo_done, 1)

                    def taken(c):
                        dve.wait_ge(ohi_done, n * CHUNKS + c + 1)
                        dve.tensor_tensor(oT_lo[:, bass.ds(g, 1), c * BANK:(c + 1) * BANK], O[:, :],
                                          oT_hi[:, bass.ds(g, 1), c * BANK:(c + 1) * BANK].bitcast(F32),
                                          ALU.subtract).then_inc(olo_done, 1)

                    for q in range(UNITS + 4):
                        if q < UNITS:
                            maximum(q)
                        if 1 <= q < UNITS + 1:
                            total(q - 1)
                        if 2 <= q < UNITS + 2:
                            turned(q - 2)
                        if q >= 4 and (q - 4) % (CH * HG) == CH * HG - 1:
                            taken((q - 4) // (CH * HG))
                dve.wait_ge(xb_bias, b + 1)
                for i in range(TILES):
                    dve.wait_ge(wo_done, b * TILES + (i | 1) + 1)
                    dve.tensor_tensor(xb[:, i, :], pX[i // 2][:, (i % 2) * E:(i % 2 + 1) * E], xb[:, i, :],
                                      ALU.add).then_inc(res_done, 1)
                for i in range(TILES):
                    dve.wait_ge(res_done, b * TILES + i + 2)
                    dve.bn_stats(bn[:, i, :], xb[:, i, :]).then_inc(bns_done, 1)
                for i in range(TILES):
                    if i == 0:
                        wait_alone(dve, bns_done, (b + 1) * TILES, spare)
                    dve.bn_aggr(mv[:, i, :], bn[:, i, :]).then_inc(agg_done, 1)
                dve.wait_ge(agg_done, (b + 1) * TILES)
                dve.tensor_scalar(rstd[:, 0, :], mv[:, :, 1], EPS, None, ALU.add).then_inc(veps_done, 1)
                dve.wait_ge(ysd_done, b + 1)
                dve.reciprocal(rstd[:, 2, :], rstd[:, 1, :]).then_inc(yr_done, 1)
                dve.wait_ge(yr_done, b + 1)
                for i in range(TILES):
                    dve.tensor_scalar(xb[:, i, :], xb[:, i, :], mv[:, i, 0:1], rstd[:, 2, i:i + 1],
                                      ALU.subtract, ALU.mult).then_inc(y_done, 1)


def local_layers(nc, xs, out, rot, rot_scale, w_qkv, w_out, ident_in, mask_in, ln_gb, w1, b1, w2, b2):
    LAYERS, B = 2, xs.shape[1]
    L = xs.shape[2] - 1
    E = xs.shape[3]
    H, D = 8, 64
    W = H * D
    KC = E // P
    OC = W // P
    PAIRS = L // P // 2
    HH = H // 2
    HID = w1.shape[3] // 2
    FT = -(-HID // P)
    FR = [min(P, HID - f * P) for f in range(FT)]
    GT = 4
    NG = L // P // GT

    with ExitStack() as ctx:
        def keep(name, shape, dt):
            return ctx.enter_context(nc.sbuf_tensor(name, shape, dt))

        def ps(name, shape, dt=F32):
            return ctx.enter_context(nc.psum_tensor(name, shape, dt))

        def sem(name):
            return ctx.enter_context(nc.semaphore(name))

        ident = keep("l_ident", [P, P], F32)
        ident_b = keep("l_ident_b", [P, P], BF16)
        mask_f = keep("l_mask_f", [P, PAIRS + 1, 2, P], F32)
        mask_b = keep("l_mask_b", [P, PAIRS + 1, 2, P], BF16)
        rot_sb = keep("l_rot", [P, 2 * PAIRS, 4, D], F32)
        rsc = keep("l_rsc", [P, 4, D], F32)
        tab = keep("l_tab", [P, 2 * PAIRS, 4, D], F32)
        wq_hi = keep("l_wq_hi", [P, KC, 3 * W], F32R)
        wq_lo = keep("l_wq_lo", [P, KC, 3 * W], F32R)
        wo_hi = keep("l_wo_hi", [P, OC, E], F32R)
        wo_lo = keep("l_wo_lo", [P, OC, E], F32R)
        stage = keep("l_stage", [P, max(2 * HID, FT * E)], F32)
        w1_hi = keep("l_w1_hi", [P, KC, 2 * HID], F32R)
        w1_lo = keep("l_w1_lo", [P, KC, 2 * HID], F32R)
        w2_hi = keep("l_w2_hi", [P, FT, E], F32R)
        w2_lo = keep("l_w2_lo", [P, FT, E], F32R)
        b2_row = keep("l_b2", [P, E], F32)
        b1_col = keep("l_b1", [P, 2, FT], F32)
        gb_col = keep("l_gb", [P, 2, KC], F32)
        half = keep("l_half", [P, 2 * H], F32)

        k_hi = keep("l_k_hi", [P, H, 2, P], F32R)
        k_lo = keep("l_k_lo", [P, H, 2, P], F32R)
        v_hi = keep("l_v_hi", [P, 2, H, D], F32R)
        v_lo = keep("l_v_lo", [P, 2, H, D], F32R)
        F = [ps(f"l_F{i}", [P, BANK]) for i in range(3)]
        S = ps("l_S", [P, HH, 2 * P])
        T = ps("l_T", [P, 2, BANK])
        O = ps("l_O", [P, BANK])

        d_c = [sem(f"l_d_c{i}") for i in range(14)]
        const_ok = sem("l_const_ok")
        split = sem("l_split")
        phase = sem("l_phase")
        spare = sem("l_spare")

        place = ExitStack()

        def sb(name, shape, dt):
            return place.enter_context(nc.sbuf_tensor(name, shape, dt))

        xt = sb("l_xt", [P, 2, E], F32)
        h2 = sb("l_h2", [P, 2, P], F32)
        hT_hi = sb("l_hT_hi", [P, 2, KC, P], F32R)
        hT_lo = sb("l_hT_lo", [P, 2, KC, P], F32R)
        qk = sb("l_qk", [P, 2, W], F32)
        sq = sb("l_sq", [P, 2 * H, D], F32)
        ss = sb("l_ss", [P, 2, 2 * H], F32)
        rn = sb("l_rn", [P, 2, 2 * H], F32)
        ta = sb("l_ta", [P, 2, H, D], F32)
        tb = sb("l_tb", [P, 2, H, D], F32)
        qd = sb("l_qd", [P, 2, H, 2, D], F32)
        q_st = sb("l_q_st", [P, H, P], F32R)
        mx = sb("l_mx", [P, 4, H], F32)
        prob = sb("l_prob", [P, H, 2, P], F32)
        pT_hi = sb("l_pT_hi", [P, 2, HH, 2, P], F32R)
        pT_lo = sb("l_pT_lo", [P, 2, HH, 2, P], F32R)
        osb = sb("l_osb", [P, H, D], F32)
        oT_hi = sb("l_oT_hi", [P, OC, P], F32R)
        oT_lo = sb("l_oT_lo", [P, OC, P], F32R)
        yb = sb("l_yb", [P, 2, E], F32)

        d_x = [sem(f"l_d_x{i}") for i in range(2)]
        d_h = [sem(f"l_d_h{i}") for i in range(2)]
        d_y = [sem(f"l_d_y{i}") for i in range(2)]
        hT_done = sem("l_hT_done")
        hT_hi_ok = sem("l_hT_hi_ok")
        hT_lo_ok = sem("l_hT_lo_ok")
        qkv_done = sem("l_qkv_done")
        qk_ok = sem("l_qk_ok")
        sq_ok = sem("l_sq_ok")
        vhi_ok = sem("l_vhi_ok")
        vlo_ok = sem("l_vlo_ok")
        ss_ok = sem("l_ss_ok")
        rn_ok = sem("l_rn_ok")
        qr_ok = sem("l_qr_ok")
        kr_ok = sem("l_kr_ok")
        qkT_done = sem("l_qkT_done")
        st_hi_ok = sem("l_st_hi_ok")
        st_lo_ok = sem("l_st_lo_ok")
        s_done = sem("l_s_done")
        mx_ok = sem("l_mx_ok")
        exp_ok = sem("l_exp_ok")
        ri_ok = sem("l_ri_ok")
        pT_done = sem("l_pT_done")
        pT_hi_ok = sem("l_pT_hi_ok")
        pT_lo_ok = sem("l_pT_lo_ok")
        pv_done = sem("l_pv_done")
        osb_ok = sem("l_osb_ok")
        oT_done = sem("l_oT_done")
        oT_hi_ok = sem("l_oT_hi_ok")
        oT_lo_ok = sem("l_oT_lo_ok")
        wo_done = sem("l_wo_done")
        y_ok = sem("l_y_ok")
        vch = sem("l_vch")
        gch = sem("l_gch")

        place.close()

        mxt = sb("m_x", [P, GT, E], F32)
        mh2 = sb("m_h2", [P, GT, P], F32)
        mz = sb("m_z", [P, GT, E], F32)
        mbn = sb("m_bn", [P, GT, 2, 6], F32)
        mmv = sb("m_mv", [P, GT, 2], F32)
        mrs = sb("m_rs", [P, 2, GT], F32)
        zT = sb("m_zT", [P, KC, GT * P], F32)
        zT_hi = sb("m_zT_hi", [P, KC, GT * P], F32R)
        zT_lo = sb("m_zT_lo", [P, KC, GT * P], F32R)
        gel = sb("m_gel", [P, 2, BANK], F32)
        hid = sb("m_hid", [P, 2, BANK], F32)
        hid_hi = sb("m_hid_hi", [P, FT, BANK], F32R)
        hid_lo = sb("m_hid_lo", [P, FT, BANK], F32R)
        my = sb("m_y", [P, GT, E], F32)
        A = [F[0], T[:, 0, :]]
        G = [F[1], T[:, 1, :]]
        ZT = [S[:, :, :].rearrange("p h n -> p (h n)")[:, 0:BANK], S[:, :, :].rearrange("p h n -> p (h n)")[:, BANK:]]
        Y = [F[2], O]
        place.close()
        d_mx, d_mh, d_my = sem("m_d_x"), sem("m_d_h"), sem("m_d_y")
        bn_ok = sem("m_bn_ok")
        ve_ok = sem("m_ve_ok")
        rs_ok = sem("m_rs_ok")
        z_ok = sem("m_z_ok")
        zT_done = sem("m_zT_done")
        zT_ok = sem("m_zT_ok")
        zhi_ok = sem("m_zhi_ok")
        zlo_ok = sem("m_zlo_ok")
        ag_done = sem("m_ag_done")
        gel_ok = sem("m_gel_ok")
        hid_ok = sem("m_hid_ok")
        hhi_ok = sem("m_hhi_ok")
        hlo_ok = sem("m_hlo_ok")
        w2_done = sem("m_w2_done")
        xb_ok = sem("m_xb_ok")
        my_ok = sem("m_y_ok")

        d_fx, d_fy, d_fo = sem("f_d_x"), sem("f_d_y"), sem("f_d_o")
        f_add, f_bn, f_ag, f_rs, f_ok = (sem(f"f_{n}") for n in ("add", "bn", "ag", "rs", "ok"))

        ENGINES = 5

        def meet(eng, k):
            eng.drain().then_inc(phase, 1)
            wait_alone(eng, phase, ENGINES * k, spare)

        block = ctx.enter_context(nc.Block())

        @block.sync
        def _(sp):
            for n, (dst, src) in enumerate([(ident[:, :], ident_in), (mask_f[:, :, :, :], mask_in),
                                            (rot_sb[:, :, :, :], rot)]):
                sp.dma_start(dst, src).then_inc(d_c[n], 16)
            with sp.Fori(0, LAYERS) as l:
                SPLITS = 2 * (2 * KC + KC + 2)
                parts = ([w_qkv[l, :, k, a * 3 * W // 2:(a + 1) * 3 * W // 2] for k in range(KC) for a in range(2)]
                         + [w1[l, :, k, :] for k in range(KC)] + [w_out[l], w2[l]])
                small = [(rsc[:, :, :], rot_scale[l]), (gb_col[:, :, :], ln_gb[l]), (b1_col[:, :, :], b1[l]),
                         (b2_row[:, :], b2[l])]
                for n, (dst, src) in enumerate(small):
                    sp.dma_start(dst, src).then_inc(d_c[3 + n], 16)
                for n, src in enumerate(parts):
                    if n:
                        sp.wait_ge(split, l * SPLITS + 2 * n)
                    src = src if len(src.shape) == 2 else src.rearrange("p a b -> p (a b)")
                    sp.dma_start(stage[:, 0:src.shape[1]], src).then_inc(d_c[7], 16)
                with sp.Fori(0, B) as b:
                    with sp.Fori(0, PAIRS) as i:
                        m = (l * B + b) * PAIRS + i
                        for u in range(2):
                            sp.wait_ge(y_ok, 2 * m + u + 1)
                            r = (2 * i + u) * P
                            sp.dma_start(xt[:, u, :], xs[l, b, bass.ds(r + 1, P), :]).then_inc(d_x[u], 16)
                            sp.dma_start(h2[:, u, :], xs[l, b, bass.ds(r, P), P:E]).then_inc(d_h[u], 16)
                            sp.wait_ge(y_ok, 2 * m + u + 2)
                            sp.dma_start(xs[2, b, bass.ds(r + 1, P), :], yb[:, u, :]).then_inc(d_y[u], 16)
                            wait_alone(sp, d_y[u], 16 * (m + 1), spare)
                meet(sp, 2 * l + 1)
                with sp.Fori(0, B) as b:
                    with sp.Fori(0, NG) as g:
                        m = (l * B + b) * NG + g
                        r = g * GT * P
                        sp.dma_start(mxt[:, :, :], xs[2, b, bass.ds(r + 1, GT * P), :].rearrange(
                            "(t p) e -> p t e", p=P)).then_inc(d_mx, 16)
                        sp.dma_start(mh2[:, :, :], xs[2, b, bass.ds(r, GT * P), P:E].rearrange(
                            "(t p) e -> p t e", p=P)).then_inc(d_mh, 16)
                        sp.wait_ge(my_ok, GT * (m + 1))
                        sp.dma_start(xs[1, b, bass.ds(r + 1, GT * P), :].rearrange("(t p) e -> p t e", p=P),
                                     my[:, :, :]).then_inc(d_my, 16)
                        wait_alone(sp, d_my, 16 * (m + 1), spare)
                meet(sp, 2 * l + 2)
                
            with sp.Fori(0, B) as b:
                with sp.Fori(0, NG) as g:
                    m = b * NG + g
                    r = g * GT * P
                    sp.dma_start(mxt[:, :, :], xs[0, b, bass.ds(r + 1, GT * P), :].rearrange(
                        "(t p) e -> p t e", p=P)).then_inc(d_fx, 16)
                    sp.dma_start(mz[:, :, :], xs[1, b, bass.ds(r + 1, GT * P), :].rearrange(
                        "(t p) e -> p t e", p=P)).then_inc(d_fy, 16)
                    sp.wait_ge(f_ok, GT * (m + 1))
                    sp.dma_start(out[b, bass.ds(r, GT * P), :].rearrange("(t p) e -> p t e", p=P),
                                 my[:, :, :]).then_inc(d_fo, 16)
                    wait_alone(sp, d_fo, 16 * (m + 1), spare)

        @block.gpsimd
        def _(pool):
            pool.memset(half[:, :], -0.5).then_inc(gch, 1)
            for t in (k_hi, k_lo):
                pool.memset(t[:, :, 1, :].bitcast(F32), 0.0).then_inc(const_ok, 1)
            for t in (v_hi, v_lo):
                pool.memset(t[:, 1, :, :].bitcast(F32), 0.0).then_inc(const_ok, 1)
            pool.wait_ge(gch, 1)
            with pool.Fori(0, LAYERS) as l:
                with pool.Fori(0, B) as b:
                    with pool.Fori(0, PAIRS) as i:
                        m = (l * B + b) * PAIRS + i
                        for u in range(2):
                            t = 2 * m + u
                            tile = bass.ds(2 * i + u, 1)
                            base = 2 * t + 1
                            pool.wait_ge(qk_ok, 2 * t + 2)
                            k3 = qk[:, 1, :].rearrange("p (h d) -> p h d", h=H)

                            def row(z, a, c):
                                return tab[:, tile, z, a:c].broadcast_to([P, H, c - a])
                            pool.tensor_tensor(ta[:, 1], k3, row(2, 0, D), ALU.mult)
                            pool.tensor_tensor(tb[:, 1, :, 0:D // 2], k3[:, :, D // 2:D], row(3, 0, D // 2), ALU.mult)
                            pool.tensor_tensor(tb[:, 1, :, D // 2:D], k3[:, :, 0:D // 2], row(3, D // 2, D),
                                               ALU.mult).then_inc(gch, 1)
                            pool.wait_ge(gch, base + 1)
                            pool.tensor_tensor(ta[:, 1], ta[:, 1], tb[:, 1], ALU.add).then_inc(gch, 1)
                            pool.wait_ge(ss_ok, t + 1)
                            pool.tensor_tensor(rn[:, u, :], ss[:, 1, :], half[:, :], ALU.pow).then_inc(rn_ok, 1)
                            pool.wait_ge(rn_ok, t + 1)
                            pool.wait_ge(gch, base + 2)
                            for c in range(2):
                                kk = pool.tensor_tensor(qd[:, 1, :, c, :], ta[:, 1],
                                                        rn[:, u, H:2 * H].unsqueeze(2).broadcast_to([P, H, D]), ALU.mult)
                            kk.then_inc(kr_ok, 1)
                meet(pool, 2 * l + 1)
                with pool.Fori(0, B) as b:
                    with pool.Fori(0, NG) as g:
                        m = (l * B + b) * NG + g
                        pool.wait_ge(ve_ok, m + 1)
                        pool.tensor_tensor(mrs[:, 1, :], mrs[:, 0, :], half[:, 0:GT], ALU.pow).then_inc(rs_ok, 1)
                        pool.wait_ge(d_mx, 16 * (m + 1))
                        pool.wait_ge(z_ok, m + 1)
                        pool.tensor_tensor(mxt[:, :, :], mxt[:, :, :], b2_row[:, :].unsqueeze(1).broadcast_to([P, GT, E]),
                                           ALU.add).then_inc(xb_ok, 1)
                        for f in range(FT):
                            r = FR[f]
                            pool.wait_ge(hhi_ok, m * FT + f + 1)
                            pool.tensor_tensor(hid_lo[0:r, f, :], hid[0:r, f % 2, :], hid_hi[0:r, f, :].bitcast(F32),
                                               ALU.subtract).then_inc(hlo_ok, 1)
                meet(pool, 2 * l + 2)
                
            with pool.Fori(0, B) as b:
                with pool.Fori(0, NG) as g:
                    m = b * NG + g
                    pool.wait_ge(f_ag, m + 1)
                    pool.tensor_tensor(mrs[:, 1, :], mrs[:, 0, :], half[:, 0:GT], ALU.pow).then_inc(f_rs, 1)

        @block.tensor
        def _(pe):
            pe.wait_ge(const_ok, 4 + 2)
            with pe.Fori(0, LAYERS) as l:
                wait_alone(pe, split, (l + 1) * 2 * (3 * KC + 2), spare)
                with pe.Fori(0, B) as b:
                    with pe.Fori(0, PAIRS) as i:
                        m = (l * B + b) * PAIRS + i
                        for u in range(2):
                            t = 2 * m + u
                            pe.wait_ge(d_x[u], 16 * (m + 1))
                            pe.wait_ge(d_h[u], 16 * (m + 1))
                            pe.transpose(F[0][:, 0:P], xt[:, u, 0:P], ident[:, :])
                            pe.transpose(F[0][:, P:2 * P], h2[:, u, :], ident[:, :]).then_inc(hT_done, 1)
                            pe.wait_ge(hT_lo_ok, t + 1)
                            for c, bank in enumerate((F[1], F[2], F[0])):
                                ops = [(a, w, k) for k in range(KC) for a, w in
                                       ((hT_hi, wq_hi), (hT_lo, wq_hi), (hT_hi, wq_lo))]
                                for z, (a, w, k) in enumerate(ops):
                                    mm = pe.matmul(bank[:, :], a[:, u, k, :], w[:, k, c * W:(c + 1) * W],
                                                   start=(z == 0), stop=(z == len(ops) - 1))
                                mm.then_inc(qkv_done, 1)
                            for z, bank in enumerate((F[1], F[2], F[0], F[1])):
                                s, hf = z // 2, z % 2
                                if z == 0:
                                    pe.wait_ge(qr_ok, t + 1)
                                    pe.wait_ge(sq_ok, 2 * t + 2)
                                if z == 2:
                                    pe.wait_ge(kr_ok, t + 1)
                                    pe.wait_ge(vlo_ok, t + 1)
                                if z == 3:
                                    pe.wait_ge(st_lo_ok, 4 * t + 1)
                                for h in range(HH):
                                    tr = pe.transpose(bank[:, h * P:(h + 1) * P],
                                                      qd[:, s, hf * HH + h, :, :].rearrange("p a d -> p (a d)"), ident[:, :])
                                tr.then_inc(qkT_done, 1)
                            for hf in range(2):
                                pe.wait_ge(st_lo_ok, 4 * t + 3 + hf)
                                if hf:
                                    pe.wait_ge(exp_ok, H * t + HH)
                                for h in range(HH):
                                    hh = hf * HH + h
                                    for z, kk in enumerate((k_hi, k_lo)):
                                        pe.matmul(S[:, h, :], q_st[:, hh, :], kk[:, hh].rearrange("p a n -> p (a n)"),
                                                  start=(z == 0), stop=False)
                                    mk = mask_b[:, bass.ds(i, 1)] if u == 0 else mask_b[:, PAIRS:PAIRS + 1]
                                    mm = pe.matmul(S[:, h, :], ident_b[:, :], mk.rearrange("p o a n -> p (o a n)"),
                                                   start=False, stop=True)
                                mm.then_inc(s_done, 1)
                                pe.wait_ge(exp_ok, H * t + HH * (hf + 1))
                                if hf:
                                    pe.wait_ge(pT_lo_ok, 4 * t + 2)
                                for c in range(2):
                                    for z in range(4):
                                        h, s = 2 * c + z // 2, z % 2
                                        tr = pe.transpose(T[:, c, z * P:(z + 1) * P], prob[:, hf * HH + h, s, :], ident[:, :])
                                    tr.then_inc(pT_done, 1)
                                pe.wait_ge(pT_lo_ok, 4 * t + 2 * hf + 2)
                                for h in range(HH):
                                    hh = hf * HH + h
                                    ops = [(a, v, s) for s in range(2) for a, v in
                                           ((pT_hi, v_hi), (pT_hi, v_lo), (pT_lo, v_hi))]
                                    for z, (a, v, s) in enumerate(ops):
                                        mm = pe.matmul(O[:, hh * D:(hh + 1) * D], a[:, hf, h, s, :], v[:, s, hh, :],
                                                       start=(z == 0), stop=(z == len(ops) - 1))
                                mm.then_inc(pv_done, 1)
                            pe.wait_ge(osb_ok, t + 1)
                            for k in range(OC):
                                tr = pe.transpose(T[:, 0, k * P:(k + 1) * P],
                                                  osb[:, 2 * k:2 * k + 2, :].rearrange("p a d -> p (a d)"), ident[:, :])
                            tr.then_inc(oT_done, 1)
                            pe.wait_ge(oT_lo_ok, t + 1)
                            ops = [(a, w, k) for k in range(OC) for a, w in
                                   ((oT_hi, wo_hi), (oT_lo, wo_hi), (oT_hi, wo_lo))]
                            for z, (a, w, k) in enumerate(ops):
                                mm = pe.matmul(O[:, 0:E], a[:, k, :], w[:, k, :], start=(z == 0), stop=(z == len(ops) - 1))
                            mm.then_inc(wo_done, 1)
                            pe.wait_ge(y_ok, t + 2)
                meet(pe, 2 * l + 1)
                with pe.Fori(0, B) as b:
                    with pe.Fori(0, NG) as g:
                        m = (l * B + b) * NG + g
                        pe.wait_ge(z_ok, m + 1)
                        for k in range(KC):
                            for t in range(GT):
                                tr = pe.transpose(ZT[k][:, t * P:(t + 1) * P], mz[:, t, k * P:(k + 1) * P], ident[:, :])
                            tr.then_inc(zT_done, 1)
                        pe.wait_ge(zlo_ok, m + 1)
                        for f in range(FT):
                            r = FR[f]
                            if f >= 2:
                                pe.wait_ge(hid_ok, m * FT + f - 1)
                            for dst, off in ((A[f % 2], 0), (G[f % 2], HID)):
                                ops = [(w, a, k) for k in range(KC) for w, a in
                                       ((w1_hi, zT_hi), (w1_lo, zT_hi), (w1_hi, zT_lo))]
                                for z, (w, a, k) in enumerate(ops):
                                    mm = pe.matmul(dst[0:r, :], w[:, k, off + f * P:off + f * P + r], a[:, k, :],
                                                   start=(z == 0), stop=(z == len(ops) - 1))
                            mm.then_inc(ag_done, 1)
                        pe.wait_ge(hlo_ok, (m + 1) * FT)
                        for t in range(GT):
                            o = Y[t // 2][:, (t % 2) * E:(t % 2 + 1) * E]
                            ops = [(a, w, f) for f in range(FT) for a, w in
                                   ((hid_hi, w2_hi), (hid_lo, w2_hi), (hid_hi, w2_lo))]
                            for z, (a, w, f) in enumerate(ops):
                                mm = pe.matmul(o, a[0:FR[f], f, t * P:(t + 1) * P], w[0:FR[f], f, :],
                                               start=(z == 0), stop=(z == len(ops) - 1))
                            mm.then_inc(w2_done, 1)
                        pe.wait_ge(my_ok, (m + 1) * GT)
                meet(pe, 2 * l + 2)
                

        @block.scalar
        def _(act):
            with act.Fori(0, LAYERS) as l:
                with act.Fori(0, B) as b:
                    with act.Fori(0, PAIRS) as i:
                        m = (l * B + b) * PAIRS + i
                        for u in range(2):
                            t = 2 * m + u
                            act.wait_ge(hT_done, t + 1)
                            act.activation(hT_hi[:, u].rearrange("p k n -> p (k n)"), F[0][:, 0:2 * P],
                                           ACT.Copy).then_inc(hT_hi_ok, 1)
                            for s in range(2):
                                act.wait_ge(qkv_done, 3 * t + s + 1)
                                act.activation(qk[:, s, :], F[1 + s][:, :], ACT.Copy).then_inc(qk_ok, 1)
                                act.activation(sq[:, s * H:(s + 1) * H, :].rearrange("p h d -> p (h d)"), F[1 + s][:, :],
                                               ACT.Square).then_inc(sq_ok, 1)
                            act.wait_ge(qkv_done, 3 * t + 3)
                            act.activation(v_hi[:, u].rearrange("p h d -> p (h d)"), F[0][:, :],
                                           ACT.Copy).then_inc(vhi_ok, 1)
                            for z, bank in enumerate((F[1], F[2], F[0], F[1])):
                                s, hf = z // 2, z % 2
                                act.wait_ge(qkT_done, 4 * t + z + 1)
                                src = bank[:, :].rearrange("p (h n) -> p h n", h=HH)
                                hs = slice(hf * HH, (hf + 1) * HH)
                                dst = q_st[:, hs, :] if s == 0 else k_hi[:, hs, u, :]
                                act.activation(dst, src, ACT.Copy).then_inc(st_hi_ok, 1)
                            for hf in range(2):
                                for h in range(HH):
                                    hh = hf * HH + h
                                    if h == 0:
                                        act.wait_ge(mx_ok, 2 * t + hf + 1)
                                    act.activation(prob[:, hh].rearrange("p a n -> p (a n)"), S[:, h, :], ACT.Exp,
                                                   bias=mx[:, 1, hh:hh + 1], scale=rn[:, u, hh:hh + 1],
                                                   accum_out=mx[:, 2, hh:hh + 1]).then_inc(exp_ok, 1)
                                for c in range(2):
                                    act.wait_ge(pT_done, 4 * t + 2 * hf + c + 1)
                                    act.activation(pT_hi[:, hf, 2 * c:2 * c + 2].rearrange("p h s n -> p (h s n)"),
                                                   T[:, c, :], ACT.Copy).then_inc(pT_hi_ok, 1)
                            act.wait_ge(oT_done, t + 1)
                            act.activation(oT_hi[:, :, :].rearrange("p k n -> p (k n)"), T[:, 0, :],
                                           ACT.Copy).then_inc(oT_hi_ok, 1)
                meet(act, 2 * l + 1)
                with act.Fori(0, B) as b:
                    with act.Fori(0, NG) as g:
                        m = (l * B + b) * NG + g
                        act.wait_ge(zT_ok, m * 2 + 2)
                        act.activation(zT_hi[:, :, :], zT[:, :, :], ACT.Copy).then_inc(zhi_ok, 1)
                        for f in range(FT):
                            r = FR[f]
                            act.wait_ge(ag_done, m * FT + f + 1)
                            act.activation(gel[0:r, f % 2, :], G[f % 2][0:r, :], ACT.Gelu,
                                           bias=b1_col[0:r, 1, f:f + 1]).then_inc(gel_ok, 1)
                            act.wait_ge(hid_ok, m * FT + f + 1)
                            act.activation(hid_hi[0:r, f, :], hid[0:r, f % 2, :], ACT.Copy).then_inc(hhi_ok, 1)
                        act.wait_ge(w2_done, (m + 1) * GT)
                meet(act, 2 * l + 2)
                

        @block.vector
        def _(dve):
            dve.wait_ge(d_c[0], 16)
            dve.tensor_copy(ident_b[:, :], ident[:, :]).then_inc(const_ok, 1)
            dve.wait_ge(d_c[1], 16)
            dve.tensor_copy(mask_b[:, :, :, :], mask_f[:, :, :, :]).then_inc(const_ok, 1)
            dve.wait_ge(d_c[2], 16)
            dve.nop().then_inc(y_ok, 1)
            with dve.Fori(0, LAYERS) as l:
                SPLITS = 2 * (3 * KC + 2)
                for n in range(4):
                    dve.wait_ge(d_c[3 + n], 16 * (l + 1))
                dve.tensor_tensor(tab[:, :, :, :].rearrange("p t z d -> p t (z d)"),
                                  rot_sb[:, :, :, :].rearrange("p t z d -> p t (z d)"),
                                  rsc[:, :, :].rearrange("p z d -> p (z d)").unsqueeze(1).broadcast_to(
                                      [P, 2 * PAIRS, 4 * D]), ALU.mult)
                HW = 3 * W // 2
                dsts = ([(wq_hi[:, k, a * HW:(a + 1) * HW], wq_lo[:, k, a * HW:(a + 1) * HW])
                         for k in range(KC) for a in range(2)]
                        + [(w1_hi[:, k, :], w1_lo[:, k, :]) for k in range(KC)]
                        + [(wo_hi[:, :, :].rearrange("p a b -> p (a b)"), wo_lo[:, :, :].rearrange("p a b -> p (a b)")),
                           (w2_hi[:, :, :].rearrange("p a b -> p (a b)"), w2_lo[:, :, :].rearrange("p a b -> p (a b)"))])
                for n, (hi, lo) in enumerate(dsts):
                    dve.wait_ge(d_c[7], 16 * (l * len(dsts) + n + 1))
                    w = hi.shape[1]
                    dve.tensor_copy(hi, stage[:, 0:w]).then_inc(split, 1)
                    dve.wait_ge(split, l * SPLITS + 2 * n + 1)
                    dve.tensor_tensor(lo, stage[:, 0:w], hi.bitcast(F32), ALU.subtract).then_inc(split, 1)
                wait_alone(dve, split, (l + 1) * SPLITS, spare)
                with dve.Fori(0, B) as b:
                    with dve.Fori(0, PAIRS) as i:
                        m = (l * B + b) * PAIRS + i
                        for u in range(2):
                            t = 2 * m + u
                            tile = bass.ds(2 * i + u, 1)
                            count = [0]
                            LINKS = 5

                            def chain(ins):
                                count[0] += 1
                                ins.then_inc(vch, 1)
                                dve.wait_ge(vch, LINKS * t + count[0])
                            dve.wait_ge(hT_hi_ok, t + 1)
                            dve.tensor_tensor(hT_lo[:, u].rearrange("p k n -> p (k n)"), F[0][:, 0:2 * P],
                                              hT_hi[:, u].rearrange("p k n -> p (k n)").bitcast(F32),
                                              ALU.subtract).then_inc(hT_lo_ok, 1)
                            dve.wait_ge(sq_ok, 2 * t + 2)
                            chain(dve.tensor_reduce(ss[:, 0, :], sq[:, :, :], AX.X, ALU.add))
                            dve.tensor_scalar(ss[:, 1, :], ss[:, 0, :], 1e-24, None, ALU.max).then_inc(ss_ok, 1)
                            dve.wait_ge(vhi_ok, t + 1)
                            dve.tensor_tensor(v_lo[:, u].rearrange("p h d -> p (h d)"), F[0][:, :],
                                              v_hi[:, u].rearrange("p h d -> p (h d)").bitcast(F32),
                                              ALU.subtract).then_inc(vlo_ok, 1)
                            q3 = qk[:, 0, :].rearrange("p (h d) -> p h d", h=H)

                            def row(z, a, c):
                                return tab[:, tile, z, a:c].broadcast_to([P, H, c - a])
                            dve.tensor_tensor(ta[:, 0], q3, row(0, 0, D), ALU.mult)
                            dve.tensor_tensor(tb[:, 0, :, 0:D // 2], q3[:, :, D // 2:D], row(1, 0, D // 2), ALU.mult)
                            chain(dve.tensor_tensor(tb[:, 0, :, D // 2:D], q3[:, :, 0:D // 2], row(1, D // 2, D), ALU.mult))
                            chain(dve.tensor_tensor(qd[:, 0, :, 0, :], ta[:, 0], tb[:, 0], ALU.add))
                            dve.tensor_copy(qd[:, 0, :, 1, :], qd[:, 0, :, 0, :]).then_inc(qr_ok, 1)
                            for z, bank in enumerate((F[1], F[2], F[0], F[1])):
                                s, hf = z // 2, z % 2
                                dve.wait_ge(st_hi_ok, 4 * t + z + 1)
                                src = bank[:, :].rearrange("p (h n) -> p h n", h=HH)
                                hs = slice(hf * HH, (hf + 1) * HH)
                                if s == 0:
                                    dve.tensor_tensor(q_st[D:P, hs, :], src[D:P], q_st[D:P, hs, :].bitcast(F32),
                                                      ALU.subtract).then_inc(st_lo_ok, 1)
                                else:
                                    dve.tensor_tensor(k_lo[:, hs, u, :], src, k_hi[:, hs, u, :].bitcast(F32),
                                                      ALU.subtract).then_inc(st_lo_ok, 1)
                            dve.wait_ge(rn_ok, t + 1)
                            for hf in range(2):
                                hs = slice(hf * HH, (hf + 1) * HH)
                                dve.wait_ge(s_done, 2 * t + hf + 1)
                                chain(dve.tensor_reduce(mx[:, 0, hs], S[:, :, :], AX.X, ALU.max, negate=True))
                                dve.tensor_tensor(mx[:, 1, hs], mx[:, 0, hs], rn[:, u, hs], ALU.mult).then_inc(mx_ok, 1)
                                dve.wait_ge(exp_ok, H * t + HH * (hf + 1))
                                dve.reciprocal(mx[:, 3, hs], mx[:, 2, hs]).then_inc(ri_ok, 1)
                                for c in range(2):
                                    dve.wait_ge(pT_hi_ok, 4 * t + 2 * hf + c + 1)
                                    dve.tensor_tensor(pT_lo[:, hf, 2 * c:2 * c + 2].rearrange("p h s n -> p (h s n)"),
                                                      T[:, c, :],
                                                      pT_hi[:, hf, 2 * c:2 * c + 2].rearrange("p h s n -> p (h s n)").bitcast(F32),
                                                      ALU.subtract).then_inc(pT_lo_ok, 1)
                            dve.wait_ge(pv_done, 2 * t + 2)
                            dve.wait_ge(ri_ok, 2 * t + 2)
                            dve.tensor_tensor(osb[:, :, :], O[:, :].rearrange("p (h d) -> p h d", h=H),
                                              mx[:, 3, :].unsqueeze(2).broadcast_to([P, H, D]), ALU.mult).then_inc(osb_ok, 1)
                            dve.wait_ge(oT_hi_ok, t + 1)
                            dve.tensor_tensor(oT_lo[:, :, :].rearrange("p k n -> p (k n)"), T[:, 0, :],
                                              oT_hi[:, :, :].rearrange("p k n -> p (k n)").bitcast(F32),
                                              ALU.subtract).then_inc(oT_lo_ok, 1)
                            dve.wait_ge(wo_done, t + 1)
                            dve.wait_ge(d_x[u], 16 * (m + 1))
                            dve.tensor_tensor(yb[:, u, :], O[:, 0:E], xt[:, u, :], ALU.add).then_inc(y_ok, 1)
                            assert count[0] == LINKS
                meet(dve, 2 * l + 1)
                with dve.Fori(0, B) as b:
                    with dve.Fori(0, NG) as g:
                        m = (l * B + b) * NG + g
                        dve.wait_ge(d_mx, 16 * (m + 1))
                        dve.wait_ge(d_mh, 16 * (m + 1))
                        for t in range(GT):
                            dve.bn_stats(mbn[:, t, 0, :], mxt[:, t, 0:P])
                            st = dve.bn_stats(mbn[:, t, 1, :], mh2[:, t, :])
                        st.then_inc(bn_ok, 1)
                        wait_alone(dve, bn_ok, 2 * m + 1, spare)
                        for t in range(GT):
                            st = dve.bn_aggr(mmv[:, t, :], mbn[:, t].rearrange("p a s -> p (a s)"))
                        st.then_inc(bn_ok, 1)
                        dve.wait_ge(bn_ok, 2 * m + 2)
                        dve.tensor_scalar(mrs[:, 0, :], mmv[:, :, 1], EPS, None, ALU.add).then_inc(ve_ok, 1)
                        dve.wait_ge(rs_ok, m + 1)
                        for t in range(GT):
                            dve.tensor_scalar(mz[:, t, 0:P], mxt[:, t, 0:P], mmv[:, t, 0:1], mrs[:, 1, t:t + 1],
                                              ALU.subtract, ALU.mult)
                            st = dve.tensor_scalar(mz[:, t, P:E], mh2[:, t, :], mmv[:, t, 0:1], mrs[:, 1, t:t + 1],
                                                   ALU.subtract, ALU.mult)
                        st.then_inc(z_ok, 1)
                        for k in range(KC):
                            dve.wait_ge(zT_done, 2 * m + k + 1)
                            dve.tensor_scalar(zT[:, k, :], ZT[k], gb_col[:, 0, k:k + 1], gb_col[:, 1, k:k + 1],
                                              ALU.mult, ALU.add).then_inc(zT_ok, 1)
                        dve.wait_ge(zhi_ok, m + 1)
                        dve.wait_ge(zT_ok, 2 * m + 2)
                        dve.tensor_tensor(zT_lo[:, :, :], zT[:, :, :], zT_hi[:, :, :].bitcast(F32),
                                          ALU.subtract).then_inc(zlo_ok, 1)
                        for f in range(FT):
                            r = FR[f]
                            dve.wait_ge(gel_ok, m * FT + f + 1)
                            if f >= 2:
                                dve.wait_ge(hlo_ok, m * FT + f - 1)
                            dve.scalar_tensor_tensor(hid[0:r, f % 2, :], A[f % 2][0:r, :], b1_col[0:r, 0, f:f + 1],
                                                     gel[0:r, f % 2, :], ALU.add, ALU.mult).then_inc(hid_ok, 1)
                        dve.wait_ge(xb_ok, m + 1)
                        for t in range(GT):
                            dve.wait_ge(w2_done, m * GT + (t | 1) + 1)
                            dve.tensor_tensor(my[:, t, :], Y[t // 2][:, (t % 2) * E:(t % 2 + 1) * E], mxt[:, t, :],
                                              ALU.add).then_inc(my_ok, 1)
                meet(dve, 2 * l + 2)
                
            with dve.Fori(0, B) as b:
                with dve.Fori(0, NG) as g:
                    m = b * NG + g
                    dve.wait_ge(d_fx, 16 * (m + 1))
                    dve.wait_ge(d_fy, 16 * (m + 1))
                    dve.tensor_tensor(mz[:, :, :], mz[:, :, :], mxt[:, :, :], ALU.add).then_inc(f_add, 1)
                    dve.wait_ge(f_add, m + 1)
                    for t in range(GT):
                        st = dve.bn_stats(mbn[:, t, 0, :], mz[:, t, :])
                    st.then_inc(f_bn, 1)
                    wait_alone(dve, f_bn, 2 * m + 1, spare)
                    for t in range(GT):
                        st = dve.bn_aggr(mmv[:, t, :], mbn[:, t, 0, :])
                    st.then_inc(f_bn, 1)
                    dve.wait_ge(f_bn, 2 * m + 2)
                    dve.tensor_scalar(mrs[:, 0, :], mmv[:, :, 1], EPS, None, ALU.add).then_inc(f_ag, 1)
                    dve.wait_ge(f_rs, m + 1)
                    for t in range(GT):
                        dve.tensor_scalar(my[:, t, :], mz[:, t, :], mmv[:, t, 0:1], mrs[:, 1, t:t + 1],
                                          ALU.subtract, ALU.mult).then_inc(f_ok, 1)


def build(nc, h, out):
    B, L, E = h["x"].shape
    xs = nc.dram_tensor("states", (3, B, L + 1, E), F32, kind="Internal").ap()
    causal_attention(nc, h["x"], h["w_qkv"], h["w_out"], h["ln_g"], h["ln_b"], h["b_out"], h["ident"], h["mask"], xs)
    local_layers(nc, xs, out, h["rot"], h["rot_scale"], h["lw_qkv"], h["lw_out"], h["ident"], h["lmask"],
                 h["ln_gb"], h["w1"], h["b1"], h["w2"], h["b2"])


def layout(v):
    import numpy as np

    p, groups, hg, d = 128, 4, 4, 16
    out = {"x": v["L0_attn_x"]}
    w = np.stack([v["L0_attn_Wq"].T, v["L0_attn_Wk"].T, v["L0_attn_Wv"].T], 1).reshape(2, p, 3, groups, hg * d)
    out["w_qkv"] = np.ascontiguousarray(w.transpose(1, 0, 3, 2, 4)).reshape(p, 2, 3, 256)
    wo = v["L0_attn_Wo"].T.reshape(groups, hg, 1, d, 256)
    wo = np.broadcast_to(wo, (groups, hg, 2, d, 256)).reshape(groups, p, 256)
    out["w_out"] = np.ascontiguousarray(wo.transpose(1, 0, 2))
    for name, a, b in (("ln_g", "gq", "gk"), ("ln_b", "bq", "bk")):
        r = np.stack([v["L0_attn_" + a], v["L0_attn_" + b]])[None, :, None, :]
        out[name] = np.ascontiguousarray(np.broadcast_to(r, (p, 2, hg, d)))
    out["b_out"] = np.ascontiguousarray(np.broadcast_to(v["L0_attn_bo"][None], (p, 256)))
    out["ident"] = np.eye(p, dtype=np.float32)
    i = np.arange(p)
    out["mask"] = np.where(i[:, None] >= i[None, :], 0.0, -1e30).astype(np.float32)
    return out


def layout_local(v):
    import numpy as np

    p, seq, window, dh, layers = 128, 1024, 128, 64, 2
    f = np.float32
    out = {}
    half_idx = np.arange(0, dh, 2, dtype=f)
    inv_freq = f(1.0) / f(10000.0) ** (half_idx / f(dh))
    t = np.arange(seq, dtype=f)
    freqs = t[:, None] * inv_freq[None, :]
    freqs = np.concatenate([freqs, freqs], -1)
    base = (half_idx + f(0.4 * dh)) / f(1.4 * dh)
    scale = base[None, :] ** ((t - seq // 2) / f(window // 2))[:, None]
    scale = np.concatenate([scale, scale], -1)
    sign = np.where(np.arange(dh) < dh // 2, -1, 1).astype(f)
    cos, sin = np.cos(freqs), np.sin(freqs) * sign
    rot = np.stack([cos * scale * f(8), sin * scale * f(8), cos / scale, sin / scale], 1).astype(f)
    out["rot"] = np.ascontiguousarray(rot.reshape(seq // p, p, 4, dh).transpose(1, 0, 2, 3))
    qs, ks = v["L0_ffn_q_scale"], v["L0_ffn_k_scale"]
    rows = np.stack([qs, np.roll(qs, dh // 2, -1), ks, np.roll(ks, dh // 2, -1)], 1)
    out["rot_scale"] = np.ascontiguousarray(np.broadcast_to(rows[:, None], (layers, p, 4, dh)))
    out["lw_qkv"] = np.ascontiguousarray(v["L0_ffn_wqkv"].reshape(layers, 2, p, -1).transpose(0, 2, 1, 3))
    out["lw_out"] = np.ascontiguousarray(v["L0_ffn_wo"].reshape(layers, 4, p, -1).transpose(0, 2, 1, 3))
    i = np.arange(p)
    own = np.where(i[:, None] >= i[None, :], 0.0, -1e30)
    prev = np.where(i[:, None] <= i[None, :], 0.0, -1e30)
    none = np.full((p, p), -1e30)
    masks = [np.stack([own, none], 1)] + [np.stack([own, prev], 1)] * 3 + [np.stack([prev, own], 1)]
    out["lmask"] = np.ascontiguousarray(np.stack(masks, 1).astype(f))
    hid = v["L0_ffn_w2"].shape[1]
    ft = -(-hid // p)
    gb = np.stack([v["L0_ffn_ln_g"], v["L0_ffn_ln_b"]], 1).reshape(layers, 2, 2, p)
    out["ln_gb"] = np.ascontiguousarray(gb.transpose(0, 3, 1, 2))
    out["w1"] = np.ascontiguousarray(v["L0_ffn_w1"].reshape(layers, 2, p, -1).transpose(0, 2, 1, 3))
    b1 = np.zeros((layers, 2, ft * p), f)
    b1[:, :, :hid] = v["L0_ffn_b1"].reshape(layers, 2, hid)
    out["b1"] = np.ascontiguousarray(b1.reshape(layers, 2, ft, p).transpose(0, 3, 1, 2))
    w2 = np.zeros((layers, ft * p, 256), f)
    w2[:, :hid] = v["L0_ffn_w2"]
    out["w2"] = np.ascontiguousarray(w2.reshape(layers, ft, p, 256).transpose(0, 2, 1, 3))
    out["b2"] = np.ascontiguousarray(np.broadcast_to(v["L0_ffn_b2"][:, None], (layers, p, 256)))
    return out


def kernel(**inputs):
    import numpy as np
    import concourse.bacc as bacc
    from concourse.bass_utils import run_bass_kernel_spmd

    v = {k: np.asarray(a) for k, a in inputs.items()}
    a = {**layout(v), **layout_local(v)}
    nc = bacc.Bacc("TRN2", target_bir_lowering=False, num_devices=1)
    h = {k: nc.dram_tensor(k, t.shape, F32, kind="ExternalInput").ap() for k, t in a.items()}
    B, L, E = a["x"].shape
    out = nc.dram_tensor("out", (B, L, E), F32, kind="ExternalOutput").ap()
    build(nc, h, out)
    r = run_bass_kernel_spmd(nc, [a], core_ids=[0])
    return r.results[0]["out"]
```

```python
from contextlib import ExitStack

import concourse.bass as bass
from concourse import mybir

F32 = mybir.dt.float32
F32R = mybir.dt.float32r
BF16 = mybir.dt.bfloat16
ALU = mybir.AluOpType
ACT = mybir.ActivationFunctionType
AX = mybir.AxisListType

P = 128
BANK = 512
EPS = 1e-5
LEAD = P


def wait_alone(eng, sem, value, spare):
    eng.wait_ge(sem, value)
    eng.sem_inc(spare, 1)


def causal_attention(nc, x, w_qkv, w_out, ln_g, ln_b, b_out, ident_in, mask_in, x_mid):
    B, L, E = x.shape
    TILES = L // P
    KC = E // P
    D = 16
    GROUPS = 4
    HG = 4
    GW = 3 * HG * D
    QW = HG * D
    CH = BANK // P
    CHUNKS = TILES // CH
    UNITS = CHUNKS * HG * CH
    BLOCKS = CHUNKS * HG
    TCH = sum(-(-(i + 1) // CH) for i in range(TILES)) * HG
    NT = 3
    assert TCH % NT == 0

    with ExitStack() as ctx:
        def sb(name, shape, dt):
            return ctx.enter_context(nc.sbuf_tensor(name, shape, dt))

        def ps(name, shape, dt=F32):
            return ctx.enter_context(nc.psum_tensor(name, shape, dt))

        def sem(name):
            return ctx.enter_context(nc.semaphore(name))

        ident = sb("a_ident", [P, P], F32)
        ident_b = sb("a_ident_b", [P, P], BF16)
        mask_f = sb("a_mask_f", [P, P], F32)
        mask_b = sb("a_mask_b", [P, P], BF16)
        g_row = sb("a_g_row", [P, 2, HG, D], F32)
        b_row = sb("a_b_row", [P, 2, HG, D], F32)
        bo_row = sb("a_bo_row", [P, E], F32)
        w_hi = sb("a_w_hi", [P, KC, GROUPS, GW], F32R)
        w_lo = sb("a_w_lo", [P, KC, GROUPS, GW], F32R)
        wo_hi = sb("a_wo_hi", [P, GROUPS, E], F32R)
        wo_lo = sb("a_wo_lo", [P, GROUPS, E], F32R)
        xb = sb("a_xb", [P, TILES, E], F32)
        xT_hi = sb("a_xT_hi", [P, KC, L], F32R)
        xT_lo = sb("a_xT_lo", [P, KC, L], F32R)
        qk = sb("a_qk", [P, 2, TILES * HG, D], F32)
        qkc = sb("a_qkc", [P, 2, TILES * HG, D], F32)
        qk_sq = sb("a_qk_sq", [P, 2, TILES * HG, D], F32)
        st = sb("a_st", [P, 5, 2 * TILES * HG], F32)
        qT = sb("a_qT", [P, 2, L], F32R)
        kT = sb("a_kT", [P, 2, L], F32R)
        v_st = sb("a_v_st", [P, TILES, HG * (P + 2 * D)], F32R)
        oT_hi = sb("a_oT_hi", [P, GROUPS, L], F32R)
        oT_lo = sb("a_oT_lo", [P, GROUPS, L], F32R)
        NP = 2
        prob = sb("a_prob", [P, NP, L], F32)
        pT_hi = sb("a_pT_hi", [P, 2, TILES, BANK], F32R)
        pT_lo = sb("a_pT_lo", [P, TILES, BANK], F32R)
        parts = pT_hi[:, 0, :, :].rearrange("p (s t) n -> p s (t n)", s=2).rearrange(
            "p s (m r d) -> p s m r d", r=4, d=D)
        parts_f = parts.bitcast(F32)
        stats = sb("a_stats", [P, 3, UNITS], F32)
        bn = sb("a_bn", [P, TILES, 6], F32)
        mv = sb("a_mv", [P, TILES, 2], F32)
        rstd = sb("a_rstd", [P, 3, TILES], F32)
        zrow = sb("a_zrow", [P, E], F32)
        stage = xb

        S = [ps(f"a_S{i}", [P, 2 * BANK]) for i in range(2)]
        T = [ps(f"a_T{i}", [P, BANK]) for i in range(NT)]
        O = ps("a_O", [P, BANK])
        pX = [S[0][:, 0:BANK], S[0][:, BANK:2 * BANK], S[1][:, 0:BANK], S[1][:, BANK:2 * BANK]]
        pR = [T[0], T[1], T[2], O]

        d_const = [sem(f"a_d_const{i}") for i in range(9)]
        d_x = sem("a_d_x")
        d_y = sem("a_d_y")
        d_z = [sem(f"a_d_z{s}") for s in range(3)]
        w_ready = sem("a_w_ready")
        zero_ready = sem("a_zero_ready")
        xT_done = sem("a_xT_done")
        xT_hi_done = sem("a_xT_hi_done")
        xT_lo_done = sem("a_xT_lo_done")
        qkv_done = sem("a_qkv_done")
        qk_ready = sem("a_qk_ready")
        v_hi_done = sem("a_v_hi_done")
        v_lo_done = sem("a_v_lo_done")
        cen_done = sem("a_cen_done")
        sq_done = sem("a_sq_done")
        gain_done = sem("a_gain_done")
        var_done = sem("a_var_done")
        sd_done = sem("a_sd_done")
        norm_done = sem("a_norm_done")
        part_hi = sem("a_part_hi")
        part_lo = sem("a_part_lo")
        pt_done = sem("a_pt_done")
        pt_act = sem("a_pt_act")
        pt_dve = sem("a_pt_dve")
        s_done = sem("a_s_done")
        max_done = sem("a_max_done")
        exp_done = sem("a_exp_done")
        rec_done = sem("a_rec_done")
        prob_ok = sem("a_prob_ok")
        t_done = sem("a_t_done")
        thi_done = sem("a_thi_done")
        tlo_done = sem("a_tlo_done")
        pv_done = sem("a_pv_done")
        ohi_done = sem("a_ohi_done")
        olo_done = sem("a_olo_done")
        wo_done = sem("a_wo_done")
        res_done = sem("a_res_done")
        veps_done = sem("a_veps_done")
        ysd_done = sem("a_ysd_done")
        bns_done = sem("a_bns_done")
        agg_done = sem("a_agg_done")
        yr_done = sem("a_yr_done")
        y_done = sem("a_y_done")
        xb_bias = sem("a_xb_bias")
        link = sem("a_link")
        glink = sem("a_glink")
        spare = sem("a_spare")

        def v_at(tile, off):
            return v_st[:, tile, :].rearrange("p (h n) -> p h n", h=HG)[:, :, off:off + D]

        unit = [(c, j, ii) for c in range(CHUNKS) for j in range(HG) for ii in range(CH)]
        tch = [(q, m, min(c * CH + ii + 1, m + CH)) for q, (c, j, ii) in enumerate(unit)
               for m in range(0, c * CH + ii + 1, CH)]
        first_tch = [min(n for n, t in enumerate(tch) if t[0] == q) for q in range(UNITS)] + [len(tch)]
        assert len(tch) == TCH

        block = ctx.enter_context(nc.Block())

        @block.sync
        def _(sp):
            for n, (dst, src) in enumerate([
                    (ident[:, :], ident_in), (mask_f[:, :], mask_in),
                    (g_row[:, :, :, :], ln_g), (b_row[:, :, :, :], ln_b), (bo_row[:, :], b_out)]):
                sp.dma_start(dst, src).then_inc(d_const[n], 16)
            for k in range(KC):
                sp.dma_start(stage[:, 4 * k:4 * k + 3, :], w_qkv[:, k]).then_inc(d_const[5 + k], 16)
            sp.wait_ge(w_ready, 2 * KC)
            sp.dma_start(stage[:, 0:GROUPS, :], w_out).then_inc(d_const[7], 16)
            sp.wait_ge(zero_ready, 1)
            for s in range(3):
                end = LEAD + B * (L + 1)
                sp.dma_start(x_mid[s, LEAD:end, :].rearrange("(b r) e -> b r e", b=B)[:, 0, :],
                             zrow[0:B, :]).then_inc(d_z[s], 16)
                sp.dma_start(x_mid[s, end:end + P, :], zrow[:, :]).then_inc(d_z[s], 16)
                sp.dma_start(x_mid[s, end + P:end + P + 1, :], zrow[0:1, :]).then_inc(d_z[s], 16)
            sp.wait_ge(w_ready, 2 * KC + 2)
            with sp.Fori(0, B) as b:
                sp.wait_ge(y_done, b * TILES + 1)
                sp.dma_start(xb[:, :, :], x[b].rearrange("(t p) e -> p t e", p=P)).then_inc(d_x, 16)
                sp.wait_ge(y_done, b * TILES + TILES + 1)
                sp.dma_start(x_mid[0, bass.ds(LEAD + b * (L + 1) + 1, L), :].rearrange("(t p) e -> p t e", p=P),
                             xb[:, :, :]).then_inc(d_y, 16)
                wait_alone(sp, d_y, b * 16 + 16, spare)
            for s in range(3):
                sp.wait_ge(d_z[s], 3 * 16)

        @block.gpsimd
        def _(pool):
            pool.memset(v_st[:, :, :].bitcast(F32), 0.0).then_inc(glink, 1)
            pool.memset(zrow[:, :], 0.0).then_inc(zero_ready, 1)
            pool.wait_ge(glink, 1)
            with pool.Fori(0, B) as b:
                pool.wait_ge(xT_done, b * (TILES // 2) + TILES // 2)
                pool.tensor_tensor(xb[:, :, :], xb[:, :, :], bo_row[:, :].unsqueeze(1).broadcast_to([P, TILES, E]),
                                   ALU.add).then_inc(xb_bias, 1)
                with pool.Fori(0, GROUPS) as g:
                    n = b * GROUPS + g
                    pool.wait_ge(cen_done, n + 1)
                    for s in range(2):
                        pool.tensor_tensor(
                            qk[:, s].rearrange("p (t h) d -> p t (h d)", h=HG),
                            qkc[:, s].rearrange("p (t h) d -> p t (h d)", h=HG),
                            g_row[:, s].rearrange("p h d -> p (h d)").unsqueeze(1).broadcast_to([P, TILES, QW]),
                            ALU.mult).then_inc(gain_done, 1)
                    for q in range(UNITS):
                        c, j, ii = unit[q]
                        w = (c * CH + ii + 1) * P
                        pool.wait_ge(rec_done, n * UNITS + q + 1)
                        pool.tensor_tensor(prob[:, q % NP, 0:w], prob[:, q % NP, 0:w],
                                           stats[:, 2, q:q + 1].broadcast_to([P, w]), ALU.mult).then_inc(prob_ok, 1)

        @block.tensor
        def _(pe):
            pe.wait_ge(w_ready, 2 * KC + 4)
            with pe.Fori(0, B) as b:
                pe.wait_ge(d_x, b * 16 + 16)
                for m in range(TILES // 2):
                    pe.wait_ge(res_done, b * TILES + 1)
                    for k in range(KC):
                        for i in range(2):
                            t = pe.transpose(pX[m][:, (2 * k + i) * P:(2 * k + i + 1) * P],
                                             xb[:, 2 * m + i, k * P:(k + 1) * P], ident[:, :])
                    t.then_inc(xT_done, 1)
                with pe.Fori(0, GROUPS) as g:
                    n = b * GROUPS + g
                    pe.wait_ge(xT_lo_done, b * (TILES // 2) + TILES // 2)
                    for i in range(TILES):
                        if i == 0:
                            pe.wait_ge(exp_done, n * UNITS + 1)
                        o = pX[i // 2][:, (i % 2) * GW:(i % 2 + 1) * GW]
                        passes = [(a, w, k) for k in range(KC) for a, w in
                                  ((xT_hi, w_hi), (xT_lo, w_hi), (xT_hi, w_lo))]
                        for z, (a, w, k) in enumerate(passes):
                            mm = pe.matmul(o, a[:, k, i * P:(i + 1) * P], w[:, k, bass.ds(g, 1), :],
                                           start=(z == 0), stop=(z == len(passes) - 1))
                        if i % 2:
                            mm.then_inc(qkv_done, 1)
                    pe.wait_ge(part_lo, 2 * n + 2)
                    for z in range(8):
                        s, p, c = z // 4, z // 2 % 2, z % 2
                        if z < 4:
                            if z == 0:
                                pe.wait_ge(tlo_done, n * TCH + 1)
                                pe.wait_ge(olo_done, n * CHUNKS + 1)
                        elif z % 2 == 0:
                            pe.wait_ge(pt_act, n * 4 + (z - 4) // 2 + 1)
                        else:
                            pe.wait_ge(pt_dve, n * 4 + (z - 4) // 2 + 1)
                        for ii in range(CH):
                            i = c * CH + ii
                            t = pe.transpose(
                                pR[z % 4][:, ii * P:(ii + 1) * P],
                                parts_f[:, s, i * HG + 2 * p:i * HG + 2 * p + 2].rearrange("p m r d -> p (m r d)"),
                                ident[:, :])
                        t.then_inc(pt_done, 1)

                    def scores(q):
                        c, j, ii = unit[q]
                        i, r, p = c * CH + ii, j % 2, j // 2
                        w = (i + 1) * P
                        if q == 0:
                            pe.wait_ge(pt_act, n * 4 + 4)
                            pe.wait_ge(pt_dve, n * 4 + 4)
                            pe.wait_ge(v_hi_done, n * 4 + 4)
                            pe.wait_ge(v_lo_done, n * 4 + 4)
                        if q >= 2:
                            pe.wait_ge(exp_done, n * UNITS + q)
                        out = S[q % 2]
                        for k0 in range(0, w, BANK):
                            k1 = min(w, k0 + BANK)
                            pe.matmul(out[:, k0:k1], qT[64 * r:64 * r + 64, p, i * P:(i + 1) * P],
                                      kT[64 * r:64 * r + 64, p, k0:k1], start=True, stop=(k1 < w))
                        pe.matmul(out[:, i * P:w], ident_b[:, :], mask_b[:, :], start=False, stop=True,
                                  ).then_inc(s_done, 1)

                    def turn(q):
                        pe.wait_ge(prob_ok, n * UNITS + q + 1)
                        for z in range(first_tch[q], first_tch[q + 1]):
                            _, k0, k1 = tch[z]
                            if z >= NT:
                                pe.wait_ge(tlo_done, n * TCH + z - NT + 2)
                            for kt in range(k0, k1):
                                t = pe.transpose(T[z % NT][:, (kt - k0) * P:(kt - k0 + 1) * P],
                                                 prob[:, q % NP, kt * P:(kt + 1) * P], ident[:, :])
                            t.then_inc(t_done, 1)

                    def mix(v):
                        c, j = v // HG, v % HG
                        pe.wait_ge(tlo_done, n * TCH + first_tch[CH * v + CH] + 1)
                        if j == 0 and c:
                            pe.wait_ge(olo_done, n * CHUNKS + c + 1)
                        for kt in range((c + 1) * CH):
                            off = max(0, kt - c * CH) * P
                            for a in (pT_hi[:, v % 2], pT_lo):
                                mm = pe.matmul(O[:, off:BANK], v_st[:, kt, j * P:(j + 1) * P], a[:, kt, off:BANK],
                                               start=(j == 0 and kt == 0 and a is not pT_lo),
                                               stop=(j == HG - 1 and kt == (c + 1) * CH - 1 and a is pT_lo))
                        mm.then_inc(pv_done, 1)

                    for q in range(UNITS + 3):
                        if q < UNITS:
                            scores(q)
                        if q >= 3 and (q - 3) % CH == CH - 1:
                            mix((q - 3) // CH)
                        if 2 <= q < UNITS + 2:
                            turn(q - 2)
                pe.wait_ge(olo_done, (b + 1) * GROUPS * CHUNKS + 1)
                for i in range(TILES):
                    o = pX[i // 2][:, (i % 2) * E:(i % 2 + 1) * E]
                    passes = [(a, w, k) for k in range(GROUPS) for a, w in
                              ((oT_hi, wo_hi), (oT_lo, wo_hi), (oT_hi, wo_lo))]
                    for z, (a, w, k) in enumerate(passes):
                        mm = pe.matmul(o, a[:, k, i * P:(i + 1) * P], w[:, k, :],
                                       start=(z == 0), stop=(z == len(passes) - 1))
                    mm.then_inc(wo_done, 1)

        @block.scalar
        def _(act):
            act.nop().then_inc(exp_done, 1)
            with act.Fori(0, B) as b:
                for m in range(TILES // 2):
                    act.wait_ge(xT_done, b * (TILES // 2) + m + 1)
                    act.activation(xT_hi[:, :, 2 * m * P:(2 * m + 2) * P],
                                   pX[m].rearrange("p (k n) -> p k n", k=KC), ACT.Copy).then_inc(xT_hi_done, 1)
                with act.Fori(0, GROUPS) as g:
                    n = b * GROUPS + g
                    for m in range(TILES // 2):
                        act.wait_ge(qkv_done, n * 4 + m + 1)
                        src = pX[m][:, 0:2 * GW].rearrange("p (i s h d) -> p i s h d", i=2, s=3, h=HG)
                        for s in range(2):
                            act.activation(qk[:, s, 2 * m * HG:(2 * m + 2) * HG, :].rearrange(
                                "p (i h) d -> p i (h d)", i=2), src[:, :, s].rearrange("p i h d -> p i (h d)"),
                                ACT.Copy).then_inc(qk_ready, 1)
                        for i in range(2):
                            t = act.activation(v_at(2 * m + i, 0), src[:, i, 2], ACT.Copy)
                        t.then_inc(v_hi_done, 1)
                    act.wait_ge(cen_done, n + 1)
                    act.activation(qk_sq[:, :, :, :], qkc[:, :, :, :], ACT.Square).then_inc(sq_done, 1)
                    act.wait_ge(var_done, n + 1)
                    act.activation(st[:, 2, :], st[:, 1, :], ACT.Sqrt).then_inc(sd_done, 1)
                    act.wait_ge(norm_done, n + 1)
                    act.activation(parts[:, 0, :, 0:2, :], qkc[:, 0].unsqueeze(2).broadcast_to([P, TILES * HG, 2, D]),
                                   ACT.Copy).then_inc(part_hi, 1)
                    act.activation(parts[:, 1, :, 0:4:2, :], qkc[:, 1].unsqueeze(2).broadcast_to([P, TILES * HG, 2, D]),
                                   ACT.Copy).then_inc(part_hi, 1)
                    for z in range(0, 8, 2):
                        s, p, c = z // 4, z // 2 % 2, z % 2
                        act.wait_ge(pt_done, n * 8 + z + 1)
                        act.activation((qT, kT)[s][:, p, c * BANK:(c + 1) * BANK], pR[z % 4][:, :],
                                       ACT.Copy).then_inc(pt_act, 1)

                    def expo(q):
                        c, j, ii = unit[q]
                        w = (c * CH + ii + 1) * P
                        act.wait_ge(max_done, n * UNITS + q + 1)
                        if q >= NP:
                            act.wait_ge(t_done, n * TCH + first_tch[q - NP + 1])
                        act.activation(prob[:, q % NP, 0:w], S[q % 2][:, 0:w], ACT.Exp, bias=stats[:, 0, q:q + 1],
                                       accum_out=stats[:, 1, q:q + 1]).then_inc(exp_done, 1)

                    def turned(q):
                        c, j, ii = unit[q]
                        v = q // CH
                        if v >= 2 and ii == 0:
                            act.wait_ge(pv_done, n * BLOCKS + v - 1)
                        for z in range(first_tch[q], first_tch[q + 1]):
                            _, k0, k1 = tch[z]
                            act.wait_ge(t_done, n * TCH + z + 1)
                            act.activation(pT_hi[:, v % 2, k0:k1, ii * P:(ii + 1) * P],
                                           T[z % NT][:, 0:(k1 - k0) * P].rearrange("p (k n) -> p k n", n=P),
                                           ACT.Copy).then_inc(thi_done, 1)

                    def taken(c):
                        act.wait_ge(pv_done, n * BLOCKS + (c + 1) * HG)
                        act.activation(oT_hi[:, bass.ds(g, 1), c * BANK:(c + 1) * BANK], O[:, :],
                                       ACT.Copy).then_inc(ohi_done, 1)

                    for q in range(UNITS + 4):
                        if q < UNITS:
                            expo(q)
                        if 2 <= q < UNITS + 2:
                            turned(q - 2)
                        if q >= 4 and (q - 4) % (CH * HG) == CH * HG - 1:
                            taken((q - 4) // (CH * HG))
                act.wait_ge(veps_done, b + 1)
                act.activation(rstd[:, 1, :], rstd[:, 0, :], ACT.Sqrt).then_inc(ysd_done, 1)

        @block.vector
        def _(dve):
            count = [0]

            def chain(ins, base):
                count[0] += 1
                ins.then_inc(link, 1)
                dve.wait_ge(link, base + count[0])

            dve.wait_ge(d_const[0], 16)
            for k in range(KC):
                dve.wait_ge(d_const[5 + k], 16)
                src = stage[:, 4 * k:4 * k + 3, :].rearrange("p a e -> p (a e)")
                wh, wl = (w[:, k].rearrange("p g n -> p (g n)") for w in (w_hi, w_lo))
                dve.tensor_copy(wh, src).then_inc(w_ready, 1)
                dve.wait_ge(w_ready, 2 * k + 1)
                dve.tensor_tensor(wl, src, wh.bitcast(F32), ALU.subtract).then_inc(w_ready, 1)
            dve.wait_ge(d_const[7], 16)
            dve.tensor_copy(wo_hi[:, :, :], stage[:, 0:GROUPS, :]).then_inc(w_ready, 1)
            dve.wait_ge(w_ready, 2 * KC + 1)
            dve.tensor_tensor(wo_lo[:, :, :], stage[:, 0:GROUPS, :], wo_hi[:, :, :].bitcast(F32),
                              ALU.subtract).then_inc(w_ready, 1)
            dve.tensor_copy(ident_b[:, :], ident[:, :]).then_inc(w_ready, 1)
            dve.wait_ge(d_const[1], 16)
            dve.tensor_copy(mask_b[:, :], mask_f[:, :]).then_inc(w_ready, 1)
            for n in range(2, 5):
                dve.wait_ge(d_const[n], 16)
            dve.nop().then_inc(y_done, 1)
            dve.nop().then_inc(res_done, 1)
            dve.nop().then_inc(tlo_done, 1)
            dve.nop().then_inc(olo_done, 1)
            LINKS = 4
            with dve.Fori(0, B) as b:
                for m in range(TILES // 2):
                    dve.wait_ge(xT_hi_done, b * (TILES // 2) + m + 1)
                    dst = slice(2 * m * P, (2 * m + 2) * P)
                    dve.tensor_tensor(xT_lo[:, :, dst], pX[m].rearrange("p (k n) -> p k n", k=KC),
                                      xT_hi[:, :, dst].bitcast(F32), ALU.subtract).then_inc(xT_lo_done, 1)
                with dve.Fori(0, GROUPS) as g:
                    n = b * GROUPS + g
                    count[0] = 0
                    base = n * LINKS
                    for m in range(TILES // 2):
                        dve.wait_ge(v_hi_done, n * 4 + m + 1)
                        src = pX[m][:, 0:2 * GW].rearrange("p (i s h d) -> p i s h d", i=2, s=3, h=HG)
                        for i in range(2):
                            t = dve.tensor_tensor(v_at(2 * m + i, D), src[:, i, 2],
                                                  v_at(2 * m + i, 0).bitcast(F32), ALU.subtract)
                        t.then_inc(v_lo_done, 1)
                    dve.wait_ge(qk_ready, n * 8 + 8)
                    qk_m = qk[:, :, :, :].rearrange("p s m d -> p (s m) d")
                    cen_m = qkc[:, :, :, :].rearrange("p s m d -> p (s m) d")
                    M = 2 * TILES * HG
                    chain(dve.tensor_reduce(st[:, 0, :], qk_m, AX.X, ALU.add), base)
                    dve.scalar_tensor_tensor(cen_m, st[:, 0, :].unsqueeze(2).broadcast_to([P, M, D]),
                                             -1.0 / D, qk_m, ALU.mult, ALU.add).then_inc(cen_done, 1)
                    dve.wait_ge(sq_done, n + 1)
                    chain(dve.tensor_reduce(st[:, 0, :], qk_sq[:, :, :, :].rearrange("p s m d -> p (s m) d"),
                                            AX.X, ALU.add), base)
                    dve.tensor_scalar(st[:, 1, :], st[:, 0, :], 1.0 / D, EPS, ALU.mult, ALU.add).then_inc(var_done, 1)
                    dve.wait_ge(sd_done, n + 1)
                    chain(dve.reciprocal(st[:, 0, :], st[:, 2, :]), base)
                    dve.wait_ge(gain_done, 2 * n + 2)
                    chain(dve.tensor_tensor(qk_m, qk_m, st[:, 0, :].unsqueeze(2).broadcast_to([P, M, D]),
                                            ALU.mult), base)
                    for s in range(2):
                        t = dve.tensor_tensor(
                            qkc[:, s].rearrange("p (t h) d -> p t (h d)", h=HG),
                            qk[:, s].rearrange("p (t h) d -> p t (h d)", h=HG),
                            b_row[:, s].rearrange("p h d -> p (h d)").unsqueeze(1).broadcast_to([P, TILES, QW]), ALU.add)
                    t.then_inc(norm_done, 1)
                    assert count[0] == LINKS
                    dve.wait_ge(part_hi, 2 * n + 1)
                    dve.wait_ge(norm_done, n + 1)
                    dve.tensor_tensor(parts[:, 0, :, 2:4, :],
                                      qkc[:, 0].unsqueeze(2).broadcast_to([P, TILES * HG, 2, D]),
                                      parts_f[:, 0, :, 0:2, :], ALU.subtract).then_inc(part_lo, 1)
                    dve.wait_ge(part_hi, 2 * n + 2)
                    dve.tensor_tensor(parts[:, 1, :, 1:4:2, :],
                                      qkc[:, 1].unsqueeze(2).broadcast_to([P, TILES * HG, 2, D]),
                                      parts_f[:, 1, :, 0:4:2, :], ALU.subtract).then_inc(part_lo, 1)
                    for z in range(1, 8, 2):
                        s, p, c = z // 4, z // 2 % 2, z % 2
                        dve.wait_ge(pt_done, n * 8 + z + 1)
                        dve.tensor_copy((qT, kT)[s][:, p, c * BANK:(c + 1) * BANK], pR[z % 4][:, :]).then_inc(pt_dve, 1)

                    def maximum(q):
                        c, j, ii = unit[q]
                        w = (c * CH + ii + 1) * P
                        dve.wait_ge(s_done, n * UNITS + q + 1)
                        dve.tensor_reduce(stats[:, 0, q:q + 1], S[q % 2][:, 0:w], AX.X, ALU.max,
                                          negate=True).then_inc(max_done, 1)

                    def total(q):
                        dve.wait_ge(exp_done, n * UNITS + q + 2)
                        dve.reciprocal(stats[:, 2, q:q + 1], stats[:, 1, q:q + 1]).then_inc(rec_done, 1)

                    def turned(q):
                        c, j, ii = unit[q]
                        v = q // CH
                        if ii == 0 and v >= 1:
                            dve.wait_ge(pv_done, n * BLOCKS + v)
                        for z in range(first_tch[q], first_tch[q + 1]):
                            _, k0, k1 = tch[z]
                            dve.wait_ge(thi_done, n * TCH + z + 1)
                            dve.tensor_tensor(pT_lo[:, k0:k1, ii * P:(ii + 1) * P],
                                              T[z % NT][:, 0:(k1 - k0) * P].rearrange("p (k n) -> p k n", n=P),
                                              pT_hi[:, v % 2, k0:k1, ii * P:(ii + 1) * P].bitcast(F32),
                                              ALU.subtract).then_inc(tlo_done, 1)

                    def taken(c):
                        dve.wait_ge(ohi_done, n * CHUNKS + c + 1)
                        dve.tensor_tensor(oT_lo[:, bass.ds(g, 1), c * BANK:(c + 1) * BANK], O[:, :],
                                          oT_hi[:, bass.ds(g, 1), c * BANK:(c + 1) * BANK].bitcast(F32),
                                          ALU.subtract).then_inc(olo_done, 1)

                    for q in range(UNITS + 4):
                        if q < UNITS:
                            maximum(q)
                        if 1 <= q < UNITS + 1:
                            total(q - 1)
                        if 2 <= q < UNITS + 2:
                            turned(q - 2)
                        if q >= 4 and (q - 4) % (CH * HG) == CH * HG - 1:
                            taken((q - 4) // (CH * HG))
                dve.wait_ge(xb_bias, b + 1)
                for i in range(TILES):
                    dve.wait_ge(wo_done, b * TILES + (i | 1) + 1)
                    dve.tensor_tensor(xb[:, i, :], pX[i // 2][:, (i % 2) * E:(i % 2 + 1) * E], xb[:, i, :],
                                      ALU.add).then_inc(res_done, 1)
                for i in range(TILES):
                    dve.wait_ge(res_done, b * TILES + i + 2)
                    dve.bn_stats(bn[:, i, :], xb[:, i, :]).then_inc(bns_done, 1)
                for i in range(TILES):
                    if i == 0:
                        wait_alone(dve, bns_done, (b + 1) * TILES, spare)
                    dve.bn_aggr(mv[:, i, :], bn[:, i, :]).then_inc(agg_done, 1)
                dve.wait_ge(agg_done, (b + 1) * TILES)
                dve.tensor_scalar(rstd[:, 0, :], mv[:, :, 1], EPS, None, ALU.add).then_inc(veps_done, 1)
                dve.wait_ge(ysd_done, b + 1)
                dve.reciprocal(rstd[:, 2, :], rstd[:, 1, :]).then_inc(yr_done, 1)
                dve.wait_ge(yr_done, b + 1)
                for i in range(TILES):
                    dve.tensor_scalar(xb[:, i, :], xb[:, i, :], mv[:, i, 0:1], rstd[:, 2, i:i + 1],
                                      ALU.subtract, ALU.mult).then_inc(y_done, 1)


def local_layers(nc, xs, B, out, rot, rot_scale, w_qkv, w_out, ident_in, mask_in, ln_gb, w1, b1, w2, b2):
    LAYERS = 2
    L, E = out.shape[1], out.shape[2]
    H, D = 8, 64
    W = H * D
    KC = E // P
    OC = W // P
    TILES = L // P
    U = 4
    TURNS = TILES // U
    assert TURNS == 2
    TL = B * TILES
    NQ = B * TURNS
    HH = H // 2
    HID = w1.shape[3] // 2
    FT = -(-HID // P)
    FR = [min(P, HID - f * P) for f in range(FT)]
    GT = 4
    NG = L // P // GT

    with ExitStack() as ctx:
        def keep(name, shape, dt):
            return ctx.enter_context(nc.sbuf_tensor(name, shape, dt))

        def ps(name, shape, dt=F32):
            return ctx.enter_context(nc.psum_tensor(name, shape, dt))

        def sem(name):
            return ctx.enter_context(nc.semaphore(name))

        ident = keep("l_ident", [P, P], F32)
        ident_b = keep("l_ident_b", [P, P], BF16)
        mask_f = keep("l_mask_f", [P, 3, 2, P], F32)
        mask_b = keep("l_mask_b", [P, 3, 2, P], BF16)
        rot_sb = keep("l_rot", [P, TILES, 4, D], F32)
        rsc = keep("l_rsc", [P, 4, D], F32)
        tab = keep("l_tab", [P, TILES, 4, D], F32)
        wq_hi = keep("l_wq_hi", [P, KC, 3 * W], F32R)
        wq_lo = keep("l_wq_lo", [P, KC, 3 * W], F32R)
        wo_hi = keep("l_wo_hi", [P, OC, E], F32R)
        wo_lo = keep("l_wo_lo", [P, OC, E], F32R)
        stage = keep("l_stage", [P, max(2 * HID, FT * E)], F32)
        w1_hi = keep("l_w1_hi", [P, KC, 2 * HID], F32R)
        w1_lo = keep("l_w1_lo", [P, KC, 2 * HID], F32R)
        w2_hi = keep("l_w2_hi", [P, FT, E], F32R)
        w2_lo = keep("l_w2_lo", [P, FT, E], F32R)
        b2_row = keep("l_b2", [P, E], F32)
        b1_col = keep("l_b1", [P, 2, FT], F32)
        gb_col = keep("l_gb", [P, 2, KC], F32)
        half = keep("l_half", [P, 2 * H], F32)

        k_hi = keep("l_k_hi", [P, H, 2, P], F32R)
        k_lo = keep("l_k_lo", [P, H, 2, P], F32R)
        v_hi = keep("l_v_hi", [P, 2, H, D], F32R)
        v_lo = keep("l_v_lo", [P, 2, H, D], F32R)
        F = [ps(f"l_F{i}", [P, BANK]) for i in range(3)]
        S = ps("l_S", [P, HH, 2 * P])
        T = ps("l_T", [P, 2, BANK])
        O = ps("l_O", [P, BANK])

        d_c = [sem(f"l_d_c{i}") for i in range(14)]
        const_ok = sem("l_const_ok")
        split = sem("l_split")
        phase = sem("l_phase")
        spare = sem("l_spare")

        place = ExitStack()
        xt = keep("l_xt", [P, U, E], F32)
        osb = keep("l_osb", [P, H, D], F32)

        def sb(name, shape, dt):
            return place.enter_context(nc.sbuf_tensor(name, shape, dt))

        h2 = sb("l_h2", [P, U, P], F32)
        hT_hi = sb("l_hT_hi", [P, KC, P], F32R)
        hT_lo = sb("l_hT_lo", [P, KC, P], F32R)
        kc = sb("l_kc", [P, W], F32)
        sq = sb("l_sq", [P, 2 * H, D], F32)
        ss = sb("l_ss", [P, 2, 2 * H], F32)
        rn = sb("l_rn", [P, 2, 2 * H], F32)
        ta = sb("l_ta", [P, 2, H, D], F32)
        tb = sb("l_tb", [P, 2, H, D], F32)
        qd = sb("l_qd", [P, 2, H, 2, D], F32)
        q_st = sb("l_q_st", [P, H, P], F32R)
        mx = sb("l_mx", [P, 4, H], F32)
        prob = sb("l_prob", [P, H, 2, P], F32)
        pT_hi = sb("l_pT_hi", [P, 2, HH, 2, P], F32R)
        pT_lo = sb("l_pT_lo", [P, 2, HH, 2, P], F32R)
        oT_hi = sb("l_oT_hi", [P, OC, P], F32R)
        oT_lo = sb("l_oT_lo", [P, OC, P], F32R)
        yb = sb("l_yb", [P, 2, E], F32)

        d_x = [sem(f"l_d_x{i}") for i in range(U)]
        d_h = [sem(f"l_d_h{i}") for i in range(U)]
        d_y = [sem(f"l_d_y{i}") for i in range(2)]
        hT_done = sem("l_hT_done")
        hT_hi_ok = sem("l_hT_hi_ok")
        hT_lo_ok = sem("l_hT_lo_ok")
        proj_done = [sem(f"l_{n}_done") for n in "qkv"]
        kc_ok = sem("l_kc_ok")
        sq_ok = [sem(f"l_{n}_sq_ok") for n in "qk"]
        sum_ok = [sem(f"l_{n}_sum_ok") for n in "qk"]
        ss_ok = [sem(f"l_{n}_ss_ok") for n in "qk"]
        rn_ok = [sem(f"l_{n}_rn_ok") for n in "qk"]
        vhi_ok = sem("l_vhi_ok")
        vlo_ok = sem("l_vlo_ok")
        q_terms = sem("l_q_terms")
        q_first = sem("l_q_first")
        qr_ok = sem("l_qr_ok")
        k_terms = sem("l_k_terms")
        k_rot = sem("l_k_rot")
        k_first = sem("l_k_first")
        kr_ok = sem("l_kr_ok")
        qkT_done = sem("l_qkT_done")
        st_hi_ok = sem("l_st_hi_ok")
        st_lo_ok = sem("l_st_lo_ok")
        s_done = sem("l_s_done")
        m_ok = sem("l_m_ok")
        mx_ok = sem("l_mx_ok")
        exp_ok = sem("l_exp_ok")
        ri_ok = sem("l_ri_ok")
        pT_done = sem("l_pT_done")
        pT_hi_ok = sem("l_pT_hi_ok")
        pT_lo_ok = sem("l_pT_lo_ok")
        pv_done = sem("l_pv_done")
        osb_ok = sem("l_osb_ok")
        oT_done = sem("l_oT_done")
        oT_hi_ok = sem("l_oT_hi_ok")
        oT_lo_ok = sem("l_oT_lo_ok")
        wo_done = sem("l_wo_done")
        y_ok = sem("l_y_ok")
        gch = sem("l_gch")
        FZ = (F[0], F[1], F[2], F[1])
        FP = (F[1], F[2], F[0])

        place.close()

        mxt = sb("m_x", [P, GT, E], F32)
        mh2 = sb("m_h2", [P, GT, P], F32)
        mz = sb("m_z", [P, GT, E], F32)
        mbn = sb("m_bn", [P, GT, 2, 6], F32)
        mmv = sb("m_mv", [P, GT, 2], F32)
        mrs = sb("m_rs", [P, 2, GT], F32)
        zT = sb("m_zT", [P, KC, GT * P], F32)
        zT_hi = sb("m_zT_hi", [P, KC, GT * P], F32R)
        zT_lo = sb("m_zT_lo", [P, KC, GT * P], F32R)
        gel = sb("m_gel", [P, 2, BANK], F32)
        hid = sb("m_hid", [P, 2, BANK], F32)
        hid_hi = sb("m_hid_hi", [P, FT, BANK], F32R)
        hid_lo = sb("m_hid_lo", [P, FT, BANK], F32R)
        my = sb("m_y", [P, GT, E], F32)
        A = [F[0], T[:, 0, :]]
        G = [F[1], T[:, 1, :]]
        ZT = [S[:, :, :].rearrange("p h n -> p (h n)")[:, 0:BANK], S[:, :, :].rearrange("p h n -> p (h n)")[:, BANK:]]
        Y = [F[2], O]
        place.close()
        d_mx, d_mh, d_my = sem("m_d_x"), sem("m_d_h"), sem("m_d_y")
        bn_ok = sem("m_bn_ok")
        ve_ok = sem("m_ve_ok")
        rs_ok = sem("m_rs_ok")
        z_ok = sem("m_z_ok")
        zT_done = sem("m_zT_done")
        zT_ok = sem("m_zT_ok")
        zhi_ok = sem("m_zhi_ok")
        zlo_ok = sem("m_zlo_ok")
        ag_done = sem("m_ag_done")
        gel_ok = sem("m_gel_ok")
        hid_ok = sem("m_hid_ok")
        hhi_ok = sem("m_hhi_ok")
        hlo_ok = sem("m_hlo_ok")
        w2_done = sem("m_w2_done")
        xb_ok = sem("m_xb_ok")
        my_ok = sem("m_y_ok")

        d_fx, d_fy, d_fo = sem("f_d_x"), sem("f_d_y"), sem("f_d_o")
        f_add, f_bn, f_ag, f_rs, f_ok = (sem(f"f_{n}") for n in ("add", "bn", "ag", "rs", "ok"))

        ENGINES = 5

        def meet(eng, k):
            eng.drain().then_inc(phase, 1)
            wait_alone(eng, phase, ENGINES * k, spare)

        def next_tile(q, u):
            return bass.ds(q * U + u + 1, 1) if u < U - 1 else bass.ds(U - q * U, 1)

        block = ctx.enter_context(nc.Block())

        @block.sync
        def _(sp):
            for n, (dst, src) in enumerate([(ident[:, :], ident_in), (mask_f[:, :, :, :], mask_in),
                                            (rot_sb[:, :, :, :], rot)]):
                sp.dma_start(dst, src).then_inc(d_c[n], 16)
            with sp.Fori(0, LAYERS) as l:
                SPLITS = 2 * (2 * KC + KC + 2)
                parts = ([w_qkv[l, :, k, a * 3 * W // 2:(a + 1) * 3 * W // 2] for k in range(KC) for a in range(2)]
                         + [w1[l, :, k, :] for k in range(KC)] + [w_out[l], w2[l]])
                small = [(rsc[:, :, :], rot_scale[l]), (gb_col[:, :, :], ln_gb[l]), (b1_col[:, :, :], b1[l]),
                         (b2_row[:, :], b2[l])]
                for n, (dst, src) in enumerate(small):
                    sp.dma_start(dst, src).then_inc(d_c[3 + n], 16)
                for n, src in enumerate(parts):
                    if n:
                        sp.wait_ge(split, l * SPLITS + 2 * n)
                    src = src if len(src.shape) == 2 else src.rearrange("p a b -> p (a b)")
                    sp.dma_start(stage[:, 0:src.shape[1]], src).then_inc(d_c[7], 16)

                def load(r, v):
                    sp.dma_start(xt[:, v, :], xs[l, bass.ds(r + 1, P), :]).then_inc(d_x[v], 16)
                    sp.dma_start(h2[:, v, :], xs[l, bass.ds(r, P), P:E]).then_inc(d_h[v], 16)

                def store(r, c, v):
                    sp.wait_ge(y_ok, c + 2)
                    sp.dma_start(xs[2, bass.ds(r + 1, P), :], yb[:, v, :]).then_inc(d_y[v], 16)

                load(LEAD, 0)
                with sp.Fori(0, B) as b:
                    with sp.Fori(0, TURNS) as q:
                        m = (l * B + b) * TURNS + q
                        row = LEAD + b * (L + 1) + q * (U * P)
                        for u in range(U):
                            load(row + ((u + 1) * P if u < U - 1 else U * P + q), (u + 1) % U)
                            store(row + (u - 1) * P if u else row + q - (P + 1), U * m + l + u, u % 2)
                store(LEAD + B * (L + 1) - 1 - P, (l + 1) * TL + l, 0)
                wait_alone(sp, d_y[0], (l + 1) * (TL // 2 + 1) * 16 + 1, spare)
                wait_alone(sp, d_y[1], (l + 1) * (TL // 2) * 16 + 1, spare)
                meet(sp, 2 * l + 1)
                with sp.Fori(0, B) as b:
                    with sp.Fori(0, NG) as g:
                        m = (l * B + b) * NG + g
                        r = LEAD + b * (L + 1) + g * (GT * P)
                        sp.dma_start(mxt[:, :, :], xs[2, bass.ds(r + 1, GT * P), :].rearrange(
                            "(t p) e -> p t e", p=P)).then_inc(d_mx, 16)
                        sp.dma_start(mh2[:, :, :], xs[2, bass.ds(r, GT * P), P:E].rearrange(
                            "(t p) e -> p t e", p=P)).then_inc(d_mh, 16)
                        sp.wait_ge(my_ok, GT * (m + 1))
                        sp.dma_start(xs[1, bass.ds(r + 1, GT * P), :].rearrange("(t p) e -> p t e", p=P),
                                     my[:, :, :]).then_inc(d_my, 16)
                        wait_alone(sp, d_my, 16 * (m + 1), spare)
                meet(sp, 2 * l + 2)
            with sp.Fori(0, B) as b:
                with sp.Fori(0, NG) as g:
                    m = b * NG + g
                    r = LEAD + b * (L + 1) + g * (GT * P)
                    sp.dma_start(mxt[:, :, :], xs[0, bass.ds(r + 1, GT * P), :].rearrange(
                        "(t p) e -> p t e", p=P)).then_inc(d_fx, 16)
                    sp.dma_start(mz[:, :, :], xs[1, bass.ds(r + 1, GT * P), :].rearrange(
                        "(t p) e -> p t e", p=P)).then_inc(d_fy, 16)
                    sp.wait_ge(f_ok, GT * (m + 1))
                    sp.dma_start(out[b, bass.ds(g * (GT * P), GT * P), :].rearrange("(t p) e -> p t e", p=P),
                                 my[:, :, :]).then_inc(d_fo, 16)
                    wait_alone(sp, d_fo, 16 * (m + 1), spare)

        @block.gpsimd
        def _(pool):
            pool.memset(half[:, :], -0.5).then_inc(gch, 1)
            for t in (k_hi, k_lo):
                pool.memset(t[:, :, 1, :].bitcast(F32), 0.0).then_inc(const_ok, 1)
            for t in (v_hi, v_lo):
                pool.memset(t[:, 1, :, :].bitcast(F32), 0.0).then_inc(const_ok, 1)
            pool.memset(xt[:, :, :], 0.0).then_inc(const_ok, 1)
            pool.memset(osb[:, :, :], 0.0).then_inc(const_ok, 1)
            pool.wait_ge(gch, 1)
            with pool.Fori(0, LAYERS) as l:

                def front(f, tile, v):
                    wait_alone(pool, kc_ok, f + 1, spare)
                    k3 = kc[:, :].rearrange("p (h d) -> p h d", h=H)

                    def row(z, a, c):
                        return tab[:, tile, z, a:c].broadcast_to([P, H, c - a])
                    pool.tensor_tensor(ta[:, 1], k3, row(2, 0, D), ALU.mult)
                    pool.tensor_tensor(tb[:, 1, :, 0:D // 2], k3[:, :, D // 2:D], row(3, 0, D // 2), ALU.mult)
                    pool.tensor_tensor(tb[:, 1, :, D // 2:D], k3[:, :, 0:D // 2], row(3, D // 2, D),
                                       ALU.mult).then_inc(k_terms, 1)
                    pool.wait_ge(k_terms, f + 1)
                    pool.tensor_tensor(ta[:, 1], ta[:, 1], tb[:, 1], ALU.add).then_inc(k_rot, 1)
                    pool.wait_ge(ss_ok[1], f + 1)
                    pool.tensor_tensor(rn[:, v, H:2 * H], ss[:, 1, H:2 * H], half[:, 0:H], ALU.pow).then_inc(rn_ok[1], 1)
                    pool.wait_ge(rn_ok[1], f + 1)
                    pool.wait_ge(k_rot, f + 1)
                    pool.tensor_tensor(qd[:, 1, :, 0, :], ta[:, 1],
                                       rn[:, v, H:2 * H].unsqueeze(2).broadcast_to([P, H, D]),
                                       ALU.mult).then_inc(k_first, 1)
                    pool.wait_ge(ss_ok[0], f + 1)
                    pool.tensor_tensor(rn[:, v, 0:H], ss[:, 1, 0:H], half[:, 0:H], ALU.pow).then_inc(rn_ok[0], 1)

                front(l * (TL + 1), slice(0, 1), 0)
                with pool.Fori(0, B) as b:
                    with pool.Fori(0, TURNS) as q:
                        m = (l * B + b) * TURNS + q
                        for u in range(U):
                            front(U * m + l + u + 1, next_tile(q, u), (u + 1) % 2)
                meet(pool, 2 * l + 1)
                with pool.Fori(0, B) as b:
                    with pool.Fori(0, NG) as g:
                        m = (l * B + b) * NG + g
                        pool.wait_ge(ve_ok, m + 1)
                        pool.tensor_tensor(mrs[:, 1, :], mrs[:, 0, :], half[:, 0:GT], ALU.pow).then_inc(rs_ok, 1)
                        pool.wait_ge(d_mx, 16 * (m + 1))
                        pool.wait_ge(z_ok, m + 1)
                        pool.tensor_tensor(mxt[:, :, :], mxt[:, :, :], b2_row[:, :].unsqueeze(1).broadcast_to([P, GT, E]),
                                           ALU.add).then_inc(xb_ok, 1)
                        for f in range(FT):
                            r = FR[f]
                            pool.wait_ge(hhi_ok, m * FT + f + 1)
                            pool.tensor_tensor(hid_lo[0:r, f, :], hid[0:r, f % 2, :], hid_hi[0:r, f, :].bitcast(F32),
                                               ALU.subtract).then_inc(hlo_ok, 1)
                meet(pool, 2 * l + 2)
            with pool.Fori(0, B) as b:
                with pool.Fori(0, NG) as g:
                    m = b * NG + g
                    pool.wait_ge(f_ag, m + 1)
                    pool.tensor_tensor(mrs[:, 1, :], mrs[:, 0, :], half[:, 0:GT], ALU.pow).then_inc(f_rs, 1)

        @block.tensor
        def _(pe):
            pe.wait_ge(const_ok, 6 + 2)
            with pe.Fori(0, LAYERS) as l:
                wait_alone(pe, split, (l + 1) * 2 * (3 * KC + 2), spare)

                def turn_x(f, v, loads):
                    pe.wait_ge(d_x[v], 16 * loads)
                    pe.wait_ge(d_h[v], 16 * loads)
                    pe.transpose(T[:, 1, 0:P], xt[:, v, 0:P], ident[:, :])
                    pe.transpose(T[:, 1, P:2 * P], h2[:, v, :], ident[:, :]).then_inc(hT_done, 1)

                def project(f, s):
                    if s == 1:
                        pe.wait_ge(hT_lo_ok, f + 1)
                    elif s == 0:
                        pe.wait_ge(st_lo_ok, 4 * f + 1)
                    else:
                        pe.wait_ge(st_lo_ok, 4 * f + 2)
                    ops = [(a, w, k) for k in range(KC) for a, w in ((hT_hi, wq_hi), (hT_lo, wq_hi), (hT_hi, wq_lo))]
                    for z, (a, w, k) in enumerate(ops):
                        mm = pe.matmul(FP[s][:, :], a[:, k, :], w[:, k, s * W:(s + 1) * W],
                                       start=(z == 0), stop=(z == len(ops) - 1))
                    mm.then_inc(proj_done[s], 1)

                def stack(f, z):
                    s, hf = z // 2, z % 2
                    if z == 0:
                        pe.wait_ge(qr_ok, f + 1)
                        pe.wait_ge(vlo_ok, f + 1)
                    elif z == 1:
                        pe.wait_ge(sq_ok[0], f + 1)
                    elif z == 2:
                        pe.wait_ge(kr_ok, f + 1)
                        pe.wait_ge(sq_ok[1], f + 1)
                    else:
                        pe.wait_ge(st_lo_ok, 4 * f + 3)
                    for h in range(HH):
                        tr = pe.transpose(FZ[z][:, h * P:(h + 1) * P],
                                          qd[:, s, hf * HH + h, :, :].rearrange("p a d -> p (a d)"), ident[:, :])
                    tr.then_inc(qkT_done, 1)

                def scores(t, f, hf, mk):
                    pe.wait_ge(st_lo_ok, 4 * f + 4 + hf)
                    if hf:
                        pe.wait_ge(exp_ok, 4 * t + 2)
                    for h in range(HH):
                        hh = hf * HH + h
                        for z, kk in enumerate((k_hi, k_lo)):
                            pe.matmul(S[:, h, :], q_st[:, hh, :], kk[:, hh].rearrange("p a n -> p (a n)"),
                                      start=(z == 0), stop=False)
                        mm = pe.matmul(S[:, h, :], ident_b[:, :], mk.rearrange("p o a n -> p (o a n)"),
                                       start=False, stop=True)
                    mm.then_inc(s_done, 1)

                def turn_p(t, hf, c):
                    pe.wait_ge(exp_ok, 4 * t + 2 * hf + c + 1)
                    for z in range(4):
                        h, s = 2 * c + z // 2, z % 2
                        tr = pe.transpose(T[:, c, z * P:(z + 1) * P], prob[:, hf * HH + h, s, :], ident[:, :])
                    tr.then_inc(pT_done, 1)

                def mix(t, f, hf):
                    if hf == 0:
                        pe.wait_ge(y_ok, f + 2)
                        pe.wait_ge(vlo_ok, f + 2)
                    for h in range(HH):
                        if h % 2 == 0:
                            pe.wait_ge(pT_lo_ok, 4 * t + 2 * hf + h // 2 + 1)
                        hh = hf * HH + h
                        ops = [(a, v, s) for s in range(2) for a, v in ((pT_hi, v_hi), (pT_hi, v_lo), (pT_lo, v_hi))]
                        for z, (a, v, s) in enumerate(ops):
                            mm = pe.matmul(O[:, hh * D:(hh + 1) * D], a[:, hf, h, s, :], v[:, s, hh, :],
                                           start=(z == 0), stop=(z == len(ops) - 1))
                    mm.then_inc(pv_done, 1)

                def turn_o(t):
                    pe.wait_ge(osb_ok, t + 1)
                    for k in range(OC):
                        tr = pe.transpose(T[:, 0, k * P:(k + 1) * P],
                                          osb[:, 2 * k:2 * k + 2, :].rearrange("p a d -> p (a d)"), ident[:, :])
                    tr.then_inc(oT_done, 1)

                def project_out(c):
                    pe.wait_ge(oT_lo_ok, c + 1)
                    ops = [(a, w, k) for k in range(OC) for a, w in ((oT_hi, wo_hi), (oT_lo, wo_hi), (oT_hi, wo_lo))]
                    for z, (a, w, k) in enumerate(ops):
                        mm = pe.matmul(O[:, 0:E], a[:, k, :], w[:, k, :], start=(z == 0), stop=(z == len(ops) - 1))
                    mm.then_inc(wo_done, 1)

                f = l * (TL + 1)
                turn_x(f, 0, l * (NQ + 1) + 1)
                for s in (1, 0):
                    project(f, s)
                for z in range(4):
                    stack(f, z)
                project(f, 2)
                with pe.Fori(0, B) as b:
                    with pe.Fori(0, TURNS) as q:
                        m = (l * B + b) * TURNS + q
                        for u in range(U):
                            t, f = U * m + u, U * m + l + u
                            turn_x(f + 1, (u + 1) % U, m + 1 if u < U - 1 else m + l + 2)
                            scores(t, f, 0, mask_b[:, bass.ds(q, 1)] if u == 0 else
                                   mask_b[:, 1:2] if u % 2 == 0 else mask_b[:, 2:3])
                            turn_o(t)
                            project(f + 1, 1)
                            project(f + 1, 0)
                            project_out(f)
                            turn_p(t, 0, 0)
                            turn_p(t, 0, 1)
                            scores(t, f, 1, mask_b[:, bass.ds(q, 1)] if u == 0 else
                                   mask_b[:, 1:2] if u % 2 == 0 else mask_b[:, 2:3])
                            stack(f + 1, 0)
                            stack(f + 1, 1)
                            mix(t, f, 0)
                            turn_p(t, 1, 0)
                            project(f + 1, 2)
                            turn_p(t, 1, 1)
                            stack(f + 1, 2)
                            stack(f + 1, 3)
                            mix(t, f, 1)
                turn_o((l + 1) * TL)
                project_out((l + 1) * TL + l)
                meet(pe, 2 * l + 1)
                with pe.Fori(0, B) as b:
                    with pe.Fori(0, NG) as g:
                        m = (l * B + b) * NG + g
                        pe.wait_ge(z_ok, m + 1)
                        for k in range(KC):
                            for t in range(GT):
                                tr = pe.transpose(ZT[k][:, t * P:(t + 1) * P], mz[:, t, k * P:(k + 1) * P], ident[:, :])
                            tr.then_inc(zT_done, 1)
                        pe.wait_ge(zlo_ok, m + 1)
                        for f in range(FT):
                            r = FR[f]
                            if f >= 2:
                                pe.wait_ge(hid_ok, m * FT + f - 1)
                            for dst, off in ((A[f % 2], 0), (G[f % 2], HID)):
                                ops = [(w, a, k) for k in range(KC) for w, a in
                                       ((w1_hi, zT_hi), (w1_lo, zT_hi), (w1_hi, zT_lo))]
                                for z, (w, a, k) in enumerate(ops):
                                    mm = pe.matmul(dst[0:r, :], w[:, k, off + f * P:off + f * P + r], a[:, k, :],
                                                   start=(z == 0), stop=(z == len(ops) - 1))
                            mm.then_inc(ag_done, 1)
                        pe.wait_ge(hlo_ok, (m + 1) * FT)
                        for t in range(GT):
                            o = Y[t // 2][:, (t % 2) * E:(t % 2 + 1) * E]
                            ops = [(a, w, f) for f in range(FT) for a, w in
                                   ((hid_hi, w2_hi), (hid_lo, w2_hi), (hid_hi, w2_lo))]
                            for z, (a, w, f) in enumerate(ops):
                                mm = pe.matmul(o, a[0:FR[f], f, t * P:(t + 1) * P], w[0:FR[f], f, :],
                                               start=(z == 0), stop=(z == len(ops) - 1))
                            mm.then_inc(w2_done, 1)
                        pe.wait_ge(my_ok, (m + 1) * GT)
                meet(pe, 2 * l + 2)

        @block.scalar
        def _(act):
            with act.Fori(0, LAYERS) as l:

                def x_hi(f):
                    act.wait_ge(hT_done, f + 1)
                    act.activation(hT_hi[:, :, :].rearrange("p k n -> p (k n)"), T[:, 1, 0:2 * P],
                                   ACT.Copy).then_inc(hT_hi_ok, 1)

                def o_hi(c):
                    act.wait_ge(oT_done, c + 1)
                    act.activation(oT_hi[:, :, :].rearrange("p k n -> p (k n)"), T[:, 0, :],
                                   ACT.Copy).then_inc(oT_hi_ok, 1)

                def copy_k(f):
                    act.wait_ge(proj_done[1], f + 1)
                    act.activation(kc[:, :], FP[1][:, :], ACT.Copy).then_inc(kc_ok, 1)

                def second(f, s):
                    act.wait_ge((q_first, k_first)[s], f + 1)
                    act.activation(qd[:, s, :, 1, :], qd[:, s, :, 0, :], ACT.Copy).then_inc((qr_ok, kr_ok)[s], 1)

                def square(f, s):
                    if s:
                        act.wait_ge(proj_done[1], f + 1)
                    else:
                        act.wait_ge(q_terms, f + 1)
                    act.activation(sq[:, s * H:(s + 1) * H, :].rearrange("p h d -> p (h d)"), FP[s][:, :],
                                   ACT.Square).then_inc(sq_ok[s], 1)

                def expo(t, hf, v):
                    act.wait_ge(mx_ok, 2 * t + hf + 1)
                    for hh in range(hf * HH, (hf + 1) * HH):
                        e = act.activation(prob[:, hh].rearrange("p a n -> p (a n)"), S[:, hh % HH, :], ACT.Exp,
                                           bias=mx[:, 1, hh:hh + 1], scale=rn[:, v, hh:hh + 1],
                                           accum_out=mx[:, 2, hh:hh + 1])
                        if hh % 2:
                            e.then_inc(exp_ok, 1)

                def p_hi(t, hf, c):
                    act.wait_ge(pT_done, 4 * t + 2 * hf + c + 1)
                    act.activation(pT_hi[:, hf, 2 * c:2 * c + 2].rearrange("p h s n -> p (h s n)"),
                                   T[:, c, :], ACT.Copy).then_inc(pT_hi_ok, 1)

                def stack_hi(f, z, v):
                    s, hf = z // 2, z % 2
                    act.wait_ge(qkT_done, 4 * f + z + 1)
                    hs = slice(hf * HH, (hf + 1) * HH)
                    act.activation(q_st[:, hs, :] if s == 0 else k_hi[:, hs, v, :],
                                   FZ[z][:, :].rearrange("p (h n) -> p h n", h=HH), ACT.Copy).then_inc(st_hi_ok, 1)

                def values_hi(f, v):
                    act.wait_ge(proj_done[2], f + 1)
                    act.activation(v_hi[:, v].rearrange("p h d -> p (h d)"), F[0][:, :], ACT.Copy).then_inc(vhi_ok, 1)

                f = l * (TL + 1)
                x_hi(f)
                copy_k(f)
                for s in (1, 0):
                    square(f, s)
                for z in range(4):
                    if z % 2 == 0:
                        second(f, z // 2)
                    stack_hi(f, z, 0)
                with act.Fori(0, B) as b:
                    with act.Fori(0, TURNS) as q:
                        m = (l * B + b) * TURNS + q
                        for u in range(U):
                            t, f, v = U * m + u, U * m + l + u, (u + 1) % 2
                            x_hi(f + 1)
                            values_hi(f, u % 2)
                            o_hi(f)
                            copy_k(f + 1)
                            expo(t, 0, u % 2)
                            square(f + 1, 1)
                            square(f + 1, 0)
                            second(f + 1, 0)
                            p_hi(t, 0, 0)
                            p_hi(t, 0, 1)
                            stack_hi(f + 1, 0, v)
                            stack_hi(f + 1, 1, v)
                            expo(t, 1, u % 2)
                            p_hi(t, 1, 0)
                            second(f + 1, 1)
                            p_hi(t, 1, 1)
                            stack_hi(f + 1, 2, v)
                            stack_hi(f + 1, 3, v)
                o_hi((l + 1) * TL + l)
                values_hi((l + 1) * TL + l, 0)
                meet(act, 2 * l + 1)
                with act.Fori(0, B) as b:
                    with act.Fori(0, NG) as g:
                        m = (l * B + b) * NG + g
                        act.wait_ge(zT_ok, m * 2 + 2)
                        act.activation(zT_hi[:, :, :], zT[:, :, :], ACT.Copy).then_inc(zhi_ok, 1)
                        for f in range(FT):
                            r = FR[f]
                            act.wait_ge(ag_done, m * FT + f + 1)
                            act.activation(gel[0:r, f % 2, :], G[f % 2][0:r, :], ACT.Gelu,
                                           bias=b1_col[0:r, 1, f:f + 1]).then_inc(gel_ok, 1)
                            act.wait_ge(hid_ok, m * FT + f + 1)
                            act.activation(hid_hi[0:r, f, :], hid[0:r, f % 2, :], ACT.Copy).then_inc(hhi_ok, 1)
                        act.wait_ge(w2_done, (m + 1) * GT)
                meet(act, 2 * l + 2)

        @block.vector
        def _(dve):
            dve.wait_ge(d_c[0], 16)
            dve.tensor_copy(ident_b[:, :], ident[:, :]).then_inc(const_ok, 1)
            dve.wait_ge(d_c[1], 16)
            dve.tensor_copy(mask_b[:, :, :, :], mask_f[:, :, :, :]).then_inc(const_ok, 1)
            dve.wait_ge(d_c[2], 16)
            dve.wait_ge(const_ok, 8)
            for c in (y_ok, osb_ok, vlo_ok, st_lo_ok, d_y[0], d_y[1]):
                dve.nop().then_inc(c, 1)
            with dve.Fori(0, LAYERS) as l:
                SPLITS = 2 * (3 * KC + 2)
                for n in range(4):
                    dve.wait_ge(d_c[3 + n], 16 * (l + 1))
                dve.tensor_tensor(tab[:, :, :, :].rearrange("p t z d -> p t (z d)"),
                                  rot_sb[:, :, :, :].rearrange("p t z d -> p t (z d)"),
                                  rsc[:, :, :].rearrange("p z d -> p (z d)").unsqueeze(1).broadcast_to(
                                      [P, TILES, 4 * D]), ALU.mult)
                HW = 3 * W // 2
                dsts = ([(wq_hi[:, k, a * HW:(a + 1) * HW], wq_lo[:, k, a * HW:(a + 1) * HW])
                         for k in range(KC) for a in range(2)]
                        + [(w1_hi[:, k, :], w1_lo[:, k, :]) for k in range(KC)]
                        + [(wo_hi[:, :, :].rearrange("p a b -> p (a b)"), wo_lo[:, :, :].rearrange("p a b -> p (a b)")),
                           (w2_hi[:, :, :].rearrange("p a b -> p (a b)"), w2_lo[:, :, :].rearrange("p a b -> p (a b)"))])
                for n, (hi, lo) in enumerate(dsts):
                    dve.wait_ge(d_c[7], 16 * (l * len(dsts) + n + 1))
                    w = hi.shape[1]
                    dve.tensor_copy(hi, stage[:, 0:w]).then_inc(split, 1)
                    dve.wait_ge(split, l * SPLITS + 2 * n + 1)
                    dve.tensor_tensor(lo, stage[:, 0:w], hi.bitcast(F32), ALU.subtract).then_inc(split, 1)
                wait_alone(dve, split, (l + 1) * SPLITS, spare)

                def x_lo(f):
                    dve.wait_ge(hT_hi_ok, f + 1)
                    dve.tensor_tensor(hT_lo[:, :, :].rearrange("p k n -> p (k n)"), T[:, 1, 0:2 * P],
                                      hT_hi[:, :, :].rearrange("p k n -> p (k n)").bitcast(F32),
                                      ALU.subtract).then_inc(hT_lo_ok, 1)

                def o_lo(c):
                    dve.wait_ge(oT_hi_ok, c + 1)
                    dve.tensor_tensor(oT_lo[:, :, :].rearrange("p k n -> p (k n)"), T[:, 0, :],
                                      oT_hi[:, :, :].rearrange("p k n -> p (k n)").bitcast(F32),
                                      ALU.subtract).then_inc(oT_lo_ok, 1)

                def residual(c, v, w, stores):
                    dve.wait_ge(wo_done, c + 1)
                    dve.wait_ge(d_y[w], 16 * stores + 1)
                    dve.tensor_tensor(yb[:, w, :], O[:, 0:E], xt[:, v, :], ALU.add).then_inc(y_ok, 1)

                def norms(f, s):
                    hs = slice(s * H, (s + 1) * H)
                    dve.wait_ge(sq_ok[s], f + 1)
                    dve.tensor_reduce(ss[:, 0, hs], sq[:, hs, :], AX.X, ALU.add).then_inc(sum_ok[s], 1)
                    dve.wait_ge(sum_ok[s], f + 1)
                    dve.tensor_scalar(ss[:, 1, hs], ss[:, 0, hs], 1e-24, None, ALU.max).then_inc(ss_ok[s], 1)

                def rotate_q(f, tile):
                    wait_alone(dve, proj_done[0], f + 1, spare)
                    q3 = F[1][:, :].rearrange("p (h d) -> p h d", h=H)

                    def row(z, a, c):
                        return tab[:, tile, z, a:c].broadcast_to([P, H, c - a])
                    dve.tensor_tensor(ta[:, 0], q3, row(0, 0, D), ALU.mult)
                    dve.tensor_tensor(tb[:, 0, :, 0:D // 2], q3[:, :, D // 2:D], row(1, 0, D // 2), ALU.mult)
                    dve.tensor_tensor(tb[:, 0, :, D // 2:D], q3[:, :, 0:D // 2], row(1, D // 2, D),
                                      ALU.mult).then_inc(q_terms, 1)
                    dve.wait_ge(q_terms, f + 1)
                    dve.tensor_tensor(qd[:, 0, :, 0, :], ta[:, 0], tb[:, 0], ALU.add).then_inc(q_first, 1)

                def stack_lo(f, z, v):
                    s, hf = z // 2, z % 2
                    dve.wait_ge(st_hi_ok, 4 * f + z + 1)
                    src = FZ[z][:, :].rearrange("p (h n) -> p h n", h=HH)
                    hs = slice(hf * HH, (hf + 1) * HH)
                    if s == 0:
                        dve.tensor_tensor(q_st[D:P, hs, :], src[D:P], q_st[D:P, hs, :].bitcast(F32),
                                          ALU.subtract).then_inc(st_lo_ok, 1)
                    else:
                        dve.tensor_tensor(k_lo[:, hs, v, :], src, k_hi[:, hs, v, :].bitcast(F32),
                                          ALU.subtract).then_inc(st_lo_ok, 1)

                def values_lo(f, v):
                    dve.wait_ge(vhi_ok, f + 1)
                    dve.tensor_tensor(v_lo[:, v].rearrange("p h d -> p (h d)"), F[0][:, :],
                                      v_hi[:, v].rearrange("p h d -> p (h d)").bitcast(F32),
                                      ALU.subtract).then_inc(vlo_ok, 1)

                def maximum(t, f, hf, v):
                    hs = slice(hf * HH, (hf + 1) * HH)
                    dve.wait_ge(s_done, 2 * t + hf + 1)
                    dve.tensor_reduce(mx[:, 0, hs], S[:, :, :], AX.X, ALU.max, negate=True).then_inc(m_ok, 1)
                    dve.wait_ge(rn_ok[0], f + 1)
                    dve.wait_ge(m_ok, 2 * t + hf + 1)
                    dve.tensor_tensor(mx[:, 1, hs], mx[:, 0, hs], rn[:, v, hs], ALU.mult).then_inc(mx_ok, 1)

                def p_lo(t, hf):
                    for c in range(2):
                        dve.wait_ge(pT_hi_ok, 4 * t + 2 * hf + c + 1)
                        dve.tensor_tensor(pT_lo[:, hf, 2 * c:2 * c + 2].rearrange("p h s n -> p (h s n)"), T[:, c, :],
                                          pT_hi[:, hf, 2 * c:2 * c + 2].rearrange("p h s n -> p (h s n)").bitcast(F32),
                                          ALU.subtract).then_inc(pT_lo_ok, 1)

                def normalise(t):
                    dve.wait_ge(exp_ok, 4 * t + 4)
                    dve.reciprocal(mx[:, 3, :], mx[:, 2, :]).then_inc(ri_ok, 1)
                    dve.wait_ge(ri_ok, t + 1)
                    dve.wait_ge(pv_done, 2 * t + 2)
                    dve.tensor_tensor(osb[:, :, :], O[:, :].rearrange("p (h d) -> p h d", h=H),
                                      mx[:, 3, :].unsqueeze(2).broadcast_to([P, H, D]), ALU.mult).then_inc(osb_ok, 1)

                f = l * (TL + 1)
                x_lo(f)
                rotate_q(f, slice(0, 1))
                for s in (1, 0):
                    norms(f, s)
                stack_lo(f, 0, 0)
                stack_lo(f, 1, 0)
                stack_lo(f, 2, 0)
                stack_lo(f, 3, 0)
                with dve.Fori(0, B) as b:
                    with dve.Fori(0, TURNS) as q:
                        m = (l * B + b) * TURNS + q
                        for u in range(U):
                            t, f, v = U * m + u, U * m + l + u, (u + 1) % 2
                            x_lo(f + 1)
                            values_lo(f, u % 2)
                            maximum(t, f, 0, u % 2)
                            o_lo(f)
                            rotate_q(f + 1, next_tile(q, u))
                            residual(f, (u - 1) % U, u % 2, 2 * m + (u // 2) + (l if u % 2 == 0 else 0))
                            norms(f + 1, 1)
                            p_lo(t, 0)
                            maximum(t, f, 1, u % 2)
                            stack_lo(f + 1, 0, v)
                            stack_lo(f + 1, 1, v)
                            norms(f + 1, 0)
                            p_lo(t, 1)
                            stack_lo(f + 1, 2, v)
                            stack_lo(f + 1, 3, v)
                            normalise(t)
                values_lo((l + 1) * TL + l, 0)
                o_lo((l + 1) * TL + l)
                residual((l + 1) * TL + l, U - 1, 0, (l + 1) * TL // 2 + l)
                meet(dve, 2 * l + 1)
                with dve.Fori(0, B) as b:
                    with dve.Fori(0, NG) as g:
                        m = (l * B + b) * NG + g
                        dve.wait_ge(d_mx, 16 * (m + 1))
                        dve.wait_ge(d_mh, 16 * (m + 1))
                        for t in range(GT):
                            dve.bn_stats(mbn[:, t, 0, :], mxt[:, t, 0:P])
                            st = dve.bn_stats(mbn[:, t, 1, :], mh2[:, t, :])
                        st.then_inc(bn_ok, 1)
                        wait_alone(dve, bn_ok, 2 * m + 1, spare)
                        for t in range(GT):
                            st = dve.bn_aggr(mmv[:, t, :], mbn[:, t].rearrange("p a s -> p (a s)"))
                        st.then_inc(bn_ok, 1)
                        dve.wait_ge(bn_ok, 2 * m + 2)
                        dve.tensor_scalar(mrs[:, 0, :], mmv[:, :, 1], EPS, None, ALU.add).then_inc(ve_ok, 1)
                        dve.wait_ge(rs_ok, m + 1)
                        for t in range(GT):
                            dve.tensor_scalar(mz[:, t, 0:P], mxt[:, t, 0:P], mmv[:, t, 0:1], mrs[:, 1, t:t + 1],
                                              ALU.subtract, ALU.mult)
                            st = dve.tensor_scalar(mz[:, t, P:E], mh2[:, t, :], mmv[:, t, 0:1], mrs[:, 1, t:t + 1],
                                                   ALU.subtract, ALU.mult)
                        st.then_inc(z_ok, 1)
                        for k in range(KC):
                            dve.wait_ge(zT_done, 2 * m + k + 1)
                            dve.tensor_scalar(zT[:, k, :], ZT[k], gb_col[:, 0, k:k + 1], gb_col[:, 1, k:k + 1],
                                              ALU.mult, ALU.add).then_inc(zT_ok, 1)
                        dve.wait_ge(zhi_ok, m + 1)
                        dve.wait_ge(zT_ok, 2 * m + 2)
                        dve.tensor_tensor(zT_lo[:, :, :], zT[:, :, :], zT_hi[:, :, :].bitcast(F32),
                                          ALU.subtract).then_inc(zlo_ok, 1)
                        for f in range(FT):
                            r = FR[f]
                            dve.wait_ge(gel_ok, m * FT + f + 1)
                            if f >= 2:
                                dve.wait_ge(hlo_ok, m * FT + f - 1)
                            dve.scalar_tensor_tensor(hid[0:r, f % 2, :], A[f % 2][0:r, :], b1_col[0:r, 0, f:f + 1],
                                                     gel[0:r, f % 2, :], ALU.add, ALU.mult).then_inc(hid_ok, 1)
                        dve.wait_ge(xb_ok, m + 1)
                        for t in range(GT):
                            dve.wait_ge(w2_done, m * GT + (t | 1) + 1)
                            dve.tensor_tensor(my[:, t, :], Y[t // 2][:, (t % 2) * E:(t % 2 + 1) * E], mxt[:, t, :],
                                              ALU.add).then_inc(my_ok, 1)
                meet(dve, 2 * l + 2)
            with dve.Fori(0, B) as b:
                with dve.Fori(0, NG) as g:
                    m = b * NG + g
                    dve.wait_ge(d_fx, 16 * (m + 1))
                    dve.wait_ge(d_fy, 16 * (m + 1))
                    dve.tensor_tensor(mz[:, :, :], mz[:, :, :], mxt[:, :, :], ALU.add).then_inc(f_add, 1)
                    dve.wait_ge(f_add, m + 1)
                    for t in range(GT):
                        st = dve.bn_stats(mbn[:, t, 0, :], mz[:, t, :])
                    st.then_inc(f_bn, 1)
                    wait_alone(dve, f_bn, 2 * m + 1, spare)
                    for t in range(GT):
                        st = dve.bn_aggr(mmv[:, t, :], mbn[:, t, 0, :])
                    st.then_inc(f_bn, 1)
                    dve.wait_ge(f_bn, 2 * m + 2)
                    dve.tensor_scalar(mrs[:, 0, :], mmv[:, :, 1], EPS, None, ALU.add).then_inc(f_ag, 1)
                    dve.wait_ge(f_rs, m + 1)
                    for t in range(GT):
                        dve.tensor_scalar(my[:, t, :], mz[:, t, :], mmv[:, t, 0:1], mrs[:, 1, t:t + 1],
                                          ALU.subtract, ALU.mult).then_inc(f_ok, 1)


def build(nc, h, out):
    B, L, E = h["x"].shape
    xs = nc.dram_tensor("states", (3, LEAD + B * (L + 1) + P + 1, E), F32, kind="Internal").ap()
    causal_attention(nc, h["x"], h["w_qkv"], h["w_out"], h["ln_g"], h["ln_b"], h["b_out"], h["ident"], h["mask"], xs)
    local_layers(nc, xs, B, out, h["rot"], h["rot_scale"], h["lw_qkv"], h["lw_out"], h["ident"], h["lmask"],
                 h["ln_gb"], h["w1"], h["b1"], h["w2"], h["b2"])


def layout(v):
    import numpy as np

    p, groups, hg, d = 128, 4, 4, 16
    out = {"x": v["L0_attn_x"]}
    w = np.stack([v["L0_attn_Wq"].T, v["L0_attn_Wk"].T, v["L0_attn_Wv"].T], 1).reshape(2, p, 3, groups, hg * d)
    out["w_qkv"] = np.ascontiguousarray(w.transpose(1, 0, 3, 2, 4)).reshape(p, 2, 3, 256)
    wo = v["L0_attn_Wo"].T.reshape(groups, hg, 1, d, 256)
    wo = np.broadcast_to(wo, (groups, hg, 2, d, 256)).reshape(groups, p, 256)
    out["w_out"] = np.ascontiguousarray(wo.transpose(1, 0, 2))
    for name, a, b in (("ln_g", "gq", "gk"), ("ln_b", "bq", "bk")):
        r = np.stack([v["L0_attn_" + a], v["L0_attn_" + b]])[None, :, None, :]
        out[name] = np.ascontiguousarray(np.broadcast_to(r, (p, 2, hg, d)))
    out["b_out"] = np.ascontiguousarray(np.broadcast_to(v["L0_attn_bo"][None], (p, 256)))
    out["ident"] = np.eye(p, dtype=np.float32)
    i = np.arange(p)
    out["mask"] = np.where(i[:, None] >= i[None, :], 0.0, -1e30).astype(np.float32)
    return out


def layout_local(v):
    import numpy as np

    p, seq, window, dh, layers = 128, 1024, 128, 64, 2
    f = np.float32
    out = {}
    half_idx = np.arange(0, dh, 2, dtype=f)
    inv_freq = f(1.0) / f(10000.0) ** (half_idx / f(dh))
    t = np.arange(seq, dtype=f)
    freqs = t[:, None] * inv_freq[None, :]
    freqs = np.concatenate([freqs, freqs], -1)
    base = (half_idx + f(0.4 * dh)) / f(1.4 * dh)
    scale = base[None, :] ** ((t - seq // 2) / f(window // 2))[:, None]
    scale = np.concatenate([scale, scale], -1)
    sign = np.where(np.arange(dh) < dh // 2, -1, 1).astype(f)
    cos, sin = np.cos(freqs), np.sin(freqs) * sign
    rot = np.stack([cos * scale * f(8), sin * scale * f(8), cos / scale, sin / scale], 1).astype(f)
    out["rot"] = np.ascontiguousarray(rot.reshape(seq // p, p, 4, dh).transpose(1, 0, 2, 3))
    qs, ks = v["L0_ffn_q_scale"], v["L0_ffn_k_scale"]
    rows = np.stack([qs, np.roll(qs, dh // 2, -1), ks, np.roll(ks, dh // 2, -1)], 1)
    out["rot_scale"] = np.ascontiguousarray(np.broadcast_to(rows[:, None], (layers, p, 4, dh)))
    out["lw_qkv"] = np.ascontiguousarray(v["L0_ffn_wqkv"].reshape(layers, 2, p, -1).transpose(0, 2, 1, 3))
    out["lw_out"] = np.ascontiguousarray(v["L0_ffn_wo"].reshape(layers, 4, p, -1).transpose(0, 2, 1, 3))
    i = np.arange(p)
    own = np.where(i[:, None] >= i[None, :], 0.0, -1e30)
    prev = np.where(i[:, None] <= i[None, :], 0.0, -1e30)
    none = np.full((p, p), -1e30)
    masks = [np.stack([own, none], 1), np.stack([own, prev], 1), np.stack([prev, own], 1)]
    out["lmask"] = np.ascontiguousarray(np.stack(masks, 1).astype(f))
    hid = v["L0_ffn_w2"].shape[1]
    ft = -(-hid // p)
    gb = np.stack([v["L0_ffn_ln_g"], v["L0_ffn_ln_b"]], 1).reshape(layers, 2, 2, p)
    out["ln_gb"] = np.ascontiguousarray(gb.transpose(0, 3, 1, 2))
    out["w1"] = np.ascontiguousarray(v["L0_ffn_w1"].reshape(layers, 2, p, -1).transpose(0, 2, 1, 3))
    b1 = np.zeros((layers, 2, ft * p), f)
    b1[:, :, :hid] = v["L0_ffn_b1"].reshape(layers, 2, hid)
    out["b1"] = np.ascontiguousarray(b1.reshape(layers, 2, ft, p).transpose(0, 3, 1, 2))
    w2 = np.zeros((layers, ft * p, 256), f)
    w2[:, :hid] = v["L0_ffn_w2"]
    out["w2"] = np.ascontiguousarray(w2.reshape(layers, ft, p, 256).transpose(0, 2, 1, 3))
    out["b2"] = np.ascontiguousarray(np.broadcast_to(v["L0_ffn_b2"][:, None], (layers, p, 256)))
    return out


def kernel(**inputs):
    import numpy as np
    import concourse.bacc as bacc
    from concourse.bass_utils import run_bass_kernel_spmd

    v = {k: np.asarray(a) for k, a in inputs.items()}
    a = {**layout(v), **layout_local(v)}
    nc = bacc.Bacc("TRN2", target_bir_lowering=False, num_devices=1)
    h = {k: nc.dram_tensor(k, t.shape, F32, kind="ExternalInput").ap() for k, t in a.items()}
    B, L, E = a["x"].shape
    out = nc.dram_tensor("out", (B, L, E), F32, kind="ExternalOutput").ap()
    build(nc, h, out)
    r = run_bass_kernel_spmd(nc, [a], core_ids=[0])
    return r.results[0]["out"]
```

```python
from contextlib import ExitStack

import concourse.bass as bass
from concourse import mybir

F32 = mybir.dt.float32
F32R = mybir.dt.float32r
BF16 = mybir.dt.bfloat16
ALU = mybir.AluOpType
ACT = mybir.ActivationFunctionType
AX = mybir.AxisListType

P = 128
BANK = 512
EPS = 1e-5
LEAD = 1024 + P
TAIL = 8 * P + 1


def wait_alone(eng, sem, value, spare):
    eng.wait_ge(sem, value)
    eng.sem_inc(spare, 1)


def causal_attention(nc, x, w_qkv, w_out, ln_g, ln_b, b_out, ident_in, mask_in, x_mid):
    B, L, E = x.shape[0] - 1, x.shape[1], x.shape[2]
    TILES = L // P
    KC = E // P
    D = 16
    GROUPS = 4
    HG = 4
    QW = HG * D
    GW = 3 * QW
    M = TILES * HG
    CH = BANK // P
    CHUNKS = TILES // CH
    PARTS = 3
    SR = PARTS * D
    STACK = 64
    VW = 32
    NP = 4
    LAG = 2
    PAIRS = TILES // 2

    pieces = [(j, i, k0, min(k0 + BANK, (i + 1) * P), i if k0 == 0 else TILES - CH + i)
              for j in range(HG) for i in range(TILES) for k0 in range(0, (i + 1) * P, BANK)]
    units = [(j, c, kt, max(0, kt - c * CH) * P) for c in range(CHUNKS) for j in range(HG) for kt in range((c + 1) * CH)]
    first_of = [0, HG * CH]
    NS = 3
    R = len(units)
    assert len(pieces) == R
    with ExitStack() as ctx:
        def sb(name, shape, dt=F32):
            return ctx.enter_context(nc.sbuf_tensor(name, shape, dt))

        def ps(name, shape, dt=F32):
            return ctx.enter_context(nc.psum_tensor(name, shape, dt))

        def sem(name):
            return ctx.enter_context(nc.semaphore("a_" + name))

        ident = sb("a_ident", [P, P])
        ident_b = sb("a_ident_b", [P, P], BF16)
        mask_f = sb("a_mask_f", [P, 2, P])
        mask_b = sb("a_mask_b", [P, 2, P], BF16)
        g_row = sb("a_g_row", [P, 2, HG, D])
        b_row = sb("a_b_row", [P, 2, HG, D])
        bo_row = sb("a_bo_row", [P, E])
        w_hi = sb("a_w_hi", [P, KC, GROUPS, GW], F32R)
        w_lo = sb("a_w_lo", [P, KC, GROUPS, GW], F32R)
        wo_hi = sb("a_wo_hi", [P, KC, E], F32R)
        wo_lo = sb("a_wo_lo", [P, KC, E], F32R)
        half = sb("a_half", [P, 2 * M])
        xb = sb("a_xb", [P, TILES, E])
        xr = sb("a_xr", [P, TILES, E])
        xT_hi = sb("a_xT_hi", [P, KC, L], F32R)
        xT_lo = sb("a_xT_lo", [P, KC, L], F32R)
        qk = sb("a_qk", [P, 2, M, D])
        qkc = sb("a_qkc", [P, 2, M, D])
        qk_sq = sb("a_qk_sq", [P, 2, M, D])
        st = sb("a_st", [P, 3, 2 * M])
        part = [sb(f"a_part_q{i}", [P, M, STACK], F32R) for i in range(2)]
        part_k = sb("a_part_k", [P, M, STACK], F32R)
        qT = sb("a_qT", [P, 2, L], F32R)
        qmT = sb("a_qmT", [P, 2, L], F32R)
        kT = [sb(f"a_kT{i}", [P, 2, L], F32R) for i in range(2)]
        vals = sb("a_vals", [P, GROUPS, TILES, HG, VW])
        pm = sb("a_pm", [P, HG, 2 * TILES - CH])
        pT = sb("a_pT", [P, NP, BANK])
        ot = sb("a_ot", [P, CHUNKS, BANK])
        inv = sb("a_inv", [P, CHUNKS, M // CHUNKS])
        on = sb("a_on", [P, TILES, E])
        oT_hi = sb("a_oT_hi", [P, KC, P], F32R)
        oT_lo = sb("a_oT_lo", [P, KC, P], F32R)
        bn = sb("a_bn", [P, TILES, 6])
        mv = sb("a_mv", [P, TILES, 2])
        rstd = sb("a_rstd", [P, 2, TILES])
        zrow = sb("a_zrow", [P, E])
        stage = xb

        X = [ps(f"a_X{i}", [P, BANK]) for i in range(2)]
        S = [ps(f"a_S{i}", [P, BANK]) for i in range(NS)]
        ST = [ps(f"a_ST{i}", [P, BANK]) for i in range(2)]
        O = ps("a_O", [P, BANK])
        Z = (X[0], X[1], S[0], S[1])

        def out_at(c):
            return ST[c][:, :].rearrange("p (i h v) -> p i h v", i=CH, h=HG)

        d_const = sem("d_const")
        d_w = [sem(f"d_w{i}") for i in range(KC + 1)]
        d_x, d_r, d_y = sem("d_x"), sem("d_r"), sem("d_y")
        d_z = [sem(f"d_z{s}") for s in range(3)]
        w_ready = sem("w_ready")
        zeros_ok = sem("zeros_ok")
        xT_done, xT_hi_ok, xT_lo_ok = sem("xT_done"), sem("xT_hi_ok"), sem("xT_lo_ok")
        qkv_done, qkv_ok = sem("qkv_done"), sem("qkv_ok")
        sum_ok, cen_ok, sq_ok, gain_ok = sem("sum_ok"), sem("cen_ok"), sem("sq_ok"), sem("gain_ok")
        sumsq_ok, var_ok, rstd_ok, scaled_ok, norm_ok = (sem("sumsq_ok"), sem("var_ok"), sem("rstd_ok"),
                                                         sem("scaled_ok"), sem("norm_ok"))
        part_hi, part_lo = sem("part_hi"), sem("part_lo")
        pt_done, pt_act, pt_dve = sem("pt_done"), sem("pt_act"), sem("pt_dve")
        s_done, max_ok = sem("s_done"), sem("max_ok")
        both_ok, mh_ok, ml_ok = sem("both_ok"), sem("mh_ok"), sem("ml_ok")
        mt_done, mt_act, mt_dve = sem("mt_done"), sem("mt_act"), sem("mt_dve")
        st_done, exp_ok, pv_done = sem("st_done"), sem("exp_ok"), sem("pv_done")
        ot_ok, on_done, inv_ok, o_ok = sem("ot_ok"), sem("on_done"), sem("inv_ok"), sem("o_ok")
        oT_done, oT_hi_ok, oT_lo_ok, wo_done = sem("oT_done"), sem("oT_hi_ok"), sem("oT_lo_ok"), sem("wo_done")
        bias_ok, res_ok, bn_ok, agg_ok = sem("bias_ok"), sem("res_ok"), sem("bn_ok"), sem("agg_ok")
        veps_ok, yr_ok, y_ok = sem("veps_ok"), sem("yr_ok"), sem("y_ok")
        spare = sem("spare")

        XT_AT = (0, 1, 2, 3)
        PROJ_AT = (5, 8, 11, 14)
        TURN_AT = [17 + 3 * i for i in range(TILES)]
        PARTS_AT = 45
        OUT_AT = [r + 2 for r in TURN_AT]

        block = ctx.enter_context(nc.Block())

        @block.sync
        def _(sp):
            for dst, src in ([
                    (ident[:, :], ident_in), (mask_f[:, :, :], mask_in),
                    (g_row[:, :, :, :], ln_g), (b_row[:, :, :, :], ln_b), (bo_row[:, :], b_out)]):
                sp.dma_start(dst, src).then_inc(d_const, 16)
            for k in range(KC):
                sp.dma_start(stage[:, 4 * k:4 * k + 3, :], w_qkv[:, k]).then_inc(d_w[k], 16)
            sp.dma_start(xr[:, :, :], x[0].rearrange("(t p) e -> p t e", p=P)).then_inc(d_r, 16)
            sp.wait_ge(w_ready, 2 * KC)
            sp.dma_start(stage[:, 0:KC, :], w_out).then_inc(d_w[KC], 16)
            sp.wait_ge(zeros_ok, 1)
            for s in range(3):
                end = LEAD + B * (L + 1)
                sp.dma_start(x_mid[s, LEAD:end, :].rearrange("(b r) e -> b r e", b=B)[:, 0, :],
                             zrow[0:B, :]).then_inc(d_z[s], 16)
                sp.dma_start(x_mid[s, end:end + TAIL - 1, :].rearrange("(t p) e -> p t e", p=P),
                             zrow[:, :].unsqueeze(1).broadcast_to([P, (TAIL - 1) // P, E])).then_inc(d_z[s], 16)
                sp.dma_start(x_mid[s, end + TAIL - 1:end + TAIL, :], zrow[0:1, :]).then_inc(d_z[s], 16)
            sp.wait_ge(w_ready, 2 * KC + 2)
            sp.dma_start(xb[:, :, :], x[0].rearrange("(t p) e -> p t e", p=P)).then_inc(d_x, 16)
            with sp.Fori(0, B) as b:
                sp.wait_ge(xT_done, (b + 1) * PAIRS)
                sp.dma_start(xb[:, :, :], x[b + 1].rearrange("(t p) e -> p t e", p=P)).then_inc(d_x, 16)
                sp.wait_ge(y_ok, (b + 1) * TILES)
                sp.dma_start(x_mid[0, bass.ds(LEAD - L + b * (L + 1), L), :].rearrange("(t p) e -> p t e", p=P),
                             xr[:, :, :]).then_inc(d_y, 16)
                sp.wait_ge(d_y, (b + 1) * 16)
                sp.dma_start(xr[:, :, :], x[b].rearrange("(t p) e -> p t e", p=P)).then_inc(d_r, 16)
            sp.wait_ge(y_ok, (B + 1) * TILES)
            sp.dma_start(x_mid[0, LEAD + B * (L + 1) - L:LEAD + B * (L + 1), :].rearrange("(t p) e -> p t e", p=P),
                         xr[:, :, :]).then_inc(d_y, 16)
            sp.wait_ge(d_y, (B + 1) * 16)
            for s in range(3):
                sp.wait_ge(d_z[s], 3 * 16)

        @block.gpsimd
        def _(pool):
            pool.memset(zrow[:, :], 0.0).then_inc(zeros_ok, 1)
            for t in (part[0][:, :, :], part[1][:, :, :], part_k[:, :, :], qmT[:, :, :], kT[1][:, :, :]):
                pool.memset(t.bitcast(F32), 0.0).then_inc(zeros_ok, 1)
            pool.memset(on[:, :, :], 0.0).then_inc(zeros_ok, 1)
            pool.memset(half[:, :], -0.5).then_inc(zeros_ok, 1)
            pool.memset(vals[:, :, :, :, 0:D], 0.0).then_inc(zeros_ok, 1)
            pool.memset(vals[:, :, :, :, D:D + 1], 1.0).then_inc(zeros_ok, 1)
            pool.memset(vals[:, :, :, :, D + 1:VW], 0.0).then_inc(zeros_ok, 1)
            pool.wait_ge(zeros_ok, 11)
            pool.memset(part_k[:, :, SR:SR + 2].bitcast(F32), 1.0).then_inc(zeros_ok, 1)
            pool.wait_ge(zeros_ok, 12)
            pool.wait_ge(d_const, 5 * 16)

            def front(f):
                pool.wait_ge(cen_ok, 2 * f + 2)
                pool.tensor_tensor(qk_sq[:, :, :, :], qkc[:, :, :, :], qkc[:, :, :, :], ALU.mult).then_inc(sq_ok, 1)
                for s in range(2):
                    g = pool.tensor_tensor(
                        qk[:, s].rearrange("p (t h) d -> p t (h d)", h=HG),
                        qkc[:, s].rearrange("p (t h) d -> p t (h d)", h=HG),
                        g_row[:, s].rearrange("p h d -> p (h d)").unsqueeze(1).broadcast_to([P, TILES, QW]), ALU.mult)
                g.then_inc(gain_ok, 1)
                pool.wait_ge(var_ok, f + 1)
                pool.tensor_tensor(st[:, 2, :], st[:, 1, :], half[:, :], ALU.pow).then_inc(rstd_ok, 1)
                pool.wait_ge(scaled_ok, 2 * f + 2)
                for s in range(2):
                    t = pool.tensor_tensor(
                        qkc[:, s].rearrange("p (t h) d -> p t (h d)", h=HG),
                        qk[:, s].rearrange("p (t h) d -> p t (h d)", h=HG),
                        b_row[:, s].rearrange("p h d -> p (h d)").unsqueeze(1).broadcast_to([P, TILES, QW]), ALU.add)
                t.then_inc(norm_ok, 1)

            def finish_bias(b):
                pool.wait_ge(d_r, (b + 1) * 16)
                pool.tensor_tensor(xr[:, :, :], xr[:, :, :], bo_row[:, :].unsqueeze(1).broadcast_to([P, TILES, E]),
                                   ALU.add).then_inc(bias_ok, 1)

            def finish_root(b):
                pool.wait_ge(veps_ok, b + 1)
                pool.tensor_tensor(rstd[:, 1, :], rstd[:, 0, :], half[:, 0:TILES], ALU.pow).then_inc(yr_ok, 1)

            front(0)
            with pool.Fori(0, B) as b:
                for g in range(GROUPS):
                    if g == 1:
                        finish_bias(b)
                    front(b * GROUPS + g + 1)
                    if g == 1:
                        finish_root(b)
            finish_bias(B)
            finish_root(B)

        @block.tensor
        def _(pe):
            pe.wait_ge(w_ready, 2 * KC + 4)
            pe.wait_ge(zeros_ok, 12)

            def turn_x(b, m):
                if m == 0:
                    pe.wait_ge(d_x, (b + 1) * 16)
                if m >= 2:
                    pe.wait_ge(xT_lo_ok, b * PAIRS + m - 1)
                for k in range(KC):
                    for i in range(2):
                        t = pe.transpose(X[m % 2][:, (2 * k + i) * P:(2 * k + i + 1) * P],
                                         xb[:, 2 * m + i, k * P:(k + 1) * P], ident[:, :])
                t.then_inc(xT_done, 1)

            def project(f, g, m, b):
                pe.wait_ge(xT_lo_ok, (b + 1) * PAIRS)
                if m >= 2:
                    pe.wait_ge(qkv_ok, f * PAIRS + m - 1)
                for i in range(2):
                    ops = [(a, w, k) for k in range(KC) for a, w in ((xT_hi, w_hi), (xT_lo, w_hi), (xT_hi, w_lo))]
                    for z, (a, w, k) in enumerate(ops):
                        mm = pe.matmul(X[m % 2][:, i * GW:(i + 1) * GW], a[:, k, (2 * m + i) * P:(2 * m + i + 1) * P],
                                       w[:, k, g, :], start=(z == 0), stop=(z == len(ops) - 1))
                mm.then_inc(qkv_done, 1)

            def turn_stack(f, z, slot):
                s, p, c = z // 4, z // 2 % 2, z % 2
                if z == 0:
                    pe.wait_ge(part_lo, 2 * f + 2)
                if z >= 4:
                    pe.wait_ge((pt_act, pt_dve)[z % 2], f * 4 + (z - 4) // 2 + 1)
                src = (part[slot], part_k)[s]
                for ii in range(CH):
                    m = (c * CH + ii) * HG + 2 * p
                    t = pe.transpose(Z[z % 4][:, ii * P:(ii + 1) * P],
                                     src[:, m:m + 2, :].rearrange("p m r -> p (m r)").bitcast(F32), ident[:, :])
                t.then_inc(pt_done, 1)

            def turn_max(n, f, z, slot):
                p, c = z // 2, z % 2
                if z == 0:
                    pe.wait_ge(ml_ok, n + 1)
                pe.wait_ge((pt_act, pt_dve)[z % 2], f * 4 + 3 + z // 2)
                for ii in range(CH):
                    m = (c * CH + ii) * HG + 2 * p
                    t = pe.transpose(Z[z][:, ii * P:(ii + 1) * P],
                                     part[slot][:, m:m + 2, :].rearrange("p m r -> p (m r)").bitcast(F32), ident[:, :])
                t.then_inc(mt_done, 1)

            def scores(n, r, slot):
                j, i, k0, k1, _ = pieces[r]
                a, p = STACK * (j % 2), j // 2
                if r >= NS:
                    pe.wait_ge(max_ok, n * R + r - NS + 1)
                diagonal = k1 == (i + 1) * P
                mm = pe.matmul(S[r % NS][:, 0:k1 - k0], qT[a:a + SR, p, i * P:(i + 1) * P],
                               kT[slot][a:a + SR, p, k0:k1], start=True, stop=not diagonal)
                if diagonal:
                    mm = pe.matmul(S[r % NS][:, k1 - k0 - P:k1 - k0], ident_b[:, :], mask_b[:, 0, :],
                                   start=False, stop=True)
                mm.then_inc(s_done, 1)

            def scores_t(e, r, slot):
                j, c, kt, q0 = units[r]
                a, p = STACK * (j % 2), j // 2
                if r >= 2:
                    pe.wait_ge(exp_ok, e * R + r - 1)
                else:
                    pe.wait_ge(o_ok, 2 * e + r + 1)
                diagonal = kt >= c * CH
                mm = pe.matmul(ST[r % 2][:, q0:BANK], kT[slot][a:a + STACK, p, kt * P:(kt + 1) * P],
                               qmT[a:a + STACK, p, c * BANK + q0:(c + 1) * BANK], start=True, stop=not diagonal)
                if diagonal:
                    mm = pe.matmul(ST[r % 2][:, q0:q0 + P], ident_b[:, :], mask_b[:, 1, :], start=False, stop=True)
                mm.then_inc(st_done, 1)

            def values(e, r, g):
                j, c, kt, q0 = units[r]
                if r in first_of:
                    pe.wait_ge(ot_ok, 2 * e + c + 2)
                pe.wait_ge(exp_ok, e * R + r + 1)
                pe.matmul(O[VW * j:VW * (j + 1), q0:BANK], vals[:, g, kt, j, :], pT[:, r % NP, q0:BANK],
                          start=(kt == 0), stop=(kt == (c + 1) * CH - 1)).then_inc(pv_done, 1)

            def turn_out(e, c):
                pe.wait_ge(ot_ok, 2 * e + c + 3)
                for ii in range(CH):
                    t = pe.transpose(ST[c][:, ii * P:(ii + 1) * P], ot[:, c, ii * P:(ii + 1) * P], ident[:, :])
                t.then_inc(on_done, 1)

            def finish_turn(b, i):
                if i == 0:
                    pe.wait_ge(o_ok, 2 * (b * GROUPS + 1) + 2)
                else:
                    pe.wait_ge(oT_lo_ok, b * TILES + i)
                for k in range(KC):
                    t = pe.transpose(X[0][:, k * P:(k + 1) * P], on[:, i, k * P:(k + 1) * P], ident[:, :])
                t.then_inc(oT_done, 1)

            def finish_out(b, i):
                pe.wait_ge(oT_lo_ok, b * TILES + i + 1)
                if i:
                    pe.wait_ge(res_ok, b * TILES + i)
                ops = [(a, w, k) for k in range(KC) for a, w in ((oT_hi, wo_hi), (oT_lo, wo_hi), (oT_hi, wo_lo))]
                for z, (a, w, k) in enumerate(ops):
                    mm = pe.matmul(X[1][:, 0:E], a[:, k, :], w[:, k, :], start=(z == 0), stop=(z == len(ops) - 1))
                mm.then_inc(wo_done, 1)

            for m in range(PAIRS):
                turn_x(0, m)
            for m in range(PAIRS):
                project(0, 0, m, 0)
            for z in range(8):
                turn_stack(0, z, 0)
            with pe.Fori(0, B) as b:
                for g in range(GROUPS):
                    n = b * GROUPS + g
                    pe.wait_ge(pt_act, 4 * n + 4)
                    pe.wait_ge(pt_dve, 4 * n + 4)
                    pe.wait_ge(mt_act, 2 * n + 1)
                    pe.wait_ge(mt_dve, 2 * n + 1)
                    last = g == GROUPS - 1
                    for r in range(R):
                        if last and r in XT_AT:
                            turn_x(b + 1, XT_AT.index(r))
                        if r in PROJ_AT:
                            project(n + 1, (g + 1) % GROUPS, PROJ_AT.index(r), b + 1 if last else b)
                        if g == 1 and r in TURN_AT:
                            if r == TURN_AT[0]:
                                pe.wait_ge(qkv_ok, (n + 2) * PAIRS)
                            finish_turn(b, TURN_AT.index(r))
                        if g == 1 and r in OUT_AT:
                            finish_out(b, OUT_AT.index(r))
                        scores(n, r, g % 2)
                        scores_t(n, r, (g + 1) % 2)
                        if r >= LAG:
                            values(n, r - LAG, (g - 1) % GROUPS)
                    if g == 1:
                        pe.wait_ge(oT_lo_ok, (b + 1) * TILES)
                        pe.wait_ge(res_ok, (b + 1) * TILES)
                    for z in range(12):
                        if z in (0, 4):
                            values(n, R - LAG + z // 4, (g - 1) % GROUPS)
                        if z == 6:
                            for c in range(CHUNKS):
                                turn_out(n, c)
                        if z == 2:
                            pe.wait_ge(max_ok, (n + 1) * R)
                        if z < 8:
                            turn_stack(n + 1, z, (g + 1) % 2)
                        else:
                            turn_max(n, n + 1, z - 8, g % 2)
            n = B * GROUPS
            pe.wait_ge(mt_act, 2 * n + 1)
            pe.wait_ge(mt_dve, 2 * n + 1)
            for r in range(R):
                scores_t(n, r, 1)
                if r >= LAG:
                    values(n, r - LAG, GROUPS - 1)
            for r in range(R - LAG, R):
                values(n, r, GROUPS - 1)
            for c in range(CHUNKS):
                turn_out(n, c)
            for i in range(TILES):
                finish_turn(B, i)
                finish_out(B, i)

        @block.scalar
        def _(act):
            def x_hi(b, m):
                act.wait_ge(xT_done, b * PAIRS + m + 1)
                act.activation(xT_hi[:, :, 2 * m * P:(2 * m + 2) * P], X[m % 2][:, :].rearrange("p (k n) -> p k n", k=KC),
                               ACT.Copy).then_inc(xT_hi_ok, 1)

            def taken(f, g, m):
                act.wait_ge(qkv_done, f * PAIRS + m + 1)
                src = X[m % 2][:, 0:2 * GW].rearrange("p (i s n) -> p s i n", i=2, s=3)
                for s in range(2):
                    act.activation(qk[:, s, 2 * m * HG:(2 * m + 2) * HG, :].rearrange("p (i h) d -> p i (h d)", i=2),
                                   src[:, s], ACT.Copy)
                for i in range(2):
                    t = act.activation(vals[:, g, 2 * m + i, :, 0:D], src[:, 2, i].rearrange("p (h d) -> p h d", h=HG),
                                       ACT.Copy)
                t.then_inc(qkv_ok, 1)

            def parts_hi(f, slot):
                act.wait_ge(norm_ok, f + 1)
                for s, (dst, at) in enumerate(((part[slot], slice(0, 2)), (part_k, slice(0, 3, 2)))):
                    act.activation(dst[:, :, 0:SR].rearrange("p m (r d) -> p m r d", d=D)[:, :, at, :],
                                   qkc[:, s].unsqueeze(2).broadcast_to([P, M, 2, D]), ACT.Copy).then_inc(part_hi, 1)

            def stack(f, z, slot):
                s, p, c = z // 4, z // 2 % 2, z % 2
                act.wait_ge(pt_done, f * 8 + z + 1)
                act.activation((qT, kT[slot])[s][:, p, c * BANK:(c + 1) * BANK], Z[z % 4][:, :], ACT.Copy).then_inc(pt_act, 1)

            def stack_max(n, z):
                p, c = z // 2, z % 2
                act.wait_ge(mt_done, n * 4 + z + 1)
                act.activation(qmT[:, p, c * BANK:(c + 1) * BANK], Z[z][:, :], ACT.Copy).then_inc(mt_act, 1)

            def expo(e, r):
                q0 = units[r][3]
                if r >= NP:
                    act.wait_ge(pv_done, e * R + r - NP + 1)
                act.wait_ge(st_done, e * R + r + 1)
                act.activation(pT[:, r % NP, q0:BANK], ST[r % 2][:, q0:BANK], ACT.Exp).then_inc(exp_ok, 1)

            def out_taken(e, c):
                act.wait_ge(pv_done, e * R + (R if c else first_of[1]))
                act.activation(ot[:, c, :], O[:, :], ACT.Copy).then_inc(ot_ok, 1)

            def finish_hi(b, i):
                act.wait_ge(oT_done, b * TILES + i + 1)
                act.activation(oT_hi[:, :, :].rearrange("p k n -> p (k n)"), X[0][:, 0:E], ACT.Copy).then_inc(oT_hi_ok, 1)

            act.wait_ge(zeros_ok, 12)
            act.nop().then_inc(mt_act, 1)
            act.nop().then_inc(ot_ok, 2)
            for m in range(PAIRS):
                x_hi(0, m)
            for m in range(PAIRS):
                taken(0, 0, m)
            parts_hi(0, 0)
            for z in range(0, 8, 2):
                stack(0, z, 0)
            with act.Fori(0, B) as b:
                for g in range(GROUPS):
                    n = b * GROUPS + g
                    last = g == GROUPS - 1
                    for r in range(R):
                        if last and r in XT_AT:
                            x_hi(b + 1, XT_AT.index(r))
                        expo(n, r)
                        if r in PROJ_AT:
                            taken(n + 1, (g + 1) % GROUPS, PROJ_AT.index(r))
                        if g == 1 and r in TURN_AT:
                            finish_hi(b, TURN_AT.index(r))
                        if r == PARTS_AT:
                            parts_hi(n + 1, (g + 1) % 2)
                        if r == first_of[1] + LAG:
                            out_taken(n, 0)
                    for z in range(0, 8, 2):
                        stack(n + 1, z, (g + 1) % 2)
                        if z == 2:
                            out_taken(n, 1)
                    for z in range(0, 4, 2):
                        stack_max(n, z)
            for r in range(R):
                expo(B * GROUPS, r)
                if r == first_of[1] + LAG:
                    out_taken(B * GROUPS, 0)
            out_taken(B * GROUPS, 1)
            for i in range(TILES):
                finish_hi(B, i)

        @block.vector
        def _(dve):
            dve.wait_ge(d_const, 5 * 16)
            for k in range(KC):
                dve.wait_ge(d_w[k], 16)
                src = stage[:, 4 * k:4 * k + 3, :].rearrange("p a e -> p (a e)")
                wh, wl = (w[:, k].rearrange("p g n -> p (g n)") for w in (w_hi, w_lo))
                dve.tensor_copy(wh, src).then_inc(w_ready, 1)
                dve.wait_ge(w_ready, 2 * k + 1)
                dve.tensor_tensor(wl, src, wh.bitcast(F32), ALU.subtract).then_inc(w_ready, 1)
            dve.wait_ge(d_w[KC], 16)
            dve.tensor_copy(wo_hi[:, :, :], stage[:, 0:KC, :]).then_inc(w_ready, 1)
            dve.wait_ge(w_ready, 2 * KC + 1)
            dve.tensor_tensor(wo_lo[:, :, :], stage[:, 0:KC, :], wo_hi[:, :, :].bitcast(F32),
                              ALU.subtract).then_inc(w_ready, 1)
            dve.tensor_copy(ident_b[:, :], ident[:, :]).then_inc(w_ready, 1)
            dve.tensor_copy(mask_b[:, :, :], mask_f[:, :, :]).then_inc(w_ready, 1)
            dve.wait_ge(zeros_ok, 12)
            dve.nop().then_inc(mt_dve, 1)
            dve.nop().then_inc(o_ok, 2)

            def x_lo(b, m):
                dve.wait_ge(xT_hi_ok, b * PAIRS + m + 1)
                dst = slice(2 * m * P, (2 * m + 2) * P)
                dve.tensor_tensor(xT_lo[:, :, dst], X[m % 2][:, :].rearrange("p (k n) -> p k n", k=KC),
                                  xT_hi[:, :, dst].bitcast(F32), ALU.subtract).then_inc(xT_lo_ok, 1)

            def norm_sum(f, s):
                dve.wait_ge(qkv_ok, (f + 1) * PAIRS)
                dve.tensor_reduce(st[:, 0, s * M:(s + 1) * M], qk[:, s], AX.X, ALU.add).then_inc(sum_ok, 1)

            def norm_centre(f, s):
                dve.wait_ge(sum_ok, 2 * f + s + 1)
                dve.scalar_tensor_tensor(qkc[:, s], st[:, 0, s * M:(s + 1) * M].unsqueeze(2).broadcast_to([P, M, D]),
                                         -1.0 / D, qk[:, s], ALU.mult, ALU.add).then_inc(cen_ok, 1)

            def norm_squares(f, s):
                dve.wait_ge(sq_ok, f + 1)
                dve.tensor_reduce(st[:, 0, s * M:(s + 1) * M], qk_sq[:, s], AX.X, ALU.add).then_inc(sumsq_ok, 1)

            def norm_variance(f, s):
                dve.wait_ge(sumsq_ok, 2 * f + 2)
                dve.tensor_scalar(st[:, 1, :], st[:, 0, :], 1.0 / D, EPS, ALU.mult, ALU.add).then_inc(var_ok, 1)

            def norm_scale(f, s):
                dve.wait_ge(rstd_ok, f + 1)
                dve.wait_ge(gain_ok, f + 1)
                dve.tensor_tensor(qk[:, s], qk[:, s], st[:, 2, s * M:(s + 1) * M].unsqueeze(2).broadcast_to([P, M, D]),
                                  ALU.mult).then_inc(scaled_ok, 1)

            def parts_lo(f, slot):
                for s, (dst, hi, lo) in enumerate(((part[slot], 0, 2), (part_k, 0, 1))):
                    dve.wait_ge(part_hi, 2 * f + s + 1)
                    rows = dst[:, :, 0:SR].rearrange("p m (r d) -> p m r d", d=D)
                    dve.tensor_tensor(rows[:, :, lo, :], qkc[:, s], rows[:, :, hi, :].bitcast(F32),
                                      ALU.subtract).then_inc(part_lo, 1)

            def stack(f, z, slot):
                s, p, c = z // 4, z // 2 % 2, z % 2
                dve.wait_ge(pt_done, f * 8 + z + 1)
                dve.tensor_copy((qT, kT[slot])[s][:, p, c * BANK:(c + 1) * BANK], Z[z % 4][:, :]).then_inc(pt_dve, 1)

            def stack_max(n, z):
                p, c = z // 2, z % 2
                dve.wait_ge(mt_done, n * 4 + z + 1)
                dve.tensor_copy(qmT[:, p, c * BANK:(c + 1) * BANK], Z[z][:, :]).then_inc(mt_dve, 1)

            def maximum(n, r):
                j, i, k0, k1, at = pieces[r]
                dve.wait_ge(s_done, n * R + r + 1)
                dve.tensor_reduce(pm[:, j, at:at + 1], S[r % NS][:, 0:k1 - k0], AX.X, ALU.max,
                                  negate=True).then_inc(max_ok, 1)

            def join_maxima(n, slot):
                dve.wait_ge(max_ok, (n + 1) * R)
                dve.tensor_tensor(pm[:, :, CH:TILES], pm[:, :, CH:TILES], pm[:, :, TILES:TILES + CH],
                                  ALU.min).then_inc(both_ok, 1)
                dst = part[slot][:, :, :].rearrange("p (i j) r -> p j i r", j=HG)
                dve.wait_ge(both_ok, n + 1)
                dve.tensor_copy(dst[:, :, :, SR], pm[:, :, 0:TILES]).then_inc(mh_ok, 1)
                dve.wait_ge(mh_ok, n + 1)
                dve.tensor_tensor(dst[:, :, :, SR + 1], pm[:, :, 0:TILES], dst[:, :, :, SR].bitcast(F32),
                                  ALU.subtract).then_inc(ml_ok, 1)

            def normalise(e, c, g):
                dve.wait_ge(on_done, 2 * e + c + 1)
                o = out_at(c)
                i = inv[:, c, :].rearrange("p (i h) -> p i h", h=HG)
                dve.reciprocal(i, o[:, :, :, D]).then_inc(inv_ok, 1)
                dve.wait_ge(inv_ok, 2 * e + c + 1)
                dve.tensor_tensor(on[:, c * CH:(c + 1) * CH, g * QW:(g + 1) * QW].rearrange("p i (h d) -> p i h d", h=HG),
                                  o[:, :, :, 0:D], i.unsqueeze(3).broadcast_to([P, CH, HG, D]), ALU.mult).then_inc(o_ok, 1)

            def finish_lo(b, i):
                dve.wait_ge(oT_hi_ok, b * TILES + i + 1)
                dve.tensor_tensor(oT_lo[:, :, :].rearrange("p k n -> p (k n)"), X[0][:, 0:E],
                                  oT_hi[:, :, :].rearrange("p k n -> p (k n)").bitcast(F32),
                                  ALU.subtract).then_inc(oT_lo_ok, 1)

            def residual(b, i):
                if i == 0:
                    dve.wait_ge(bias_ok, b + 1)
                dve.wait_ge(wo_done, b * TILES + i + 1)
                dve.tensor_tensor(xr[:, i, :], X[1][:, 0:E], xr[:, i, :], ALU.add).then_inc(res_ok, 1)

            def statistics(b, i):
                dve.wait_ge(res_ok, b * TILES + i + 1)
                dve.bn_stats(bn[:, i, :], xr[:, i, :]).then_inc(bn_ok, 1)

            def variance(b):
                wait_alone(dve, bn_ok, (b + 1) * TILES, spare)
                for i in range(TILES):
                    a = dve.bn_aggr(mv[:, i, :], bn[:, i, :])
                a.then_inc(agg_ok, 1)
                dve.wait_ge(agg_ok, b + 1)
                dve.tensor_scalar(rstd[:, 0, :], mv[:, :, 1], EPS, None, ALU.add).then_inc(veps_ok, 1)

            def scale(b):
                dve.wait_ge(yr_ok, b + 1)
                for i in range(TILES):
                    dve.tensor_scalar(xr[:, i, :], xr[:, i, :], mv[:, i, 0:1], rstd[:, 1, i:i + 1],
                                      ALU.subtract, ALU.mult).then_inc(y_ok, 1)

            for m in range(PAIRS):
                x_lo(0, m)
            norm_at = {17: (norm_sum, 0), 18: (norm_sum, 1), 19: (norm_centre, 0), 20: (norm_centre, 1),
                       26: (norm_squares, 0), 27: (norm_squares, 1), 28: (norm_variance, 0),
                       41: (norm_scale, 0), 42: (norm_scale, 1)}
            for step, s in norm_at.values():
                step(0, s)
            parts_lo(0, 0)
            for z in range(1, 8, 2):
                stack(0, z, 0)
            with dve.Fori(0, B) as b:
                for g in range(GROUPS):
                    n = b * GROUPS + g
                    last = g == GROUPS - 1
                    for r in range(R):
                        if last and r in XT_AT:
                            x_lo(b + 1, XT_AT.index(r))
                        maximum(n, r)
                        if r in norm_at:
                            norm_at[r][0](n + 1, norm_at[r][1])
                        if g == 1 and r in TURN_AT:
                            finish_lo(b, TURN_AT.index(r))
                        if g == 1 and r in OUT_AT:
                            residual(b, OUT_AT.index(r))
                        if g == 1 and r - 1 in OUT_AT:
                            statistics(b, OUT_AT.index(r - 1))
                        if r == PARTS_AT + 1:
                            parts_lo(n + 1, (g + 1) % 2)
                    join_maxima(n, g % 2)
                    if g == 1:
                        variance(b)
                    for z in range(1, 8, 2):
                        stack(n + 1, z, (g + 1) % 2)
                        if z == 5:
                            for c in range(CHUNKS):
                                normalise(n, c, (g - 1) % GROUPS)
                    for z in range(1, 4, 2):
                        stack_max(n, z)
                    if g == 1:
                        scale(b)
            for c in range(CHUNKS):
                normalise(B * GROUPS, c, GROUPS - 1)
            for i in range(TILES):
                finish_lo(B, i)
                residual(B, i)
            for i in range(TILES):
                statistics(B, i)
            variance(B)
            scale(B)


def local_layers(nc, xs, B, out, rot, rot_scale, w_qkv, w_out, ident_in, mask_in, ln_gb, w1, b1, w2, b2):
    LAYERS = 2
    L, E = out.shape[1], out.shape[2]
    H, D = 8, 64
    W = H * D
    KC = E // P
    OC = W // P
    TILES = L // P
    U = 4
    TURNS = TILES // U
    assert TURNS == 2
    TL = B * TILES
    NQ = B * TURNS
    HH = H // 2
    HID = w1.shape[3] // 2
    FT = -(-HID // P)
    FR = [min(P, HID - f * P) for f in range(FT)]
    GT = 4
    NG = L // P // GT
    assert NG == 2
    NGL = B * NG

    with ExitStack() as ctx:
        def keep(name, shape, dt):
            return ctx.enter_context(nc.sbuf_tensor(name, shape, dt))

        def ps(name, shape, dt=F32):
            return ctx.enter_context(nc.psum_tensor(name, shape, dt))

        def sem(name):
            return ctx.enter_context(nc.semaphore(name))

        ident = keep("l_ident", [P, P], F32)
        ident_b = keep("l_ident_b", [P, P], BF16)
        mask_f = keep("l_mask_f", [P, 3, 2, P], F32)
        mask_b = keep("l_mask_b", [P, 3, 2, P], BF16)
        rot_sb = keep("l_rot", [P, TILES, 4, D], F32)
        rsc = keep("l_rsc", [P, 4, D], F32)
        tab = keep("l_tab", [P, TILES, 4, D], F32)
        wq_hi = keep("l_wq_hi", [P, KC, 3 * W], F32R)
        wq_lo = keep("l_wq_lo", [P, KC, 3 * W], F32R)
        wo_hi = keep("l_wo_hi", [P, OC, E], F32R)
        wo_lo = keep("l_wo_lo", [P, OC, E], F32R)
        stage = keep("l_stage", [P, 2, max(2 * HID, FT * E)], F32)
        w1_hi = keep("l_w1_hi", [P, KC, 2 * HID], F32R)
        w1_lo = keep("l_w1_lo", [P, KC, 2 * HID], F32R)
        w2_hi = keep("l_w2_hi", [P, FT, E], F32R)
        w2_lo = keep("l_w2_lo", [P, FT, E], F32R)
        b2_row = keep("l_b2", [P, E], F32)
        b1_col = keep("l_b1", [P, 2, FT], F32)
        gb_col = keep("l_gb", [P, 2, KC], F32)
        half = keep("l_half", [P, 2 * H], F32)

        k_hi = keep("l_k_hi", [P, H, 2, P], F32R)
        k_lo = keep("l_k_lo", [P, H, 2, P], F32R)
        vs = keep("l_v", [P, 2, H, 2, D], F32R)
        F = [ps(f"l_F{i}", [P, BANK]) for i in range(3)]
        S = ps("l_S", [P, HH, 2 * P])
        T = ps("l_T", [P, 2, BANK])
        O = ps("l_O", [P, BANK])

        d_c = [sem(f"l_d_c{i}") for i in range(9)]
        const_ok = sem("l_const_ok")
        split = sem("l_split")
        phase = sem("l_phase")
        spare = sem("l_spare")

        place = ExitStack()
        xt = keep("l_xt", [P, U, E], F32)
        osb = keep("l_osb", [P, H, D], F32)

        def sb(name, shape, dt):
            return place.enter_context(nc.sbuf_tensor(name, shape, dt))

        h2 = sb("l_h2", [P, U, P], F32)
        hT_hi = sb("l_hT_hi", [P, KC, P], F32R)
        hT_lo = sb("l_hT_lo", [P, KC, P], F32R)
        kc = sb("l_kc", [P, W], F32)
        sq = sb("l_sq", [P, 2 * H, D], F32)
        ss = sb("l_ss", [P, 2, 2 * H], F32)
        rn = sb("l_rn", [P, 2, 2 * H], F32)
        ta = sb("l_ta", [P, 2, H, D], F32)
        tb = sb("l_tb", [P, 2, H, D], F32)
        qd = sb("l_qd", [P, 2, H, 2, D], F32)
        q_st = sb("l_q_st", [P, H, P], F32R)
        mx = sb("l_mx", [P, 4, H], F32)
        prob = sb("l_prob", [P, H, 2, P], F32)
        pT_hi = sb("l_pT_hi", [P, 2, HH, 2, P], F32R)
        pT_lo = sb("l_pT_lo", [P, 2, HH, 2, P], F32R)
        oT_hi = sb("l_oT_hi", [P, OC, P], F32R)
        oT_lo = sb("l_oT_lo", [P, OC, P], F32R)
        yb = sb("l_yb", [P, 2, E], F32)
        ol = sb("l_ol", [P, 2, HH, D], F32)
        ob = sb("l_ob", [P, 2, HH, D], F32)

        d_x = [sem(f"l_d_x{i}") for i in range(U)]
        d_h = [sem(f"l_d_h{i}") for i in range(U)]
        d_y = [sem(f"l_d_y{i}") for i in range(2)]
        hT_done = sem("l_hT_done")
        hT_hi_ok = sem("l_hT_hi_ok")
        hT_lo_ok = sem("l_hT_lo_ok")
        proj_done = [sem(f"l_{n}_done") for n in "qkv"]
        kc_ok = sem("l_kc_ok")
        sq_ok = [sem(f"l_{n}_sq_ok") for n in "qk"]
        sum_ok = [sem(f"l_{n}_sum_ok") for n in "qk"]
        ss_ok = [sem(f"l_{n}_ss_ok") for n in "qk"]
        rn_ok = [sem(f"l_{n}_rn_ok") for n in "qk"]
        vhi_ok = sem("l_vhi_ok")
        vlo_ok = sem("l_vlo_ok")
        q_terms = sem("l_q_terms")
        q_first = sem("l_q_first")
        qr_ok = sem("l_qr_ok")
        k_terms = sem("l_k_terms")
        k_rot = sem("l_k_rot")
        k_first = sem("l_k_first")
        kr_ok = sem("l_kr_ok")
        qkT_done = sem("l_qkT_done")
        st_hi_ok = sem("l_st_hi_ok")
        st_lo_ok = sem("l_st_lo_ok")
        s_done = sem("l_s_done")
        m_ok = sem("l_m_ok")
        mx_ok = sem("l_mx_ok")
        exp_ok = sem("l_exp_ok")
        ri_ok = sem("l_ri_ok")
        pT_done = sem("l_pT_done")
        pT_hi_ok = sem("l_pT_hi_ok")
        pT_lo_ok = sem("l_pT_lo_ok")
        pv_done = sem("l_pv_done")
        ol_ok = sem("l_ol_ok")
        both_ok = sem("l_both_ok")
        osb_ok = sem("l_osb_ok")
        oT_done = sem("l_oT_done")
        oT_hi_ok = sem("l_oT_hi_ok")
        oT_lo_ok = sem("l_oT_lo_ok")
        wo_done = sem("l_wo_done")
        y_ok = sem("l_y_ok")
        gch = sem("l_gch")
        FZ = (F[0], F[1], F[2], F[1])
        FP = (F[1], F[2], F[0])

        place.close()

        mx2 = sb("m_x", [P, 2, GT, E], F32)
        mh2 = sb("m_h2", [P, 2, GT, P], F32)
        mz = sb("m_z", [P, GT, E], F32)
        mbn = sb("m_bn", [P, GT, 2, 6], F32)
        mmv = sb("m_mv", [P, GT, 2], F32)
        mrs = sb("m_rs", [P, 2, GT], F32)
        zT = sb("m_zT", [P, KC, GT * P], F32)
        zT_hi = sb("m_zT_hi", [P, KC, GT * P], F32R)
        zT_lo = sb("m_zT_lo", [P, KC, GT * P], F32R)
        gel = sb("m_gel", [P, 2, BANK], F32)
        hid = sb("m_hid", [P, 2, BANK], F32)
        hid_hi = sb("m_hid_hi", [P, FT, BANK], F32R)
        hid_lo = sb("m_hid_lo", [P, FT, BANK], F32R)
        my = sb("m_y", [P, GT, E], F32)
        A = [F[0], T[:, 0, :]]
        G = [F[1], T[:, 1, :]]
        ZT = [F[0], F[1]]
        s_flat = S[:, :, :].rearrange("p h n -> p (h n)")
        Y = [F[2], O, s_flat[:, 0:BANK], s_flat[:, BANK:2 * BANK]]
        place.close()
        d_mx, d_my = [sem(f"m_d_x{i}") for i in range(2)], sem("m_d_y")
        bn_ok = sem("m_bn_ok")
        ve_ok = sem("m_ve_ok")
        rs_ok = sem("m_rs_ok")
        z_ok = sem("m_z_ok")
        zT_done = sem("m_zT_done")
        zT_ok = sem("m_zT_ok")
        zhi_ok = sem("m_zhi_ok")
        zlo_ok = sem("m_zlo_ok")
        ag_done = sem("m_ag_done")
        gel_ok = sem("m_gel_ok")
        hid_ok = sem("m_hid_ok")
        hhi_ok = sem("m_hhi_ok")
        hlo_ok = sem("m_hlo_ok")
        w2_done = sem("m_w2_done")
        xb_ok = sem("m_xb_ok")
        my_ok = sem("m_y_ok")

        fx, fy, fs, fo = (sb(f"f_{n}", [P, 2, GT, E], F32) for n in "xyso")
        fbn = sb("f_bns", [P, 2, GT, 6], F32)
        fmv = sb("f_mv", [P, 2, GT, 2], F32)
        frs = sb("f_rstd", [P, 2, 2, GT], F32)
        place.close()
        d_f = [sem(f"f_d_x{i}") for i in range(2)]
        d_fo = [sem(f"f_d_o{i}") for i in range(2)]
        f_add, f_bn, f_ag, f_rs, f_ok = (sem(f"f_{n}") for n in ("add", "bn", "ag", "rs", "ok"))

        ENGINES = 5

        def meet(eng, k):
            eng.drain().then_inc(phase, 1)
            wait_alone(eng, phase, ENGINES * k, spare)

        def next_tile(q, u):
            return bass.ds(q * U + u + 1, 1) if u < U - 1 else bass.ds(U - q * U, 1)

        block = ctx.enter_context(nc.Block())

        @block.sync
        def _(sp):
            for n, (dst, src) in enumerate([(ident[:, :], ident_in), (mask_f[:, :, :, :], mask_in),
                                            (rot_sb[:, :, :, :], rot)]):
                sp.dma_start(dst, src).then_inc(d_c[n], 16)
            with sp.Fori(0, LAYERS) as l:
                SPLITS = 2 * (2 * KC + KC + 2)
                parts = ([w_qkv[l, :, k, a * 3 * W // 2:(a + 1) * 3 * W // 2] for k in range(KC) for a in range(2)]
                         + [w1[l, :, k, :] for k in range(KC)] + [w_out[l], w2[l]])
                small = [(rsc[:, :, :], rot_scale[l]), (gb_col[:, :, :], ln_gb[l]), (b1_col[:, :, :], b1[l]),
                         (b2_row[:, :], b2[l])]
                for n, (dst, src) in enumerate(small):
                    sp.dma_start(dst, src).then_inc(d_c[3 + n], 16)
                for n, src in enumerate(parts):
                    if n >= 2:
                        sp.wait_ge(split, l * SPLITS + 2 * (n - 1))
                    src = src if len(src.shape) == 2 else src.rearrange("p a b -> p (a b)")
                    sp.dma_start(stage[:, n % 2, 0:src.shape[1]], src).then_inc(d_c[7 + n % 2], 16)

                def load(r, v):
                    sp.dma_start(xt[:, v, :], xs[l, bass.ds(r + 1, P), :]).then_inc(d_x[v], 16)
                    sp.dma_start(h2[:, v, :], xs[l, bass.ds(r, P), P:E]).then_inc(d_h[v], 16)

                def store(r, c, v):
                    sp.wait_ge(y_ok, c + 2)
                    sp.dma_start(xs[2, bass.ds(r + 1, P), :], yb[:, v, :]).then_inc(d_y[v], 16)

                load(LEAD, 0)
                with sp.Fori(0, B) as b:
                    with sp.Fori(0, TURNS) as q:
                        m = (l * B + b) * TURNS + q
                        row = LEAD + b * (L + 1) + q * (U * P)
                        for u in range(U):
                            load(row + ((u + 1) * P if u < U - 1 else U * P + q), (u + 1) % U)
                            store(row + (u - 1) * P if u else row + q - (P + 1), U * m + l + u, u % 2)
                store(LEAD + B * (L + 1) - 1 - P, (l + 1) * TL + l, 0)
                wait_alone(sp, d_y[0], (l + 1) * (TL // 2 + 1) * 16 + 1, spare)
                wait_alone(sp, d_y[1], (l + 1) * (TL // 2) * 16 + 1, spare)
                meet(sp, 2 * l + 1)

                def mload(r, v):
                    sp.dma_start(mx2[:, v], xs[2, bass.ds(r + 1, GT * P), :].rearrange(
                        "(t p) e -> p t e", p=P)).then_inc(d_mx[v], 16)
                    sp.dma_start(mh2[:, v], xs[2, bass.ds(r, GT * P), P:E].rearrange(
                        "(t p) e -> p t e", p=P)).then_inc(d_mx[v], 16)

                mload(LEAD, 0)
                with sp.Fori(0, B) as b:
                    for g in range(NG):
                        m = (l * B + b) * NG + g
                        r = LEAD + b * (L + 1) + g * (GT * P)
                        mload(r + GT * P + (1 if g == NG - 1 else 0), (g + 1) % 2)
                        sp.wait_ge(my_ok, GT * (m + 1) + 1)
                        sp.dma_start(xs[1, bass.ds(r + 1, GT * P), :].rearrange("(t p) e -> p t e", p=P),
                                     my[:, :, :]).then_inc(d_my, 16)
                        wait_alone(sp, d_my, 16 * (m + 1), spare)
                meet(sp, 2 * l + 2)

            def fload(r, v):
                sp.dma_start(fx[:, v], xs[0, bass.ds(r + 1, GT * P), :].rearrange(
                    "(p t) e -> p t e", p=P)).then_inc(d_f[v], 16)

            for g in range(NG):
                fload(LEAD + g * (GT * P), g)
            with sp.Fori(0, B) as b:
                for g in range(NG):
                    wait_alone(sp, f_add, b * NG + g + 1, spare)
                    fload(LEAD + (b + 1) * (L + 1) + g * (GT * P), g)
            for g in range(NG):
                sp.wait_ge(d_f[g], 32 * (B + 1))
            for g in range(NG):
                sp.wait_ge(d_fo[g], 16 * B + 1)

        @block.gpsimd
        def _(pool):
            pool.memset(half[:, :], -0.5).then_inc(gch, 1)
            for t in (k_hi, k_lo):
                pool.memset(t[:, :, 1, :].bitcast(F32), 0.0).then_inc(const_ok, 1)
            pool.memset(vs[:, 1].bitcast(F32), 0.0).then_inc(const_ok, 1)
            pool.memset(xt[:, :, :], 0.0).then_inc(const_ok, 1)
            pool.memset(osb[:, :, :], 0.0).then_inc(const_ok, 1)
            pool.wait_ge(gch, 1)
            with pool.Fori(0, LAYERS) as l:

                def front(f, tile, v):
                    wait_alone(pool, kc_ok, f + 1, spare)
                    k3 = kc[:, :].rearrange("p (h d) -> p h d", h=H)

                    def row(z, a, c):
                        return tab[:, tile, z, a:c].broadcast_to([P, H, c - a])
                    pool.tensor_tensor(ta[:, 1], k3, row(2, 0, D), ALU.mult)
                    pool.tensor_tensor(tb[:, 1, :, 0:D // 2], k3[:, :, D // 2:D], row(3, 0, D // 2), ALU.mult)
                    pool.tensor_tensor(tb[:, 1, :, D // 2:D], k3[:, :, 0:D // 2], row(3, D // 2, D),
                                       ALU.mult).then_inc(k_terms, 1)
                    pool.wait_ge(k_terms, f + 1)
                    pool.tensor_tensor(ta[:, 1], ta[:, 1], tb[:, 1], ALU.add).then_inc(k_rot, 1)
                    pool.wait_ge(ss_ok[1], f + 1)
                    pool.tensor_tensor(rn[:, v, H:2 * H], ss[:, 1, H:2 * H], half[:, 0:H], ALU.pow).then_inc(rn_ok[1], 1)
                    pool.wait_ge(rn_ok[1], f + 1)
                    pool.wait_ge(k_rot, f + 1)
                    pool.tensor_tensor(qd[:, 1, :, 0, :], ta[:, 1],
                                       rn[:, v, H:2 * H].unsqueeze(2).broadcast_to([P, H, D]),
                                       ALU.mult).then_inc(k_first, 1)
                    pool.wait_ge(ss_ok[0], f + 1)
                    pool.tensor_tensor(rn[:, v, 0:H], ss[:, 1, 0:H], half[:, 0:H], ALU.pow).then_inc(rn_ok[0], 1)

                front(l * (TL + 1), slice(0, 1), 0)
                with pool.Fori(0, B) as b:
                    with pool.Fori(0, TURNS) as q:
                        m = (l * B + b) * TURNS + q
                        for u in range(U):
                            front(U * m + l + u + 1, next_tile(q, u), (u + 1) % 2)
                meet(pool, 2 * l + 1)

                def root(f):
                    pool.wait_ge(ve_ok, f + 1)
                    pool.tensor_tensor(mrs[:, 1, :], mrs[:, 0, :], half[:, 0:GT], ALU.pow).then_inc(rs_ok, 1)

                def bias(f, v):
                    pool.wait_ge(z_ok, f + 1)
                    pool.tensor_tensor(mx2[:, v], mx2[:, v], b2_row[:, :].unsqueeze(1).broadcast_to([P, GT, E]),
                                       ALU.add).then_inc(xb_ok, 1)

                def hidden_lo(m, k):
                    pool.wait_ge(hhi_ok, m * FT + k + 1)
                    pool.tensor_tensor(hid_lo[0:FR[k], k, :], hid[0:FR[k], k % 2, :],
                                       hid_hi[0:FR[k], k, :].bitcast(F32), ALU.subtract).then_inc(hlo_ok, 1)

                root(l * (NGL + 1))
                bias(l * (NGL + 1), 0)
                with pool.Fori(0, B) as b:
                    for g in range(NG):
                        m = (l * B + b) * NG + g
                        for k in range(FT):
                            hidden_lo(m, k)
                            if k == 2:
                                root(m + l + 1)
                            if k == 4:
                                bias(m + l + 1, (g + 1) % 2)
                meet(pool, 2 * l + 2)

            def froot(k, v):
                pool.wait_ge(f_ag, k + 1)
                pool.tensor_tensor(frs[:, v, 1, :], frs[:, v, 0, :], half[:, 0:GT], ALU.pow).then_inc(f_rs, 1)

            froot(0, 0)
            with pool.Fori(0, B) as b:
                for g in range(NG):
                    froot(b * NG + g + 1, (g + 1) % 2)

        @block.tensor
        def _(pe):
            pe.wait_ge(const_ok, 5 + 2)
            with pe.Fori(0, LAYERS) as l:
                wait_alone(pe, split, (l + 1) * 2 * (3 * KC + 2), spare)

                def turn_x(f, v, loads):
                    pe.wait_ge(d_x[v], 16 * loads)
                    pe.wait_ge(d_h[v], 16 * loads)
                    pe.transpose(T[:, 1, 0:P], xt[:, v, 0:P], ident[:, :])
                    pe.transpose(T[:, 1, P:2 * P], h2[:, v, :], ident[:, :]).then_inc(hT_done, 1)

                def project(f, s):
                    if s == 1:
                        pe.wait_ge(hT_lo_ok, f + 1)
                    elif s == 0:
                        pe.wait_ge(st_lo_ok, 4 * f + 1)
                    else:
                        pe.wait_ge(st_lo_ok, 4 * f + 2)
                    ops = [(a, w, k) for k in range(KC) for a, w in ((hT_hi, wq_hi), (hT_lo, wq_hi), (hT_hi, wq_lo))]
                    for z, (a, w, k) in enumerate(ops):
                        mm = pe.matmul(FP[s][:, :], a[:, k, :], w[:, k, s * W:(s + 1) * W],
                                       start=(z == 0), stop=(z == len(ops) - 1))
                    mm.then_inc(proj_done[s], 1)

                def stack(f, z):
                    s, hf = z // 2, z % 2
                    if z == 0:
                        pe.wait_ge(qr_ok, f + 1)
                        pe.wait_ge(vlo_ok, f + 1)
                    elif z == 1:
                        pe.wait_ge(sq_ok[0], f + 1)
                    elif z == 2:
                        pe.wait_ge(kr_ok, f + 1)
                        pe.wait_ge(sq_ok[1], f + 1)
                    else:
                        pe.wait_ge(st_lo_ok, 4 * f + 3)
                    for h in range(HH):
                        tr = pe.transpose(FZ[z][:, h * P:(h + 1) * P],
                                          qd[:, s, hf * HH + h, :, :].rearrange("p a d -> p (a d)"), ident[:, :])
                    tr.then_inc(qkT_done, 1)

                def scores(t, f, hf, mk):
                    pe.wait_ge(st_lo_ok, 4 * f + 4 + hf)
                    if hf:
                        pe.wait_ge(exp_ok, 4 * t + 2)
                    for h in range(HH):
                        hh = hf * HH + h
                        for z, kk in enumerate((k_hi, k_lo)):
                            pe.matmul(S[:, h, :], q_st[:, hh, :], kk[:, hh].rearrange("p a n -> p (a n)"),
                                      start=(z == 0), stop=False)
                        mm = pe.matmul(S[:, h, :], ident_b[:, :], mk.rearrange("p o a n -> p (o a n)"),
                                       start=False, stop=True)
                    mm.then_inc(s_done, 1)

                def turn_p(t, hf, c):
                    pe.wait_ge(exp_ok, 4 * t + 2 * hf + c + 1)
                    for z in range(4):
                        h, s = 2 * c + z // 2, z % 2
                        tr = pe.transpose(T[:, c, z * P:(z + 1) * P], prob[:, hf * HH + h, s, :], ident[:, :])
                    tr.then_inc(pT_done, 1)

                def mix(t, f, hf):
                    if hf == 0:
                        pe.wait_ge(y_ok, f + 2)
                        pe.wait_ge(vlo_ok, f + 2)
                    else:
                        pe.wait_ge(both_ok, 2 * t + 1)
                    for h in range(HH):
                        if h % 2 == 0:
                            pe.wait_ge(pT_lo_ok, 4 * t + 2 * hf + h // 2 + 1)
                        hh = hf * HH + h
                        ops = ((pT_hi, 2, 0), (pT_lo, 1, 0), (pT_lo, 1, 1), (pT_hi, 2, 1))
                        for z, (a, n, s) in enumerate(ops):
                            mm = pe.matmul(O[:, 2 * h * D:(2 * h + n) * D], a[:, hf, h, s, :],
                                           vs[:, s, hh, 0:n, :].rearrange("p a d -> p (a d)"),
                                           start=(z == 0), stop=(z == len(ops) - 1))
                    mm.then_inc(pv_done, 1)

                def turn_o(t):
                    pe.wait_ge(osb_ok, t + 1)
                    for k in range(OC):
                        tr = pe.transpose(T[:, 0, k * P:(k + 1) * P],
                                          osb[:, 2 * k:2 * k + 2, :].rearrange("p a d -> p (a d)"), ident[:, :])
                    tr.then_inc(oT_done, 1)

                def project_out(c):
                    pe.wait_ge(oT_lo_ok, c + 1)
                    ops = [(a, w, k) for k in range(OC) for a, w in ((oT_hi, wo_hi), (oT_lo, wo_hi), (oT_hi, wo_lo))]
                    for z, (a, w, k) in enumerate(ops):
                        mm = pe.matmul(O[:, 0:E], a[:, k, :], w[:, k, :], start=(z == 0), stop=(z == len(ops) - 1))
                    mm.then_inc(wo_done, 1)

                f = l * (TL + 1)
                turn_x(f, 0, l * (NQ + 1) + 1)
                for s in (1, 0):
                    project(f, s)
                for z in range(4):
                    stack(f, z)
                project(f, 2)
                with pe.Fori(0, B) as b:
                    with pe.Fori(0, TURNS) as q:
                        m = (l * B + b) * TURNS + q
                        for u in range(U):
                            t, f = U * m + u, U * m + l + u
                            turn_x(f + 1, (u + 1) % U, m + 1 if u < U - 1 else m + l + 2)
                            scores(t, f, 0, mask_b[:, bass.ds(q, 1)] if u == 0 else
                                   mask_b[:, 1:2] if u % 2 == 0 else mask_b[:, 2:3])
                            turn_o(t)
                            project(f + 1, 1)
                            project(f + 1, 0)
                            project_out(f)
                            turn_p(t, 0, 0)
                            turn_p(t, 0, 1)
                            scores(t, f, 1, mask_b[:, bass.ds(q, 1)] if u == 0 else
                                   mask_b[:, 1:2] if u % 2 == 0 else mask_b[:, 2:3])
                            stack(f + 1, 0)
                            stack(f + 1, 1)
                            mix(t, f, 0)
                            turn_p(t, 1, 0)
                            project(f + 1, 2)
                            turn_p(t, 1, 1)
                            stack(f + 1, 2)
                            stack(f + 1, 3)
                            mix(t, f, 1)
                turn_o((l + 1) * TL)
                project_out((l + 1) * TL + l)
                meet(pe, 2 * l + 1)

                def turn_z(f):
                    pe.wait_ge(z_ok, f + 1)
                    for k in range(KC):
                        for t in range(GT):
                            tr = pe.transpose(ZT[k][:, t * P:(t + 1) * P], mz[:, t, k * P:(k + 1) * P], ident[:, :])
                        tr.then_inc(zT_done, 1)

                def widen(m, f, k):
                    r = FR[k]
                    if k == 0:
                        pe.wait_ge(zlo_ok, 2 * f + 2)
                    if k >= 2:
                        pe.wait_ge(hid_ok, m * FT + k - 1)
                    for dst, off in ((A[k % 2], 0), (G[k % 2], HID)):
                        ops = [(w, a, c) for c in range(KC) for w, a in
                               ((w1_hi, zT_hi), (w1_lo, zT_hi), (w1_hi, zT_lo))]
                        for z, (w, a, c) in enumerate(ops):
                            mm = pe.matmul(dst[0:r, :], w[:, c, off + k * P:off + k * P + r], a[:, c, :],
                                           start=(z == 0), stop=(z == len(ops) - 1))
                    mm.then_inc(ag_done, 1)

                def narrow(m, k):
                    if k == 0:
                        pe.wait_ge(my_ok, GT * m + 1)
                    pe.wait_ge(hlo_ok, m * FT + k + 1)
                    for t in range(GT):
                        for z, (a, w) in enumerate(((hid_hi, w2_hi), (hid_lo, w2_hi), (hid_hi, w2_lo))):
                            mm = pe.matmul(Y[t][:, 0:E], a[0:FR[k], k, t * P:(t + 1) * P], w[0:FR[k], k, :],
                                           start=(k == 0 and z == 0), stop=(k == FT - 1 and z == 2))
                        if k == FT - 1:
                            mm.then_inc(w2_done, 1)

                turn_z(l * (NGL + 1))
                with pe.Fori(0, B) as b:
                    for g in range(NG):
                        m = (l * B + b) * NG + g
                        for k in range(FT):
                            widen(m, m + l, k)
                            if k >= 2:
                                narrow(m, k - 2)
                        pe.wait_ge(hid_ok, m * FT + FT - 1)
                        turn_z(m + l + 1)
                        narrow(m, FT - 2)
                        narrow(m, FT - 1)
                meet(pe, 2 * l + 2)

        @block.scalar
        def _(act):
            with act.Fori(0, LAYERS) as l:

                def x_hi(f):
                    act.wait_ge(hT_done, f + 1)
                    act.activation(hT_hi[:, :, :].rearrange("p k n -> p (k n)"), T[:, 1, 0:2 * P],
                                   ACT.Copy).then_inc(hT_hi_ok, 1)

                def o_hi(c):
                    act.wait_ge(oT_done, c + 1)
                    act.activation(oT_hi[:, :, :].rearrange("p k n -> p (k n)"), T[:, 0, :],
                                   ACT.Copy).then_inc(oT_hi_ok, 1)

                def copy_k(f):
                    act.wait_ge(proj_done[1], f + 1)
                    act.activation(kc[:, :], FP[1][:, :], ACT.Copy).then_inc(kc_ok, 1)

                def second(f, s):
                    act.wait_ge((q_first, k_first)[s], f + 1)
                    act.activation(qd[:, s, :, 1, :], qd[:, s, :, 0, :], ACT.Copy).then_inc((qr_ok, kr_ok)[s], 1)

                def square(f, s):
                    if s:
                        act.wait_ge(proj_done[1], f + 1)
                    else:
                        act.wait_ge(q_terms, f + 1)
                    act.activation(sq[:, s * H:(s + 1) * H, :].rearrange("p h d -> p (h d)"), FP[s][:, :],
                                   ACT.Square).then_inc(sq_ok[s], 1)

                def expo(t, hf, v, c):
                    if c == 0:
                        act.wait_ge(mx_ok, 2 * t + hf + 1)
                    for hh in (hf * HH + 2 * c, hf * HH + 2 * c + 1):
                        e = act.activation(prob[:, hh].rearrange("p a n -> p (a n)"), S[:, hh % HH, :], ACT.Exp,
                                           bias=mx[:, 1, hh:hh + 1], scale=rn[:, v, hh:hh + 1],
                                           accum_out=mx[:, 2, hh:hh + 1])
                        if hh % 2:
                            e.then_inc(exp_ok, 1)

                def p_hi(t, hf, c):
                    act.wait_ge(pT_done, 4 * t + 2 * hf + c + 1)
                    act.activation(pT_hi[:, hf, 2 * c:2 * c + 2].rearrange("p h s n -> p (h s n)"),
                                   T[:, c, :], ACT.Copy).then_inc(pT_hi_ok, 1)

                def out_lo(t, hf):
                    act.wait_ge(pv_done, 2 * t + hf + 1)
                    act.activation(ol[:, hf], O[:, :].rearrange("p (h a d) -> p h a d", h=HH, a=2)[:, :, 1, :],
                                   ACT.Copy).then_inc(ol_ok, 1)

                def stack_hi(f, z, v):
                    s, hf = z // 2, z % 2
                    act.wait_ge(qkT_done, 4 * f + z + 1)
                    hs = slice(hf * HH, (hf + 1) * HH)
                    act.activation(q_st[:, hs, :] if s == 0 else k_hi[:, hs, v, :],
                                   FZ[z][:, :].rearrange("p (h n) -> p h n", h=HH), ACT.Copy).then_inc(st_hi_ok, 1)

                def values_hi(f, v):
                    act.wait_ge(proj_done[2], f + 1)
                    act.activation(vs[:, v, :, 0, :], F[0][:, :].rearrange("p (h d) -> p h d", h=H), ACT.Copy).then_inc(vhi_ok, 1)

                f = l * (TL + 1)
                x_hi(f)
                copy_k(f)
                for s in (1, 0):
                    square(f, s)
                for z in range(4):
                    if z % 2 == 0:
                        second(f, z // 2)
                    stack_hi(f, z, 0)
                with act.Fori(0, B) as b:
                    with act.Fori(0, TURNS) as q:
                        m = (l * B + b) * TURNS + q
                        for u in range(U):
                            t, f, v = U * m + u, U * m + l + u, (u + 1) % 2
                            x_hi(f + 1)
                            values_hi(f, u % 2)
                            o_hi(f)
                            copy_k(f + 1)
                            expo(t, 0, u % 2, 0)
                            expo(t, 0, u % 2, 1)
                            square(f + 1, 1)
                            square(f + 1, 0)
                            second(f + 1, 0)
                            p_hi(t, 0, 0)
                            p_hi(t, 0, 1)
                            stack_hi(f + 1, 0, v)
                            stack_hi(f + 1, 1, v)
                            expo(t, 1, u % 2, 0)
                            out_lo(t, 0)
                            expo(t, 1, u % 2, 1)
                            second(f + 1, 1)
                            p_hi(t, 1, 0)
                            p_hi(t, 1, 1)
                            stack_hi(f + 1, 2, v)
                            stack_hi(f + 1, 3, v)
                            out_lo(t, 1)
                o_hi((l + 1) * TL + l)
                values_hi((l + 1) * TL + l, 0)
                meet(act, 2 * l + 1)

                def z_hi(f):
                    for k in range(KC):
                        act.wait_ge(zT_ok, 2 * f + k + 1)
                        act.activation(zT_hi[:, k, :], zT[:, k, :], ACT.Copy).then_inc(zhi_ok, 1)

                z_hi(l * (NGL + 1))
                with act.Fori(0, B) as b:
                    for g in range(NG):
                        m = (l * B + b) * NG + g
                        for k in range(FT):
                            r = FR[k]
                            act.wait_ge(ag_done, m * FT + k + 1)
                            act.activation(gel[0:r, k % 2, :], G[k % 2][0:r, :], ACT.Gelu,
                                           bias=b1_col[0:r, 1, k:k + 1]).then_inc(gel_ok, 1)
                            act.wait_ge(hid_ok, m * FT + k + 1)
                            act.activation(hid_hi[0:r, k, :], hid[0:r, k % 2, :], ACT.Copy).then_inc(hhi_ok, 1)
                        z_hi(m + l + 1)
                meet(act, 2 * l + 2)

            def fload(r, v):
                act.dma_start(fy[:, v], xs[1, bass.ds(r + 1, GT * P), :].rearrange(
                    "(p t) e -> p t e", p=P)).then_inc(d_f[v], 16)

            for g in range(NG):
                fload(LEAD + g * (GT * P), g)
            with act.Fori(0, B) as b:
                for g in range(NG):
                    act.wait_ge(f_add, b * NG + g + 1)
                    fload(LEAD + (b + 1) * (L + 1) + g * (GT * P), g)
                    act.wait_ge(f_ok, GT * (b * NG + g + 1) + 1)
                    act.dma_start(out[b, g * GT * P:(g + 1) * GT * P, :].rearrange("(p t) e -> p t e", p=P),
                                  fo[:, g]).then_inc(d_fo[g], 16)

        @block.vector
        def _(dve):
            dve.wait_ge(d_c[0], 16)
            dve.tensor_copy(ident_b[:, :], ident[:, :]).then_inc(const_ok, 1)
            dve.wait_ge(d_c[1], 16)
            dve.tensor_copy(mask_b[:, :, :, :], mask_f[:, :, :, :]).then_inc(const_ok, 1)
            dve.wait_ge(d_c[2], 16)
            dve.wait_ge(const_ok, 5 + 2)
            for c in (y_ok, osb_ok, vlo_ok, st_lo_ok, d_y[0], d_y[1], my_ok, d_fo[0], d_fo[1], f_ok):
                dve.nop().then_inc(c, 1)
            with dve.Fori(0, LAYERS) as l:
                SPLITS = 2 * (3 * KC + 2)
                for n in range(4):
                    dve.wait_ge(d_c[3 + n], 16 * (l + 1))
                dve.tensor_tensor(tab[:, :, :, :].rearrange("p t z d -> p t (z d)"),
                                  rot_sb[:, :, :, :].rearrange("p t z d -> p t (z d)"),
                                  rsc[:, :, :].rearrange("p z d -> p (z d)").unsqueeze(1).broadcast_to(
                                      [P, TILES, 4 * D]), ALU.mult)
                HW = 3 * W // 2
                dsts = ([(wq_hi[:, k, a * HW:(a + 1) * HW], wq_lo[:, k, a * HW:(a + 1) * HW])
                         for k in range(KC) for a in range(2)]
                        + [(w1_hi[:, k, :], w1_lo[:, k, :]) for k in range(KC)]
                        + [(wo_hi[:, :, :].rearrange("p a b -> p (a b)"), wo_lo[:, :, :].rearrange("p a b -> p (a b)")),
                           (w2_hi[:, :, :].rearrange("p a b -> p (a b)"), w2_lo[:, :, :].rearrange("p a b -> p (a b)"))])
                for n, (hi, lo) in enumerate(dsts):
                    dve.wait_ge(d_c[7 + n % 2], 16 * (l * len(dsts) // 2 + n // 2 + 1))
                    w = hi.shape[1]
                    dve.tensor_copy(hi, stage[:, n % 2, 0:w]).then_inc(split, 1)
                    dve.wait_ge(split, l * SPLITS + 2 * n + 1)
                    dve.tensor_tensor(lo, stage[:, n % 2, 0:w], hi.bitcast(F32), ALU.subtract).then_inc(split, 1)
                wait_alone(dve, split, (l + 1) * SPLITS, spare)

                def x_lo(f):
                    dve.wait_ge(hT_hi_ok, f + 1)
                    dve.tensor_tensor(hT_lo[:, :, :].rearrange("p k n -> p (k n)"), T[:, 1, 0:2 * P],
                                      hT_hi[:, :, :].rearrange("p k n -> p (k n)").bitcast(F32),
                                      ALU.subtract).then_inc(hT_lo_ok, 1)

                def o_lo(c):
                    dve.wait_ge(oT_hi_ok, c + 1)
                    dve.tensor_tensor(oT_lo[:, :, :].rearrange("p k n -> p (k n)"), T[:, 0, :],
                                      oT_hi[:, :, :].rearrange("p k n -> p (k n)").bitcast(F32),
                                      ALU.subtract).then_inc(oT_lo_ok, 1)

                def residual(c, v, w, stores):
                    dve.wait_ge(wo_done, c + 1)
                    dve.wait_ge(d_y[w], 16 * stores + 1)
                    dve.tensor_tensor(yb[:, w, :], O[:, 0:E], xt[:, v, :], ALU.add).then_inc(y_ok, 1)

                def norms(f, s):
                    hs = slice(s * H, (s + 1) * H)
                    dve.wait_ge(sq_ok[s], f + 1)
                    dve.tensor_reduce(ss[:, 0, hs], sq[:, hs, :], AX.X, ALU.add).then_inc(sum_ok[s], 1)
                    dve.wait_ge(sum_ok[s], f + 1)
                    dve.tensor_scalar(ss[:, 1, hs], ss[:, 0, hs], 1e-24, None, ALU.max).then_inc(ss_ok[s], 1)

                def rotate_q(f, tile):
                    wait_alone(dve, proj_done[0], f + 1, spare)
                    q3 = F[1][:, :].rearrange("p (h d) -> p h d", h=H)

                    def row(z, a, c):
                        return tab[:, tile, z, a:c].broadcast_to([P, H, c - a])
                    dve.tensor_tensor(ta[:, 0], q3, row(0, 0, D), ALU.mult)
                    dve.tensor_tensor(tb[:, 0, :, 0:D // 2], q3[:, :, D // 2:D], row(1, 0, D // 2), ALU.mult)
                    dve.tensor_tensor(tb[:, 0, :, D // 2:D], q3[:, :, 0:D // 2], row(1, D // 2, D),
                                      ALU.mult).then_inc(q_terms, 1)
                    dve.wait_ge(q_terms, f + 1)
                    dve.tensor_tensor(qd[:, 0, :, 0, :], ta[:, 0], tb[:, 0], ALU.add).then_inc(q_first, 1)

                def stack_lo(f, z, v):
                    s, hf = z // 2, z % 2
                    dve.wait_ge(st_hi_ok, 4 * f + z + 1)
                    src = FZ[z][:, :].rearrange("p (h n) -> p h n", h=HH)
                    hs = slice(hf * HH, (hf + 1) * HH)
                    if s == 0:
                        dve.tensor_tensor(q_st[D:P, hs, :], src[D:P], q_st[D:P, hs, :].bitcast(F32),
                                          ALU.subtract).then_inc(st_lo_ok, 1)
                    else:
                        dve.tensor_tensor(k_lo[:, hs, v, :], src, k_hi[:, hs, v, :].bitcast(F32),
                                          ALU.subtract).then_inc(st_lo_ok, 1)

                def values_lo(f, v):
                    dve.wait_ge(vhi_ok, f + 1)
                    dve.tensor_tensor(vs[:, v, :, 1, :], F[0][:, :].rearrange("p (h d) -> p h d", h=H),
                                      vs[:, v, :, 0, :].bitcast(F32), ALU.subtract).then_inc(vlo_ok, 1)

                def maximum(t, f, hf, v):
                    hs = slice(hf * HH, (hf + 1) * HH)
                    dve.wait_ge(s_done, 2 * t + hf + 1)
                    dve.tensor_reduce(mx[:, 0, hs], S[:, :, :], AX.X, ALU.max, negate=True).then_inc(m_ok, 1)
                    dve.wait_ge(rn_ok[0], f + 1)
                    dve.wait_ge(m_ok, 2 * t + hf + 1)
                    dve.tensor_tensor(mx[:, 1, hs], mx[:, 0, hs], rn[:, v, hs], ALU.mult).then_inc(mx_ok, 1)

                def p_lo(t, hf):
                    for c in range(2):
                        dve.wait_ge(pT_hi_ok, 4 * t + 2 * hf + c + 1)
                        dve.tensor_tensor(pT_lo[:, hf, 2 * c:2 * c + 2].rearrange("p h s n -> p (h s n)"), T[:, c, :],
                                          pT_hi[:, hf, 2 * c:2 * c + 2].rearrange("p h s n -> p (h s n)").bitcast(F32),
                                          ALU.subtract).then_inc(pT_lo_ok, 1)

                def normalise(t, hf):
                    hs = slice(hf * HH, (hf + 1) * HH)
                    dve.wait_ge(exp_ok, 4 * t + 2 * hf + 2)
                    dve.reciprocal(mx[:, 3, hs], mx[:, 2, hs]).then_inc(ri_ok, 1)
                    dve.wait_ge(ol_ok, 2 * t + hf + 1)
                    dve.tensor_tensor(ob[:, hf], O[:, :].rearrange("p (h a d) -> p h a d", h=HH, a=2)[:, :, 0, :],
                                      ol[:, hf], ALU.add).then_inc(both_ok, 1)
                    dve.wait_ge(ri_ok, 2 * t + hf + 1)
                    dve.wait_ge(both_ok, 2 * t + hf + 1)
                    o = dve.tensor_tensor(osb[:, hs, :], ob[:, hf], mx[:, 3, hs].unsqueeze(2).broadcast_to([P, HH, D]),
                                          ALU.mult)
                    if hf:
                        o.then_inc(osb_ok, 1)

                f = l * (TL + 1)
                x_lo(f)
                rotate_q(f, slice(0, 1))
                for s in (1, 0):
                    norms(f, s)
                stack_lo(f, 0, 0)
                stack_lo(f, 1, 0)
                stack_lo(f, 2, 0)
                stack_lo(f, 3, 0)
                with dve.Fori(0, B) as b:
                    with dve.Fori(0, TURNS) as q:
                        m = (l * B + b) * TURNS + q
                        for u in range(U):
                            t, f, v = U * m + u, U * m + l + u, (u + 1) % 2
                            x_lo(f + 1)
                            values_lo(f, u % 2)
                            maximum(t, f, 0, u % 2)
                            o_lo(f)
                            rotate_q(f + 1, next_tile(q, u))
                            residual(f, (u - 1) % U, u % 2, 2 * m + (u // 2) + (l if u % 2 == 0 else 0))
                            norms(f + 1, 1)
                            p_lo(t, 0)
                            maximum(t, f, 1, u % 2)
                            stack_lo(f + 1, 0, v)
                            stack_lo(f + 1, 1, v)
                            norms(f + 1, 0)
                            normalise(t, 0)
                            p_lo(t, 1)
                            stack_lo(f + 1, 2, v)
                            stack_lo(f + 1, 3, v)
                            normalise(t, 1)
                values_lo((l + 1) * TL + l, 0)
                o_lo((l + 1) * TL + l)
                residual((l + 1) * TL + l, U - 1, 0, (l + 1) * TL // 2 + l)
                meet(dve, 2 * l + 1)

                def z_statistics(f, v, loads):
                    wait_alone(dve, d_mx[v], 32 * loads, spare)
                    for t in range(GT):
                        dve.bn_stats(mbn[:, t, 0, :], mx2[:, v, t, 0:P])
                        st = dve.bn_stats(mbn[:, t, 1, :], mh2[:, v, t, :])
                    st.then_inc(bn_ok, 1)

                def z_variance(f):
                    wait_alone(dve, bn_ok, 2 * f + 1, spare)
                    for t in range(GT):
                        st = dve.bn_aggr(mmv[:, t, :], mbn[:, t].rearrange("p a s -> p (a s)"))
                    st.then_inc(bn_ok, 1)
                    dve.wait_ge(bn_ok, 2 * f + 2)
                    dve.tensor_scalar(mrs[:, 0, :], mmv[:, :, 1], EPS, None, ALU.add).then_inc(ve_ok, 1)

                def z_scale(f, v):
                    dve.wait_ge(rs_ok, f + 1)
                    for t in range(GT):
                        dve.tensor_scalar(mz[:, t, 0:P], mx2[:, v, t, 0:P], mmv[:, t, 0:1], mrs[:, 1, t:t + 1],
                                          ALU.subtract, ALU.mult)
                        st = dve.tensor_scalar(mz[:, t, P:E], mh2[:, v, t, :], mmv[:, t, 0:1], mrs[:, 1, t:t + 1],
                                               ALU.subtract, ALU.mult)
                    st.then_inc(z_ok, 1)

                def z_stack(f):
                    for k in range(KC):
                        dve.wait_ge(zT_done, 2 * f + k + 1)
                        dve.tensor_scalar(zT[:, k, :], ZT[k][:, :], gb_col[:, 0, k:k + 1], gb_col[:, 1, k:k + 1],
                                          ALU.mult, ALU.add).then_inc(zT_ok, 1)
                    for k in range(KC):
                        dve.wait_ge(zhi_ok, 2 * f + k + 1)
                        dve.tensor_tensor(zT_lo[:, k, :], zT[:, k, :], zT_hi[:, k, :].bitcast(F32),
                                          ALU.subtract).then_inc(zlo_ok, 1)

                f = l * (NGL + 1)
                z_statistics(f, 0, l * (B + 1) + 1)
                z_variance(f)
                z_scale(f, 0)
                z_stack(f)
                with dve.Fori(0, B) as b:
                    for g in range(NG):
                        m = (l * B + b) * NG + g
                        f, v = m + l + 1, (g + 1) % 2
                        for k in range(FT):
                            r = FR[k]
                            dve.wait_ge(gel_ok, m * FT + k + 1)
                            if k >= 2:
                                dve.wait_ge(hlo_ok, m * FT + k - 1)
                            dve.scalar_tensor_tensor(hid[0:r, k % 2, :], A[k % 2][0:r, :], b1_col[0:r, 0, k:k + 1],
                                                     gel[0:r, k % 2, :], ALU.add, ALU.mult).then_inc(hid_ok, 1)
                            if k == 1:
                                z_statistics(f, v, l * B + b + 1 if v else (l + 1) + l * B + b + 1)
                            elif k == 2:
                                z_variance(f)
                            elif k == 3:
                                z_scale(f, v)
                        z_stack(f)
                        dve.wait_ge(xb_ok, m + l + 1)
                        for t in range(GT):
                            dve.wait_ge(w2_done, m * GT + t + 1)
                            dve.tensor_tensor(my[:, t, :], Y[t][:, 0:E], mx2[:, g % 2, t, :], ALU.add).then_inc(my_ok, 1)
                meet(dve, 2 * l + 2)

            def fstatistics(k, v, loads):
                dve.wait_ge(d_f[v], 32 * loads)
                dve.tensor_tensor(fs[:, v], fy[:, v], fx[:, v], ALU.add).then_inc(f_add, 1)
                dve.wait_ge(f_add, k + 1)
                for t in range(GT):
                    st = dve.bn_stats(fbn[:, v, t, :], fs[:, v, t, :])
                st.then_inc(f_bn, 1)
                wait_alone(dve, f_bn, 2 * k + 1, spare)
                for t in range(GT):
                    st = dve.bn_aggr(fmv[:, v, t, :], fbn[:, v, t, :])
                st.then_inc(f_bn, 1)
                dve.wait_ge(f_bn, 2 * k + 2)
                dve.tensor_scalar(frs[:, v, 0, :], fmv[:, v, :, 1], EPS, None, ALU.add).then_inc(f_ag, 1)

            fstatistics(0, 0, 1)
            with dve.Fori(0, B) as b:
                for g in range(NG):
                    k = b * NG + g
                    dve.wait_ge(f_ok, GT * k + 1)
                    fstatistics(k + 1, (g + 1) % 2, b + 1 if g == 0 else b + 2)
                    dve.wait_ge(f_rs, k + 1)
                    dve.wait_ge(d_fo[g], 16 * b + 1)
                    for t in range(GT):
                        dve.tensor_scalar(fo[:, g, t, :], fs[:, g, t, :], fmv[:, g, t, 0:1], frs[:, g, 1, t:t + 1],
                                          ALU.subtract, ALU.mult).then_inc(f_ok, 1)


def build(nc, h, out):
    L, E = h["x"].shape[1:]
    B = h["x"].shape[0] - 1
    xs = nc.dram_tensor("states", (3, LEAD + B * (L + 1) + TAIL, E), F32, kind="Internal").ap()
    causal_attention(nc, h["x"], h["w_qkv"], h["w_out"], h["ln_g"], h["ln_b"], h["b_out"], h["ident"], h["mask"], xs)
    local_layers(nc, xs, B, out, h["rot"], h["rot_scale"], h["lw_qkv"], h["lw_out"], h["ident"], h["lmask"],
                 h["ln_gb"], h["w1"], h["b1"], h["w2"], h["b2"])


def layout(v):
    import numpy as np

    p, groups, hg, d = 128, 4, 4, 16
    x = v["L0_attn_x"]
    out = {"x": np.concatenate([x, np.zeros_like(x[:1])])}
    w = np.stack([v["L0_attn_Wq"].T, v["L0_attn_Wk"].T, v["L0_attn_Wv"].T], 1).reshape(2, p, 3, groups, hg * d)
    out["w_qkv"] = np.ascontiguousarray(w.transpose(1, 0, 3, 2, 4)).reshape(p, 2, 3, 256)
    out["w_out"] = np.ascontiguousarray(v["L0_attn_Wo"].T.reshape(2, p, 256).transpose(1, 0, 2))
    for name, a, b in (("ln_g", "gq", "gk"), ("ln_b", "bq", "bk")):
        r = np.stack([v["L0_attn_" + a], v["L0_attn_" + b]])[None, :, None, :]
        out[name] = np.ascontiguousarray(np.broadcast_to(r, (p, 2, hg, d)))
    out["b_out"] = np.ascontiguousarray(np.broadcast_to(v["L0_attn_bo"][None], (p, 256)))
    out["ident"] = np.eye(p, dtype=np.float32)
    i = np.arange(p)
    mask = np.where(i[:, None] >= i[None, :], 0.0, -1e30).astype(np.float32)
    out["mask"] = np.ascontiguousarray(np.stack([mask, mask.T], 1))
    return out


def layout_local(v):
    import numpy as np

    p, seq, window, dh, layers = 128, 1024, 128, 64, 2
    f = np.float32
    out = {}
    half_idx = np.arange(0, dh, 2, dtype=f)
    inv_freq = f(1.0) / f(10000.0) ** (half_idx / f(dh))
    t = np.arange(seq, dtype=f)
    freqs = t[:, None] * inv_freq[None, :]
    freqs = np.concatenate([freqs, freqs], -1)
    base = (half_idx + f(0.4 * dh)) / f(1.4 * dh)
    scale = base[None, :] ** ((t - seq // 2) / f(window // 2))[:, None]
    scale = np.concatenate([scale, scale], -1)
    sign = np.where(np.arange(dh) < dh // 2, -1, 1).astype(f)
    cos, sin = np.cos(freqs), np.sin(freqs) * sign
    rot = np.stack([cos * scale * f(8), sin * scale * f(8), cos / scale, sin / scale], 1).astype(f)
    out["rot"] = np.ascontiguousarray(rot.reshape(seq // p, p, 4, dh).transpose(1, 0, 2, 3))
    qs, ks = v["L0_ffn_q_scale"], v["L0_ffn_k_scale"]
    rows = np.stack([qs, np.roll(qs, dh // 2, -1), ks, np.roll(ks, dh // 2, -1)], 1)
    out["rot_scale"] = np.ascontiguousarray(np.broadcast_to(rows[:, None], (layers, p, 4, dh)))
    out["lw_qkv"] = np.ascontiguousarray(v["L0_ffn_wqkv"].reshape(layers, 2, p, -1).transpose(0, 2, 1, 3))
    out["lw_out"] = np.ascontiguousarray(v["L0_ffn_wo"].reshape(layers, 4, p, -1).transpose(0, 2, 1, 3))
    i = np.arange(p)
    own = np.where(i[:, None] >= i[None, :], 0.0, -1e30)
    prev = np.where(i[:, None] <= i[None, :], 0.0, -1e30)
    none = np.full((p, p), -1e30)
    masks = [np.stack([own, none], 1), np.stack([own, prev], 1), np.stack([prev, own], 1)]
    out["lmask"] = np.ascontiguousarray(np.stack(masks, 1).astype(f))
    hid = v["L0_ffn_w2"].shape[1]
    ft = -(-hid // p)
    gb = np.stack([v["L0_ffn_ln_g"], v["L0_ffn_ln_b"]], 1).reshape(layers, 2, 2, p)
    out["ln_gb"] = np.ascontiguousarray(gb.transpose(0, 3, 1, 2))
    out["w1"] = np.ascontiguousarray(v["L0_ffn_w1"].reshape(layers, 2, p, -1).transpose(0, 2, 1, 3))
    b1 = np.zeros((layers, 2, ft * p), f)
    b1[:, :, :hid] = v["L0_ffn_b1"].reshape(layers, 2, hid)
    out["b1"] = np.ascontiguousarray(b1.reshape(layers, 2, ft, p).transpose(0, 3, 1, 2))
    w2 = np.zeros((layers, ft * p, 256), f)
    w2[:, :hid] = v["L0_ffn_w2"]
    out["w2"] = np.ascontiguousarray(w2.reshape(layers, ft, p, 256).transpose(0, 2, 1, 3))
    out["b2"] = np.ascontiguousarray(np.broadcast_to(v["L0_ffn_b2"][:, None], (layers, p, 256)))
    return out


def kernel(**inputs):
    import numpy as np
    import concourse.bacc as bacc
    from concourse.bass_utils import run_bass_kernel_spmd

    v = {k: np.asarray(a) for k, a in inputs.items()}
    a = {**layout(v), **layout_local(v)}
    nc = bacc.Bacc("TRN2", target_bir_lowering=False, num_devices=1)
    h = {k: nc.dram_tensor(k, t.shape, F32, kind="ExternalInput").ap() for k, t in a.items()}
    B, L, E = v["L0_attn_x"].shape
    out = nc.dram_tensor("out", (B, L, E), F32, kind="ExternalOutput").ap()
    build(nc, h, out)
    r = run_bass_kernel_spmd(nc, [a], core_ids=[0])
    return r.results[0]["out"]
```
